# Optimizing a Trainium2 kernel written in Bass

```python
import numpy as np
import jax
import jax.numpy as jnp

def _softmax(x, axis=-1):
    return jax.nn.softmax(x, axis=axis)

def _gelu(x):
    return jax.nn.gelu(x, approximate=True)

def _silu(x):
    return jax.nn.silu(x)

def _sigmoid(x):
    return jax.nn.sigmoid(x)

def _layernorm(x, axis=-1, eps=1e-05):
    m = jnp.mean(x, axis=axis, keepdims=True)
    v = jnp.var(x, axis=axis, keepdims=True)
    return (x - m) / jnp.sqrt(v + eps)

def _scatter_add(tgt, idx, src, axis=0):
    return tgt.at[idx].add(src)

def _segment_sum(src, seg, n):
    return jax.ops.segment_sum(src, seg, n)
kernel_name = 'mk_flamingo_gated_d2_seqx_r8_52343a'

def setup_inputs(seed: int=0):
    np.random.seed(seed)
    _w = jnp.asarray

    def _rec_inputs():
        import jax
        import jax.numpy as jnp
        _rk = jax.random.key(seed)
        x = 7.22e-05 + 1 * jax.random.normal(jax.random.fold_in(_rk, 1), (16, 64, 512), jnp.float32)
        _lenS = 64 - jax.random.randint(jax.random.fold_in(_rk, 7), (16,), 0, max(1, 64 // 4) + 1, jnp.int32)
        _lenS2 = 64 - jax.random.randint(jax.random.fold_in(_rk, 8), (16,), 0, max(1, 64 // 4) + 1, jnp.int32)
        _ctx_4096P = jax.random.normal(jax.random.fold_in(_rk, 11), (16, 16, 512), jnp.float32)
        _ctx_4096c = jax.random.dirichlet(jax.random.fold_in(_rk, 511), 0.3 * jnp.ones((16,), jnp.float32), (16, 64))
        _ctx_4096t = jnp.einsum('bsk,bkd->bsd', _ctx_4096c, _ctx_4096P)
        _ctx_4096t = _ctx_4096t * jax.lax.rsqrt(jnp.mean(jnp.square(_ctx_4096t)) + 1e-12) * 0.953939
        ctx_4096 = 4.13588e-05 + 0.999923 * (_ctx_4096t + 0.3 * jax.random.normal(jax.random.fold_in(_rk, 611), (16, 64, 512), jnp.float32))
        _validS = jnp.arange(64)[None, :] < _lenS[:, None]
        _validS2 = jnp.arange(64)[None, :] < _lenS2[:, None]
        _causal = jnp.tril(jnp.ones((64, 64), dtype=bool))
        mask_BxSxS2_ff0 = jnp.where(jnp.ones((16, 64, 64), dtype=bool), 0.0, -1000000000.0).astype(jnp.float32)
        _g = jax.random.normal(jax.random.fold_in(_rk, 9001), (2, 2), jnp.float32)
        _g = jnp.sign(_g) * jnp.maximum(jnp.abs(_g), 1.0) + (_g == 0) * 1.0
        g_xattn = _g[0]
        g_ffn = _g[1]
        return (x, ctx_4096, mask_BxSxS2_ff0, g_xattn, g_ffn)
    x, ctx_4096, mask_BxSxS2_ff0, g_xattn, g_ffn = _rec_inputs()

    def _L0_xattn_setup():
        import jax, jax.numpy as jnp
        import numpy as np
        HEADS = 8
        WINDOW = 16

        def _pointwise(W, b, t):
            return jnp.einsum('oc,bct->bot', W, t) + b[None, :, None]
        key = jax.random.key(seed)
        ks = jax.random.split(key, 10)
        B, C, T = (4, 64, 512)
        s = 0.02
        return {'x': jax.random.normal(ks[0], (B, C, T), jnp.float32), 'cond': jax.random.normal(ks[1], (B, C, T), jnp.float32), 'Wq': jax.random.normal(ks[2], (C, C), jnp.float32) * s, 'bq': jnp.zeros((C,), jnp.float32), 'Wk': jax.random.normal(ks[3], (C, C), jnp.float32) * s, 'bk': jnp.zeros((C,), jnp.float32), 'Wv': jax.random.normal(ks[4], (C, C), jnp.float32) * s, 'bv': jnp.zeros((C,), jnp.float32), 'Wo': jax.random.normal(ks[5], (C, C), jnp.float32) * s, 'bo': jnp.zeros((C,), jnp.float32)}
    _L0_xattn_all = _L0_xattn_setup()
    _L0_xattn_in = {k: v for k, v in _L0_xattn_all.items() if k in ('Wq', 'bq', 'Wk', 'bk', 'Wv', 'bv', 'Wo', 'bo')}
    del _L0_xattn_all

    def _L0_ffn_setup():
        import jax, jax.numpy as jnp
        import numpy as np
        B, S, D, O, E, R = (2, 512, 512, 512, 8, 16)
        TOP_K = 2
        SCALING = 32.0 / 16.0
        key = jax.random.key(seed)
        k = jax.random.split(key, 6)
        x = jax.random.normal(k[0], (B, S, D), dtype=jnp.float32)
        W_base = jax.random.normal(k[1], (O, D), dtype=jnp.float32) * 0.02
        b_base = jax.random.normal(k[2], (O,), dtype=jnp.float32) * 0.02
        W_router = jax.random.normal(k[3], (E, D), dtype=jnp.float32) * 0.01
        lora_A = jax.random.normal(k[4], (E, R, D), dtype=jnp.float32) * (1.0 / np.sqrt(D))
        lora_B = jax.random.normal(k[5], (E, O, R), dtype=jnp.float32) * 0.02
        return {'x': x, 'W_base': W_base, 'b_base': b_base, 'W_router': W_router, 'lora_A': lora_A, 'lora_B': lora_B}
    _L0_ffn_all = _L0_ffn_setup()
    _L0_ffn_in = {k: v for k, v in _L0_ffn_all.items() if k in ('W_base', 'b_base', 'W_router', 'lora_A', 'lora_B')}
    del _L0_ffn_all

    def _L1_xattn_setup():
        import jax, jax.numpy as jnp
        import numpy as np
        BS, SEQ, D_MODEL = (4, 128, 512)
        N_Q_HEADS, N_KV_HEADS, D_K, D_V = (32, 8, 128, 128)
        ROPE_BASE = 10000.0

        def _rotate_half(x):
            x1, x2 = jnp.split(x, 2, axis=-1)
            return jnp.concatenate([-x2, x1], axis=-1)

        def _apply_rope(x, pos0):
            d = x.shape[-1]
            seq = x.shape[2]
            inv_freq = 1.0 / ROPE_BASE ** (jnp.arange(0, d, 2, dtype=jnp.float32) / d)
            pos = (pos0 + jnp.arange(seq)).astype(jnp.float32)
            ang = pos[:, None] * inv_freq[None, :]
            cos = jnp.concatenate([jnp.cos(ang), jnp.cos(ang)], axis=-1)
            sin = jnp.concatenate([jnp.sin(ang), jnp.sin(ang)], axis=-1)
            return x * cos[None, None] + _rotate_half(x) * sin[None, None]
        key = jax.random.key(seed)
        ks = jax.random.split(key, 8)
        w_scale = 0.02
        return {'query': jax.random.normal(ks[0], (BS, SEQ, D_MODEL), dtype=jnp.float32), 'key': jax.random.normal(ks[1], (BS, SEQ, D_MODEL), dtype=jnp.float32), 'value': jax.random.normal(ks[2], (BS, SEQ, D_MODEL), dtype=jnp.float32), 'mask': jnp.zeros((BS, SEQ, SEQ), dtype=jnp.float32), 'wq': jax.random.normal(ks[3], (D_MODEL, N_Q_HEADS * D_K), dtype=jnp.float32) * w_scale, 'wk': jax.random.normal(ks[4], (D_MODEL, N_KV_HEADS * D_K), dtype=jnp.float32) * w_scale, 'wv': jax.random.normal(ks[5], (D_MODEL, N_KV_HEADS * D_V), dtype=jnp.float32) * w_scale, 'wo': jax.random.normal(ks[6], (N_Q_HEADS * D_V, D_MODEL), dtype=jnp.float32) * w_scale, 'curr_seq_pos': 0}
    _L1_xattn_all = _L1_xattn_setup()
    _L1_xattn_in = {k: v for k, v in _L1_xattn_all.items() if k in ('wq', 'wk', 'wv', 'wo')}
    del _L1_xattn_all

    def _L1_ffn_setup():
        import jax, jax.numpy as jnp
        import numpy as np
        HID = 512
        INTER = 1376
        BITS = 4
        PACK = 8
        MAXQ = 15
        GROUP = 128

        def _dequant(qweight, scales, qzeros, g_idx):
            shifts = jnp.arange(PACK, dtype=jnp.uint32) * BITS
            qw = qweight.astype(jnp.uint32)
            w = (qw[:, None, :] >> shifts[None, :, None] & MAXQ).reshape(-1, qweight.shape[1])
            qz = qzeros.astype(jnp.uint32)
            z = ((qz[:, :, None] >> shifts[None, None, :] & MAXQ) + 1).reshape(qzeros.shape[0], -1)
            s = scales[g_idx]
            return (w.astype(scales.dtype) - z[g_idx].astype(scales.dtype)) * s
        key = jax.random.key(seed)
        ks = jax.random.split(key, 16)

        def qw(k, K, N):
            return jax.random.randint(k, (K // PACK, N), 0, 2147483647, dtype=jnp.int32)

        def qz(k, G, N):
            return jax.random.randint(k, (G, N // PACK), 0, 2147483647, dtype=jnp.int32)

        def sc(k, G, N):
            return jax.random.uniform(k, (G, N), jnp.float32, 0.001, 0.01)
        Gk = HID // GROUP
        Gd = INTER // GROUP
        return {'x': jax.random.normal(ks[0], (4, 256, HID), jnp.float32), 'gate_qweight': qw(ks[1], HID, INTER), 'gate_scales': sc(ks[2], Gk, INTER), 'gate_qzeros': qz(ks[3], Gk, INTER), 'gate_g_idx': (jnp.arange(HID) // GROUP).astype(jnp.int32), 'up_qweight': qw(ks[4], HID, INTER), 'up_scales': sc(ks[5], Gk, INTER), 'up_qzeros': qz(ks[6], Gk, INTER), 'up_g_idx': (jnp.arange(HID) // GROUP).astype(jnp.int32), 'down_qweight': qw(ks[7], INTER, HID), 'down_scales': sc(ks[8], Gd, HID), 'down_qzeros': qz(ks[9], Gd, HID), 'down_g_idx': (jnp.arange(INTER) // GROUP).astype(jnp.int32)}
    _L1_ffn_all = _L1_ffn_setup()
    _L1_ffn_in = {k: v for k, v in _L1_ffn_all.items() if k in ('gate_qweight', 'gate_scales', 'gate_qzeros', 'gate_g_idx', 'up_qweight', 'up_scales', 'up_qzeros', 'up_g_idx', 'down_qweight', 'down_scales', 'down_qzeros', 'down_g_idx')}
    del _L1_ffn_all
    return {'x': x, 'ctx_4096': ctx_4096, 'mask_BxSxS2_ff0': mask_BxSxS2_ff0, 'g_xattn': g_xattn, 'g_ffn': g_ffn, 'L0_xattn_Wq': _L0_xattn_in['Wq'], 'L0_xattn_bq': _L0_xattn_in['bq'], 'L0_xattn_Wk': _L0_xattn_in['Wk'], 'L0_xattn_bk': _L0_xattn_in['bk'], 'L0_xattn_Wv': _L0_xattn_in['Wv'], 'L0_xattn_bv': _L0_xattn_in['bv'], 'L0_xattn_Wo': _L0_xattn_in['Wo'], 'L0_xattn_bo': _L0_xattn_in['bo'], 'L0_ffn_W_base': _L0_ffn_in['W_base'], 'L0_ffn_b_base': _L0_ffn_in['b_base'], 'L0_ffn_W_router': _L0_ffn_in['W_router'], 'L0_ffn_lora_A': _L0_ffn_in['lora_A'], 'L0_ffn_lora_B': _L0_ffn_in['lora_B'], 'L1_xattn_wq': _L1_xattn_in['wq'], 'L1_xattn_wk': _L1_xattn_in['wk'], 'L1_xattn_wv': _L1_xattn_in['wv'], 'L1_xattn_wo': _L1_xattn_in['wo'], 'L1_ffn_gate_qweight': _L1_ffn_in['gate_qweight'], 'L1_ffn_gate_scales': _L1_ffn_in['gate_scales'], 'L1_ffn_gate_qzeros': _L1_ffn_in['gate_qzeros'], 'L1_ffn_gate_g_idx': _L1_ffn_in['gate_g_idx'], 'L1_ffn_up_qweight': _L1_ffn_in['up_qweight'], 'L1_ffn_up_scales': _L1_ffn_in['up_scales'], 'L1_ffn_up_qzeros': _L1_ffn_in['up_qzeros'], 'L1_ffn_up_g_idx': _L1_ffn_in['up_g_idx'], 'L1_ffn_down_qweight': _L1_ffn_in['down_qweight'], 'L1_ffn_down_scales': _L1_ffn_in['down_scales'], 'L1_ffn_down_qzeros': _L1_ffn_in['down_qzeros'], 'L1_ffn_down_g_idx': _L1_ffn_in['down_g_idx']}

def reference(x, ctx_4096, mask_BxSxS2_ff0, g_xattn, g_ffn, L0_xattn_Wq, L0_xattn_bq, L0_xattn_Wk, L0_xattn_bk, L0_xattn_Wv, L0_xattn_bv, L0_xattn_Wo, L0_xattn_bo, L0_ffn_W_base, L0_ffn_b_base, L0_ffn_W_router, L0_ffn_lora_A, L0_ffn_lora_B, L1_xattn_wq, L1_xattn_wk, L1_xattn_wv, L1_xattn_wo, L1_ffn_gate_qweight, L1_ffn_gate_scales, L1_ffn_gate_qzeros, L1_ffn_gate_g_idx, L1_ffn_up_qweight, L1_ffn_up_scales, L1_ffn_up_qzeros, L1_ffn_up_g_idx, L1_ffn_down_qweight, L1_ffn_down_scales, L1_ffn_down_qzeros, L1_ffn_down_g_idx):
    import jax
    import jax.numpy as jnp

    def _L0_xattn_ref(x, cond, Wq, bq, Wk, bk, Wv, bv, Wo, bo):
        import jax, jax.numpy as jnp
        import numpy as np
        HEADS = 8
        WINDOW = 16

        def _pointwise(W, b, t):
            return jnp.einsum('oc,bct->bot', W, t) + b[None, :, None]
        B, C, T = x.shape
        H, W = (HEADS, WINDOW)
        hd = C // H
        scale = hd ** (-0.5)
        pad_left = W // 2
        pad_right = W - pad_left - 1
        q = _pointwise(Wq, bq, x)
        k = _pointwise(Wk, bk, cond)
        v = _pointwise(Wv, bv, cond)
        k = jnp.pad(k, ((0, 0), (0, 0), (pad_left, pad_right)))
        v = jnp.pad(v, ((0, 0), (0, 0), (pad_left, pad_right)))
        idx = jnp.arange(T)[:, None] + jnp.arange(W)[None, :]
        k_win = k[:, :, idx].reshape(B, H, hd, T, W)
        v_win = v[:, :, idx].reshape(B, H, hd, T, W)
        qh = q.reshape(B, H, hd, T)
        dots = jnp.einsum('bhdt,bhdtw->bhtw', qh, k_win) * scale
        attn = jax.nn.softmax(dots, axis=-1)
        out = jnp.einsum('bhtw,bhdtw->bhdt', attn, v_win)
        out = out.reshape(B, C, T)
        return _pointwise(Wo, bo, out)

    def _L0_ffn_ref(x, W_base, b_base, W_router, lora_A, lora_B):
        import jax, jax.numpy as jnp
        import numpy as np
        B, S, D, O, E, R = (2, 512, 512, 512, 8, 16)
        TOP_K = 2
        SCALING = 32.0 / 16.0
        d = x.shape[-1]
        n_experts = W_router.shape[0]
        xf = x.reshape(-1, d)
        logits = xf @ W_router.T
        probs = jax.nn.softmax(logits, axis=-1)
        topk_p, topk_i = jax.lax.top_k(probs, TOP_K)
        topk_p = topk_p / jnp.sum(topk_p, axis=-1, keepdims=True)
        w = jnp.sum(jax.nn.one_hot(topk_i, n_experts, dtype=xf.dtype) * topk_p[..., None], axis=1)
        h = jnp.einsum('td,erd->ter', xf, lora_A)
        lora_out = jnp.einsum('ter,eor,te->to', h, lora_B, w) * SCALING
        base = x @ W_base.T + b_base
        return base + lora_out.reshape(x.shape[:-1] + (W_base.shape[0],))

    def _L1_xattn_ref(query, key, value, mask, wq, wk, wv, wo, curr_seq_pos):
        import jax, jax.numpy as jnp
        import numpy as np
        BS, SEQ, D_MODEL = (4, 128, 512)
        N_Q_HEADS, N_KV_HEADS, D_K, D_V = (32, 8, 128, 128)
        ROPE_BASE = 10000.0

        def _rotate_half(x):
            x1, x2 = jnp.split(x, 2, axis=-1)
            return jnp.concatenate([-x2, x1], axis=-1)

        def _apply_rope(x, pos0):
            d = x.shape[-1]
            seq = x.shape[2]
            inv_freq = 1.0 / ROPE_BASE ** (jnp.arange(0, d, 2, dtype=jnp.float32) / d)
            pos = (pos0 + jnp.arange(seq)).astype(jnp.float32)
            ang = pos[:, None] * inv_freq[None, :]
            cos = jnp.concatenate([jnp.cos(ang), jnp.cos(ang)], axis=-1)
            sin = jnp.concatenate([jnp.sin(ang), jnp.sin(ang)], axis=-1)
            return x * cos[None, None] + _rotate_half(x) * sin[None, None]
        bs, sq, _ = query.shape
        n_groups = N_Q_HEADS // N_KV_HEADS
        q = (query @ wq).reshape(bs, sq, N_Q_HEADS, D_K).transpose((0, 2, 1, 3))
        sk = key.shape[1]
        k = (key @ wk).reshape(bs, sk, N_KV_HEADS, 1, D_K)
        k = jnp.repeat(k, n_groups, axis=3).reshape(bs, sk, N_Q_HEADS, D_K).transpose((0, 2, 1, 3))
        v = (value @ wv).reshape(bs, sk, N_KV_HEADS, 1, D_V)
        v = jnp.repeat(v, n_groups, axis=3).reshape(bs, sk, N_Q_HEADS, D_V).transpose((0, 2, 1, 3))
        scale = jnp.sqrt(jnp.float32(D_K))
        q = _apply_rope(q, curr_seq_pos)
        k = _apply_rope(k, curr_seq_pos)
        raw = jnp.einsum('bhqd,bhkd->bhqk', q, k) / scale
        masked = raw + mask[:bs, None, curr_seq_pos:curr_seq_pos + sq, :sk]
        attn = jax.nn.softmax(masked, axis=-1)
        out = jnp.einsum('bhqk,bhkd->bhqd', attn, v)
        out = out.transpose((0, 2, 1, 3)).reshape(bs, sq, N_Q_HEADS * D_V)
        return out @ wo

    def _L1_ffn_ref(x, gate_qweight, gate_scales, gate_qzeros, gate_g_idx, up_qweight, up_scales, up_qzeros, up_g_idx, down_qweight, down_scales, down_qzeros, down_g_idx):
        import jax, jax.numpy as jnp
        import numpy as np
        HID = 512
        INTER = 1376
        BITS = 4
        PACK = 8
        MAXQ = 15
        GROUP = 128

        def _dequant(qweight, scales, qzeros, g_idx):
            shifts = jnp.arange(PACK, dtype=jnp.uint32) * BITS
            qw = qweight.astype(jnp.uint32)
            w = (qw[:, None, :] >> shifts[None, :, None] & MAXQ).reshape(-1, qweight.shape[1])
            qz = qzeros.astype(jnp.uint32)
            z = ((qz[:, :, None] >> shifts[None, None, :] & MAXQ) + 1).reshape(qzeros.shape[0], -1)
            s = scales[g_idx]
            return (w.astype(scales.dtype) - z[g_idx].astype(scales.dtype)) * s
        Wg = _dequant(gate_qweight, gate_scales, gate_qzeros, gate_g_idx)
        Wu = _dequant(up_qweight, up_scales, up_qzeros, up_g_idx)
        Wd = _dequant(down_qweight, down_scales, down_qzeros, down_g_idx)
        xf = x.reshape(-1, x.shape[-1])
        h = jax.nn.silu(xf @ Wg) * (xf @ Wu)
        out = h @ Wd
        return out.reshape(x.shape[:-1] + (Wd.shape[1],))
    x = x + jnp.tanh(g_xattn[0]) * _L0_xattn_ref(_layernorm(x, axis=-1), ctx_4096, L0_xattn_Wq, L0_xattn_bq, L0_xattn_Wk, L0_xattn_bk, L0_xattn_Wv, L0_xattn_bv, L0_xattn_Wo, L0_xattn_bo)
    x = x + jnp.tanh(g_ffn[0]) * _L0_ffn_ref(_layernorm(x, axis=-1), L0_ffn_W_base, L0_ffn_b_base, L0_ffn_W_router, L0_ffn_lora_A, L0_ffn_lora_B)
    x = x + jnp.tanh(g_xattn[1]) * _L1_xattn_ref(_layernorm(x, axis=-1), ctx_4096, ctx_4096, mask_BxSxS2_ff0, L1_xattn_wq, L1_xattn_wk, L1_xattn_wv, L1_xattn_wo, 0)
    x = x + jnp.tanh(g_ffn[1]) * _L1_ffn_ref(_layernorm(x, axis=-1), L1_ffn_gate_qweight, L1_ffn_gate_scales, L1_ffn_gate_qzeros, L1_ffn_gate_g_idx, L1_ffn_up_qweight, L1_ffn_up_scales, L1_ffn_up_qzeros, L1_ffn_up_g_idx, L1_ffn_down_qweight, L1_ffn_down_scales, L1_ffn_down_qzeros, L1_ffn_down_g_idx)
    return x

_drawn_inputs = setup_inputs


def setup_inputs(seed=0):
    import zlib

    import numpy as np

    out = dict(_drawn_inputs(seed))
    spreads = {'g_ffn': (-1.0, 0.2),
     'L0_xattn_bq': (0.0, 0.8),
     'L0_xattn_bk': (0.0, 0.8),
     'L0_xattn_bv': (0.0, 0.8),
     'L0_xattn_bo': (0.0, 0.1)}
    factors = {'L0_xattn_Wq': 8.0,
     'L0_xattn_Wk': 8.0,
     'L0_xattn_Wv': 6.01,
     'L0_xattn_Wo': 3.958,
     'L0_ffn_b_base': 4.056,
     'L1_xattn_wq': 2.994,
     'L1_xattn_wk': 2.965}
    for name, (base, spread) in spreads.items():
        noise = np.random.default_rng([zlib.crc32(name.encode()), seed]).standard_normal(out[name].shape)
        drawn = base * np.exp(spread * noise) if base else spread * noise
        out[name] = jnp.asarray(drawn.astype(out[name].dtype))
    for name, factor in factors.items():
        out[name] = (out[name] * factor).astype(out[name].dtype)
    return out
```

```python
from contextlib import ExitStack

import numpy as np

import concourse.bass as bass
from concourse import mybir

F32 = mybir.dt.float32
F32R = mybir.dt.float32r
I32 = mybir.dt.int32
U32 = mybir.dt.uint32
BF16 = mybir.dt.bfloat16
ALU = mybir.AluOpType
ACT = mybir.ActivationFunctionType
AX = mybir.AxisListType

P = 128
B, C, D = 16, 64, 512
TOK = B * C
NT = TOK // P
BT = P // C
DC = D // P
HALF = 512
NHALF = TOK // HALF
TPH = HALF // P
EPS = 1e-5

LH, LHD, WIN = 8, 8, 16
PAD_L = WIN // 2
TPAD = D + WIN - 1
BH = BT * LH
WG = P // BH
GW = 4

NE, RANK = 8, 16
LORA_SCALE = 32.0 / 16.0

NQ, NKV, DK = 32, 8, 128
GRP = NQ // NKV

INTER, PACK, BITS = 1376, 8, 4
NTI = -(-INTER // P)
GK, GD = D // 128, INTER // 128


MATS = (("gate", D, INTER, GK), ("up", D, INTER, GK), ("down", INTER, D, GD))
ROW0 = (0, D, 2 * D)
COL0 = (0, INTER, 2 * INTER)


def inner(t):
    return min(P, INTER - P * t)


def build_program(nc, a, out):
    with ExitStack() as top:
        def sbuf(ctx, name, shape, dt=F32):
            return ctx.enter_context(nc.sbuf_tensor(name, shape, dt))

        ps = top.enter_context(nc.psum_tensor("ps", [P, 8, 512], F32))
        x = sbuf(top, "x", [P, NT, D])
        ident = sbuf(top, "ident", [P, P])
        gate = sbuf(top, "gate", [P, 4])
        stats = sbuf(top, "stats", [P, NT, 6])
        mv = sbuf(top, "mv", [P, NT, 2])
        veps = sbuf(top, "veps", [P, NT])
        rstd = sbuf(top, "rstd", [P, NT])
        mhalf = sbuf(top, "mhalf", [P, NT])
        g = dict(ps=ps, x=x, ident=ident, gate=gate, stats=stats, mv=mv, veps=veps, rstd=rstd, mhalf=mhalf)
        for name in ("wq_landed", "wo_landed", "wkv_landed"):
            g[name] = top.enter_context(nc.semaphore(name))
        g["onehot"] = sbuf(top, "onehot", [P, 2 * D + INTER], BF16)
        g["rows"] = sbuf(top, "rows", [P, 2 * INTER + D], BF16)
        with ExitStack() as first:
            g["wq_raw"] = sbuf(first, "wq_raw", [P, DC, GRP * DK])
            g["wo_raw"] = sbuf(first, "wo_raw", [P, GRP, D])
            g["wkv_raw"] = sbuf(first, "wkv_raw", [P, 2, DC, DK])
            windowed_attention(nc, a, g)
            for name in ("xh", "xl", "ch", "cl"):
                g[name] = sbuf(first, name, [P, DC, TOK], F32R)
            routed_lora(nc, a, g)
            rotary_attention(nc, a, g)
        with ExitStack() as last:
            for name in ("xh", "xl"):
                g[name] = sbuf(last, name + "4", [P, DC, TOK], F32R)
            g["h"] = sbuf(last, "h", [P, NTI, TOK])
            g["wd"] = sbuf(last, "wd", [P, NTI, D])
            gate_up(nc, a, g)
            down(nc, a, g, out)


def qkv_weight_loads(eng, a, g, kv):
    n = GRP * DK
    eng.dma_start(g["wkv_raw"][:, 0, :, :], a["wk"].rearrange("(c p) n -> p c n", p=P)[:, :, kv * DK:(kv + 1) * DK])\
       .then_inc(g["wkv_landed"], 16)
    eng.dma_start(g["wkv_raw"][:, 1, :, :], a["wv"].rearrange("(c p) n -> p c n", p=P)[:, :, kv * DK:(kv + 1) * DK])\
       .then_inc(g["wkv_landed"], 16)
    eng.dma_start(g["wq_raw"][:, :, :], a["wq"].rearrange("(c p) n -> p c n", p=P)[:, :, kv * n:(kv + 1) * n])\
       .then_inc(g["wq_landed"], 16)


def out_weight_load(eng, a, g, kv):
    n = GRP * DK
    eng.dma_start(g["wo_raw"][:, :, :], a["wo"][kv * n:(kv + 1) * n, :].rearrange("(h p) n -> p h n", p=P))\
       .then_inc(g["wo_landed"], 16)


def windowed_attention(nc, a, g):
    ps, x, ident, gate = g["ps"], g["x"], g["ident"], g["gate"]
    stats, mv, veps, rstd, mhalf = g["stats"], g["mv"], g["veps"], g["rstd"], g["mhalf"]
    with ExitStack() as ctx:
        def sb(name, shape, dt=F32):
            return ctx.enter_context(nc.sbuf_tensor(name, shape, dt))

        def sem(name):
            return ctx.enter_context(nc.semaphore(name))

        ctxt = sb("ctxt", [P, NT, D])
        w4 = sb("w4", [P, 4, P])
        bias = sb("bias", [P, 4])
        gbo = sb("gbo", [P, 1])
        graw = sb("graw", [P, 4])
        sel = sb("sel", [P, 2, 32])
        spread_f = sb("spread_f", [P, WG, P])
        spread = sb("spread", [P, WG, P], F32R)
        xn = sb("xn", [P, 2, D])
        q = sb("q", [P, 2, D])
        kpad = sb("kpad", [P, 2, TPAD])
        vpad = sb("vpad", [P, 3, TPAD])
        prod = sb("prod", [P, WIN, D])
        sc = sb("sc", [P, 2, D])
        mx = sb("mx", [P, D // P, BH])
        att = sb("att", [P, D // P, WIN, BH])
        sm = sb("sm", [P, D // P, BH])
        rs = sb("rs", [P, D // P, BH])
        ath = sb("ath", [P, 2, D], F32R)
        atl = sb("atl", [P, 2, D], F32R)
        r = sb("r", [P, WIN, D])
        r2 = sb("r2", [P, WIN // 2, D])
        o = sb("o", [P, D])

        x_landed = [sem(f"x_landed{i}") for i in range(NT)]
        ctx_landed = [sem(f"ctx_landed{i}") for i in range(NT)]
        const_landed = sem("const_landed")
        half_set = sem("half_set")
        pad_zeroed = sem("pad_zeroed")
        gate_ready = sem("gate_ready")
        spread_ready = sem("spread_ready")
        dve_step = sem("dve_step")
        var_ready = sem("var_ready")
        rstd_ready = sem("rstd_ready")
        xn_ready = sem("xn_ready")
        qkv_done = sem("qkv_done")
        qkv_ready = sem("qkv_ready")
        prod_ready = sem("prod_ready")
        prod_used = sem("prod_used")
        sc_ready = sem("sc_ready")
        fwd_done = sem("fwd_done")
        shifted = sem("shifted")
        exp_ready = sem("exp_ready")
        att_ready = sem("att_ready")
        back_done = sem("back_done")
        ath_ready = sem("ath_ready")
        atl_ready = sem("atl_ready")
        spread_done = sem("spread_done")
        r_ready = sem("r_ready")
        rsum_ready = sem("rsum_ready")
        out_done = sem("out_done")
        o_ready = sem("o_ready")
        x_ready = sem("x_ready")
        st = stat_sems(sem)

        S = [ps[:, 0, :], ps[:, 1, :]]
        T2 = ps[:, 2:4, :]
        T_time = T2.rearrange("p a (b g m) -> p (a b) g m", b=2, g=2)
        T_win = T2.rearrange("p a (b w h) -> p (a b) w h", b=2, w=WIN)
        RING = [ps[:, 4, :], ps[:, 5, :], ps[:, 6, :]]
        M = ps[:, 7, :]

        NCONST = 14
        ORDER = [w + d for w in range(0, WIN // 2, 2) for d in (0, 1, WIN // 2, WIN // 2 + 1)]
        RINGS = 2 + WIN

        block = ctx.enter_context(nc.Block())

        @block.sync
        def _(sp):
            xr = a["x"].rearrange("b s d -> (b s) d")
            cr = a["ctx"].rearrange("b s d -> (b s) d")
            sp.dma_start(x[:, 0, :], xr[0:P, :]).then_inc(x_landed[0], 16)
            sp.dma_start(ctxt[:, 0, :], cr[0:P, :]).then_inc(ctx_landed[0], 16)
            for j, w in enumerate(("Wq", "Wk", "Wv", "Wo")):
                sp.dma_start(w4[:, j, :], a[w]).then_inc(const_landed, 16)
            for j, w in enumerate(("bq", "bk", "bv", "bo")):
                for b in range(BT):
                    sp.dma_start(bias[b * C:(b + 1) * C, j:j + 1], a[w].rearrange("(c o) -> c o", o=1))\
                      .then_inc(const_landed, 16)
            sp.dma_start(sel[:, :, :], a["sel"].rearrange("p (a b) -> p a b", a=2)).then_inc(const_landed, 16)
            sp.dma_start(ident[:, :], a["ident"]).then_inc(const_landed, 16)
            for i in range(1, NT):
                sp.dma_start(x[:, i, :], xr[i * P:(i + 1) * P, :]).then_inc(x_landed[i], 16)
                sp.dma_start(ctxt[:, i, :], cr[i * P:(i + 1) * P, :]).then_inc(ctx_landed[i], 16)
            qkv_weight_loads(sp, a, g, 0)
            out_weight_load(sp, a, g, 0)

        @block.gpsimd
        def _(pool):
            pool.memset(kpad[:, :, :], 0.0).then_inc(pad_zeroed, 1)
            pool.memset(vpad[:, :, :], 0.0).then_inc(pad_zeroed, 1)
            pool.memset(mhalf[:, :], -0.5).then_inc(half_set, 1)
            pool.wait_ge(half_set, 1)
            pool.wait_ge(var_ready, 1)
            pool.tensor_tensor(rstd[:, 0:1], veps[:, 0:1], mhalf[:, 0:1], ALU.pow).then_inc(rstd_ready, 1)
            pool.wait_ge(var_ready, 2)
            pool.tensor_tensor(rstd[:, 1:NT], veps[:, 1:NT], mhalf[:, 1:NT], ALU.pow).then_inc(rstd_ready, 1)
            for i in range(NT):
                for w in range(0, WIN // 2, 2):
                    pool.wait_ge(r_ready, WIN * i + 2 * w + 4)
                    if i >= 1 and w == 0:
                        pool.wait_ge(out_done, i)
                    pool.tensor_tensor(r2[:, w:w + 2, :], r[:, w:w + 2, :], r[:, WIN // 2 + w:WIN // 2 + w + 2, :],
                                       ALU.add).then_inc(rsum_ready, 1)
            row_scales(pool, g, st)

        @block.scalar
        def _(act):
            act.dma_start(spread_f[:, :, :], a["spread"].rearrange("p (w c) -> p w c", w=WG)).then_inc(const_landed, 16)
            act.dma_start(graw[:, 0:2], a["g_xattn"].partition_broadcast(P)).then_inc(const_landed, 16)
            act.dma_start(graw[:, 2:4], a["g_ffn"].partition_broadcast(P)).then_inc(const_landed, 16)
            act.wait_ge(const_landed, 16 * (NCONST + 3))
            act.activation(gate[:, :], graw[:, :], ACT.Tanh).then_inc(gate_ready, 1)
            act.wait_ge(gate_ready, 1)
            act.activation(gbo[:, :], bias[:, 3:4], ACT.Copy, scale=gate[:, 0:1]).then_inc(gate_ready, 1)
            act.activation(spread[:, :, :], spread_f[:, :, :], ACT.Copy).then_inc(spread_ready, 1)
            act.wait_ge(pad_zeroed, 2)

            def project(i):
                act.wait_ge(qkv_done, 3 * i + 1)
                if i >= 2:
                    act.wait_ge(prod_ready, 4 * (i - 1))
                act.activation(q[:, i % 2, :], M, ACT.Identity, bias=bias[:, 0:1]).then_inc(qkv_ready, 1)
                act.wait_ge(qkv_done, 3 * i + 2)
                act.activation(kpad[:, i % 2, PAD_L:PAD_L + D], RING[0], ACT.Identity, bias=bias[:, 1:2])\
                   .then_inc(qkv_ready, 1)
                act.wait_ge(qkv_done, 3 * i + 3)
                if i >= 3:
                    act.wait_ge(r_ready, WIN * (i - 2))
                act.activation(vpad[:, i % 3, PAD_L:PAD_L + D], RING[1], ACT.Identity, bias=bias[:, 2:3])\
                   .then_inc(qkv_ready, 1)

            def output(i):
                act.wait_ge(out_done, i + 1)
                if i >= 1:
                    act.wait_ge(x_ready, i)
                act.activation(o[:, :], M, ACT.Identity, bias=gbo[:, 0:1], scale=gate[:, 0:1]).then_inc(o_ready, 1)

            project(0)
            for s in range(NT + 2):
                if 1 <= s <= NT:
                    act.wait_ge(shifted, s)
                    act.activation(att[:, :, :, :], att[:, :, :, :], ACT.Exp, scale=float(LHD) ** -0.5)\
                       .then_inc(exp_ready, 1)
                if s >= 2:
                    output(s - 2)
                if s + 1 < NT:
                    project(s + 1)
                if 1 <= s <= NT:
                    act.wait_ge(back_done, s)
                    if s >= 2:
                        act.wait_ge(spread_done, WIN * (s - 1))
                    act.activation(ath[:, :, :], T2, ACT.Copy).then_inc(ath_ready, 1)
                if s < NT:
                    act.wait_ge(prod_used, 4 * (s + 1))
                    if s >= 1:
                        act.wait_ge(fwd_done, s)
                    act.activation(sc[:, :, :], ps[:, 0:2, :], ACT.Copy).then_inc(sc_ready, 1)

        @block.vector
        def _(dve):
            chain = [0]

            def link(ins):
                chain[0] += 1
                ins.then_inc(dve_step, 1)
                dve.wait_ge(dve_step, chain[0])

            def statistics(i):
                dve.wait_ge(x_landed[i], 16)
                link(dve.bn_stats(stats[:, i, :], x[:, i, :]))
                link(dve.bn_aggr(mv[:, i, :], stats[:, i, :]))

            def normalise(i):
                dve.wait_ge(rstd_ready, 1 if i == 0 else 2)
                if i >= 2:
                    dve.wait_ge(qkv_done, 3 * (i - 2) + 1)
                dve.tensor_scalar(xn[:, i % 2, :], x[:, i, :], mv[:, i, 0:1], rstd[:, i:i + 1],
                                  ALU.subtract, ALU.mult).then_inc(xn_ready, 1)

            def products(i, w0):
                if i >= 1:
                    dve.wait_ge(prod_used, 4 * (i - 1) + w0 // GW + 1)
                k0 = kpad[:, i % 2, w0:w0 + D]
                windows = bass.AP(k0.tensor, k0.offset, [list(k0.ap[0]), [1, GW], [1, D]])
                qb = q[:, i % 2, :].unsqueeze(1).broadcast_to([P, GW, D])
                dve.tensor_tensor(prod[:, w0:w0 + GW, :], qb, windows, ALU.mult).then_inc(prod_ready, 1)

            statistics(0)
            dve.tensor_scalar(veps[:, 0:1], mv[:, 0, 1:2], EPS, None, ALU.add).then_inc(var_ready, 1)
            normalise(0)
            for i in range(1, NT):
                statistics(i)
            dve.tensor_scalar(veps[:, 1:NT], mv[:, 1:NT, 1], EPS, None, ALU.add).then_inc(var_ready, 1)
            normalise(1)
            for s in range(NT + 2):
                if 1 <= s <= NT:
                    dve.wait_ge(fwd_done, s)
                    link(dve.tensor_reduce(mx[:, :, :], T_win.rearrange("p b w h -> p b h w"), AX.X, ALU.max))
                    if s >= 2:
                        dve.wait_ge(back_done, s - 1)
                    dve.tensor_tensor(att[:, :, :, :], T_win, mx[:, :, :].unsqueeze(2).broadcast_to([P, D // P, WIN, BH]),
                                      ALU.subtract).then_inc(shifted, 1)
                if s < NT:
                    dve.wait_ge(qkv_ready, 3 * (s + 1))
                    products(s, 0)
                    products(s, GW)
                if 1 <= s <= NT:
                    dve.wait_ge(exp_ready, s)
                    link(dve.tensor_reduce(sm[:, :, :], att[:, :, :, :].rearrange("p b w h -> p b h w"), AX.X, ALU.add))
                    link(dve.reciprocal(rs[:, :, :], sm[:, :, :]))
                    dve.tensor_tensor(att[:, :, :, :], att[:, :, :, :],
                                      rs[:, :, :].unsqueeze(2).broadcast_to([P, D // P, WIN, BH]), ALU.mult)\
                       .then_inc(att_ready, 1)
                if s >= 2:
                    i = s - 2
                    dve.wait_ge(o_ready, i + 1)
                    dve.tensor_tensor(x[:, i, :], x[:, i, :], o[:, :], ALU.add).then_inc(x_ready, 1)
                    dve.wait_ge(x_ready, i + 1)
                    row_sums(dve, g, st, i)
                if s < NT:
                    products(s, 2 * GW)
                    products(s, 3 * GW)
                if 1 <= s <= NT:
                    i = s - 1
                    dve.wait_ge(ath_ready, s)
                    dve.tensor_tensor(atl[:, :, :], T2, ath[:, :, :].bitcast(F32), ALU.subtract).then_inc(atl_ready, 1)
                    for n, w in enumerate(ORDER):
                        if i >= 1 and n % 4 == 0:
                            dve.wait_ge(rsum_ready, 4 * (i - 1) + n // 4 + 1)
                        dve.wait_ge(spread_done, WIN * i + n + 1)
                        dve.tensor_tensor(r[:, w, :], RING[(2 + n) % 3], vpad[:, i % 3, w:w + D], ALU.mult)\
                           .then_inc(r_ready, 1)
                if s + 2 < NT:
                    normalise(s + 2)

            row_variances(dve, g, st)

        @block.tensor
        def _(pe):
            pe.wait_ge(const_landed, 16 * (NCONST + 3))

            def project(i):
                pe.wait_ge(xn_ready, i + 1)
                if i >= 3:
                    pe.wait_ge(o_ready, i - 2)
                pe.matmul(M, w4[:, 0, :], xn[:, i % 2, :], start=True, stop=True).then_inc(qkv_done, 1)
                pe.wait_ge(ctx_landed[i], 16)
                if i >= 3:
                    pe.wait_ge(r_ready, WIN * (i - 2))
                for j in (1, 2):
                    pe.matmul(RING[j - 1], w4[:, j, :], ctxt[:, i, :], start=True, stop=True).then_inc(qkv_done, 1)

            def reduce_heads(i, part):
                pe.wait_ge(prod_ready, 4 * i + part + 1)
                if i >= 1 and part == 0:
                    pe.wait_ge(sc_ready, i)
                for u in (2 * part, 2 * part + 1):
                    dst = S[u // 4][32 * (u % 4):32 * (u % 4) + 32, :]
                    pe.matmul(dst, sel[:, 0, :], prod[:, 2 * u, :], start=True, stop=False)
                    last = pe.matmul(dst, sel[:, 1, :], prod[:, 2 * u + 1, :], start=False, stop=True)
                last.then_inc(prod_used, 1)

            def output(i):
                if i + 2 < NT:
                    pe.wait_ge(qkv_ready, 3 * (i + 2) + 1)
                for w in range(WIN // 2):
                    pe.wait_ge(rsum_ready, 4 * i + w // 2 + 1)
                    last = pe.matmul(M, w4[:, 3, :], r2[:, w, :], start=(w == 0), stop=(w == WIN // 2 - 1))
                last.then_inc(out_done, 1)

            project(0)
            for s in range(NT + 2):
                if s >= 2:
                    output(s - 2)
                if s > NT:
                    continue
                if s < NT:
                    reduce_heads(s, 0)
                    reduce_heads(s, 1)
                if s >= 1:
                    pe.wait_ge(att_ready, s)
                    for grp in range(2):
                        for b in range(D // P):
                            last = pe.transpose(T2[:, grp, b * P:(b + 1) * P],
                                                att[:, b, grp * WG:(grp + 1) * WG, :].rearrange("p w h -> p (w h)"), ident[:, :])
                    last.then_inc(back_done, 1)
                if s < NT:
                    reduce_heads(s, 2)
                    reduce_heads(s, 3)
                if s + 1 < NT:
                    project(s + 1)
                if s >= 1:
                    i = s - 1
                    if i == 0:
                        pe.wait_ge(spread_ready, 1)
                    pe.wait_ge(atl_ready, s)
                    for n, w in enumerate(ORDER):
                        if n < 3:
                            pe.wait_ge(qkv_ready, 3 * min(s + 2, NT))
                        if n >= 3:
                            pe.wait_ge(r_ready, WIN * i + n - 2)
                        elif i >= 1:
                            pe.wait_ge(r_ready, WIN * i)
                        pe.matmul(RING[(2 + n) % 3], spread[:, w % WG, :], ath[:, w // WG, :], start=True, stop=False)
                        pe.matmul(RING[(2 + n) % 3], spread[:, w % WG, :], atl[:, w // WG, :], start=False, stop=True)\
                          .then_inc(spread_done, 1)
                if s < NT:
                    pe.wait_ge(sc_ready, s + 1)
                    if s >= 1:
                        pe.wait_ge(atl_ready, s)
                    for b in range(D // P):
                        for grp in range(2):
                            last = pe.transpose(T_time[:, b, grp, :], sc[:, grp, b * P:(b + 1) * P], ident[:, :])
                    last.then_inc(fwd_done, 1)


def norm_sems(sem, tag):
    names = ("xn_ready", "xt_done", "xh_ready", "xl_ready")
    return {n: sem(f"{tag}_{n}") for n in names}


def stat_sems(sem):
    return {n: sem(f"next_{n}") for n in ("sums_done", "aggr_done", "var_ready", "rstd_ready")}


def row_sums(dve, g, st, i):
    dve.bn_stats(g["stats"][:, i, :], g["x"][:, i, :]).then_inc(st["sums_done"], 1)


def row_variances(dve, g, st):
    dve.wait_ge(st["sums_done"], NT)
    for i in range(NT):
        last = dve.bn_aggr(g["mv"][:, i, :], g["stats"][:, i, :])
    last.then_inc(st["aggr_done"], 1)
    dve.wait_ge(st["aggr_done"], 1)
    dve.tensor_scalar(g["veps"][:, :], g["mv"][:, :, 1], EPS, None, ALU.add).then_inc(st["var_ready"], 1)


def row_scales(pool, g, st):
    pool.wait_ge(st["var_ready"], 1)
    pool.tensor_tensor(g["rstd"][:, :], g["veps"][:, :], g["mhalf"][:, :], ALU.pow).then_inc(st["rstd_ready"], 1)


def norm_vector(dve, g, n, xn, banks):
    ps, x, mv, rstd = g["ps"], g["x"], g["mv"], g["rstd"]

    def low_part(i):
        dve.wait_ge(n["xh_ready"], i + 1)
        t = slice(i * P, (i + 1) * P)
        dve.tensor_tensor(g["xl"][:, :, t], ps[:, banks[i % 2], :].rearrange("p (c t) -> p c t", c=DC),
                          g["xh"][:, :, t].bitcast(F32), ALU.subtract).then_inc(n["xl_ready"], 1)

    for i in range(NT):
        if i >= 2:
            dve.wait_ge(n["xt_done"], i - 1)
        dve.tensor_scalar(xn[:, i % 2, :], x[:, i, :], mv[:, i, 0:1], rstd[:, i:i + 1],
                          ALU.subtract, ALU.mult).then_inc(n["xn_ready"], 1)
        if i >= 1:
            low_part(i - 1)
    low_part(NT - 1)


def norm_scalar(act, g, n, banks):
    for i in range(NT):
        act.wait_ge(n["xt_done"], i + 1)
        act.activation(g["xh"][:, :, i * P:(i + 1) * P], g["ps"][:, banks[i % 2], :].rearrange("p (c t) -> p c t", c=DC),
                       ACT.Copy).then_inc(n["xh_ready"], 1)


def norm_tensor(pe, g, n, xn, banks):
    for i in range(NT):
        pe.wait_ge(n["xn_ready"], i + 1)
        if i >= 2:
            pe.wait_ge(n["xl_ready"], i - 1)
        for c in range(DC):
            last = pe.transpose(g["ps"][:, banks[i % 2], c * P:(c + 1) * P], xn[:, i % 2, c * P:(c + 1) * P], g["ident"][:, :])
        last.then_inc(n["xt_done"], 1)


def three_passes(pe, dst, lhs, rhs, chunks, first=True, final=True):
    for c in range(chunks):
        (lh, ll), (rh, rl) = lhs(c), rhs(c)
        pe.matmul(dst, lh, rh, start=(first and c == 0), stop=False)
        pe.matmul(dst, lh, rl, start=False, stop=False)
        last = pe.matmul(dst, ll, rh, start=False, stop=(final and c == chunks - 1))
    return last


def routed_lora(nc, a, g):
    ps, x, ident, gate = g["ps"], g["x"], g["ident"], g["gate"]
    ER = NE * RANK
    with ExitStack() as ctx:
        def sb(name, shape, dt=F32):
            return ctx.enter_context(nc.sbuf_tensor(name, shape, dt))

        def sem(name):
            return ctx.enter_context(nc.semaphore("b_" + name))

        xn = sb("b_xn", [P, 2, D])
        wb_raw = sb("wb_raw", [P, DC, D])
        wbh = sb("wbh", [P, DC, D], F32R)
        wbl = sb("wbl", [P, DC, D], F32R)
        la_raw = sb("la_raw", [P, DC, ER + NE])
        lah = sb("lah", [P, DC, ER + NE], F32R)
        lal = sb("lal", [P, DC, ER + NE], F32R)
        lb = sb("lb", [P, D])
        bb = sb("bb", [P, D])
        gb = sb("gb", [P, D])
        iota = sb("iota", [P, NE])
        lgT = sb("lgT", [NE, TOK])
        hT = sb("hT", [P, TOK])
        lg = sb("lg", [P, NT, NE])
        top8 = sb("top8", [P, NT, 8])
        idx = sb("idx", [P, NT, 8], U32)
        idxf = sb("idxf", [P, NT, 8])
        dl = sb("dl", [P, NT])
        e2 = sb("e2", [P, NT])
        den = sb("den", [P, NT])
        w1 = sb("w1", [P, NT])
        w2 = sb("w2", [P, NT])
        wa = sb("wa", [P, NT, NE])
        wc = sb("wc", [P, NT, NE])
        wx = sb("wx", [P, 2, ER])
        hwT = sb("hwT", [P, 2, P])
        c_raw = sb("c_raw", [P, 2, HALF])
        ch, cl = g["ch"], g["cl"]
        gnum = sb("gnum", [P, 1])
        gi = sb("gi", [P, INTER], I32)
        gf = sb("gf", [P, INTER])
        srow = sb("srow", [P, INTER])
        rest = sb("rest", [P, INTER])
        zq = sb("zq", [P, INTER // PACK], I32)

        loaded = sem("loaded")
        wh_ready = sem("wh_ready")
        wl_ready = sem("wl_ready")
        gb_ready = sem("gb_ready")
        xb_ready = sem("xb_ready")
        step = sem("step")
        n = norm_sems(sem, "n")
        st = stat_sems(sem)
        c_landed = [sem(f"c_landed{i}") for i in range(2)]
        ch_ready = sem("ch_ready")
        cl_ready = sem("cl_ready")
        gnum_landed = sem("gnum_landed")
        cleared = sem("cleared")
        idx_landed = sem("idx_landed")
        rows_ready = sem("rows_ready")
        small_done = sem("small_done")
        small_ready = sem("small_ready")
        lg_done = sem("lg_done")
        lg_ready = sem("lg_ready")
        diff_ready = sem("diff_ready")
        e2_ready = sem("e2_ready")
        wx_ready = sem("wx_ready")
        wxT_done = sem("wxT_done")
        hw_ready = sem("hw_ready")
        out_done = sem("out_done")
        x_ready = sem("x_ready")

        XT = (0, 1)
        SMALL = (2, 3)
        LG, WX, OUT = 4, 5, (6, 7, 0, 1)

        block = ctx.enter_context(nc.Block())

        def load_groups(sp, m):
            name, k, ncols, groups = MATS[m]
            if m == 0:
                sp.wait_ge(cleared, 2)
            else:
                sp.wait_ge(rows_ready, m)
            sp.dma_start(gi[:, 0:k], a[name + "_g_idx"].partition_broadcast(P)).then_inc(idx_landed, 16)
            for b in range(3):
                sp.dma_start(srow[32 * b:32 * b + groups, 0:ncols], a[name + "_scales"]).then_inc(idx_landed, 16)
            sp.dma_start(zq[96:96 + groups, 0:ncols // PACK], a[name + "_qzeros"]).then_inc(idx_landed, 16)

        @block.sync
        def _(sp):
            sp.dma_start(wb_raw[:, :, :], a["W_base"].rearrange("(c p) n -> p c n", p=P)).then_inc(loaded, 16)
            sp.dma_start(la_raw[:, :, 0:ER], a["lora_A"].rearrange("(c p) n -> p c n", p=P)).then_inc(loaded, 16)
            sp.dma_start(la_raw[:, :, ER:], a["W_router"].rearrange("(c p) n -> p c n", p=P)).then_inc(loaded, 16)
            sp.dma_start(lb[:, :], a["lora_B"]).then_inc(loaded, 16)
            sp.dma_start(bb[:, :], a["b_base"].partition_broadcast(P)).then_inc(loaded, 16)
            sp.dma_start(iota[:, :], a["iota"].partition_broadcast(P)).then_inc(loaded, 16)
            sp.dma_start(gnum[:, :], a["gnum"]).then_inc(gnum_landed, 16)
            load_groups(sp, 0)
            cT = a["ctxT"].rearrange("(c p) t -> p c t", p=P)
            for u in range(DC * NHALF):
                c, h = u % DC, u // DC
                if u >= 2:
                    sp.wait_ge(cl_ready, u - 1)
                sp.dma_start(c_raw[:, u % 2, :], cT[:, c, h * HALF:(h + 1) * HALF]).then_inc(c_landed[u % 2], 16)
            load_groups(sp, 1)
            load_groups(sp, 2)

        @block.gpsimd
        def _(pool):
            pool.memset(srow[:, :], 0.0).then_inc(cleared, 1)
            pool.memset(zq[:, :], 0).then_inc(cleared, 1)
            pool.wait_ge(wh_ready, 2)
            pool.tensor_tensor(lal[:, :, :], la_raw[:, :, :], lah[:, :, :].bitcast(F32), ALU.subtract).then_inc(wl_ready, 1)
            pool.tensor_tensor(wbl[:, :, :], wb_raw[:, :, :], wbh[:, :, :].bitcast(F32), ALU.subtract).then_inc(wl_ready, 1)
            pool.wait_ge(gb_ready, 1)
            for i in range(NT):
                pool.wait_ge(n["xn_ready"], i + 1)
                pool.tensor_tensor(x[:, i, :], x[:, i, :], gb[:, :], ALU.add).then_inc(xb_ready, 1)
            for u in range(DC * NHALF):
                c, h = u % DC, u // DC
                t = slice(h * HALF, (h + 1) * HALF)
                pool.wait_ge(ch_ready, u + 1)
                pool.tensor_tensor(cl[:, c, t], c_raw[:, u % 2, :], ch[:, c, t].bitcast(F32), ALU.subtract).then_inc(cl_ready, 1)
            row_scales(pool, g, st)

        @block.scalar
        def _(act):
            act.wait_ge(loaded, 16 * 6)
            act.activation(lah[:, :, :], la_raw[:, :, :], ACT.Copy).then_inc(wh_ready, 1)
            act.activation(wbh[:, :, :], wb_raw[:, :, :], ACT.Copy).then_inc(wh_ready, 1)
            act.activation(gb[:, :], bb[:, :], ACT.Copy, scale=gate[:, 2:3]).then_inc(gb_ready, 1)
            norm_scalar(act, g, n, XT)
            for h in range(NHALF):
                t = slice(h * HALF, (h + 1) * HALF)
                act.wait_ge(small_done, 2 * h + 1)
                act.activation(lgT[:, t], ps[0:NE, SMALL[0], :], ACT.Copy).then_inc(small_ready, 1)
                act.wait_ge(small_done, 2 * h + 2)
                act.activation(hT[:, t], ps[:, SMALL[1], :], ACT.Copy).then_inc(small_ready, 1)
            act.wait_ge(diff_ready, 1)
            act.activation(e2[:, :], dl[:, :], ACT.Exp).then_inc(e2_ready, 1)
            for u in range(DC * NHALF):
                c, h = u % DC, u // DC
                act.wait_ge(c_landed[u % 2], 16 * (u // 2 + 1))
                act.activation(ch[:, c, h * HALF:(h + 1) * HALF], c_raw[:, u % 2, :], ACT.Copy).then_inc(ch_ready, 1)

        @block.vector
        def _(dve):
            norm_vector(dve, g, n, xn, XT)
            chain = [0]

            def link(ins):
                chain[0] += 1
                ins.then_inc(step, 1)
                dve.wait_ge(step, chain[0])

            def groups_of(m):
                name, k, ncols, groups = MATS[m]
                rows = g["rows"]
                dve.wait_ge(idx_landed, 80 * (m + 1))
                link(dve.tensor_copy(gf[:, 0:k], gi[:, 0:k]))
                link(dve.tensor_scalar(rest[:, 0:k], gf[:, 0:k], 0.0, float(groups), ALU.is_lt, ALU.mult))
                link(dve.tensor_tensor(gf[:, 0:k], gf[:, 0:k], rest[:, 0:k], ALU.add))
                link(dve.tensor_scalar(gf[:, 0:k], gf[:, 0:k], float(groups - 1), 0.0, ALU.min, ALU.max))
                dve.tensor_scalar(g["onehot"][:, ROW0[m]:ROW0[m] + k], gf[:, 0:k], gnum[:, 0:1], None, ALU.is_equal)
                cols = slice(COL0[m], COL0[m] + ncols)
                link(dve.tensor_copy(rows[0:96, cols], srow[0:96, 0:ncols]))
                link(dve.tensor_tensor(rest[0:96, 0:ncols], srow[0:96, 0:ncols], rows[0:96, cols], ALU.subtract))
                link(dve.tensor_copy(rows[32:64, cols], rest[32:64, 0:ncols]))
                link(dve.tensor_copy(rows[64:96, cols], rest[64:96, 0:ncols]))
                link(dve.tensor_tensor(rest[64:96, 0:ncols], rest[64:96, 0:ncols], rows[64:96, cols], ALU.subtract))
                link(dve.tensor_copy(rows[64:96, cols], rest[64:96, 0:ncols]))
                for j in range(PACK):
                    last = dve.tensor_scalar(gi[96:128, j:ncols:PACK], zq[96:128, 0:ncols // PACK], BITS * j, 15,
                                             ALU.logical_shift_right, ALU.bitwise_and)
                link(last)
                dve.tensor_scalar(rows[96:128, cols], gi[96:128, 0:ncols], 1.0, None, ALU.add).then_inc(rows_ready, 1)

            dve.wait_ge(gnum_landed, 16)
            groups_of(0)
            dve.wait_ge(lg_done, 1)
            link(dve.tensor_copy(lg[:, :, :], ps[:, LG, 0:NT * NE].rearrange("p (i e) -> p i e", e=NE)))
            for i in range(NT):
                last = dve.max(top8[:, i, :], lg[:, i, :])
            link(last)
            for i in range(NT):
                last = dve.max_index(idx[:, i, :], top8[:, i, :], lg[:, i, :])
            link(last)
            dve.tensor_tensor(dl[:, :], top8[:, :, 1], top8[:, :, 0], ALU.subtract).then_inc(diff_ready, 1)
            link(dve.tensor_copy(idxf[:, :, :], idx[:, :, :]))
            dve.wait_ge(e2_ready, 1)
            link(dve.tensor_scalar(den[:, :], e2[:, :], 1.0, None, ALU.add))
            link(dve.reciprocal(w1[:, :], den[:, :]))
            link(dve.tensor_tensor(w2[:, :], w1[:, :], e2[:, :], ALU.mult))
            for i in range(NT):
                dve.tensor_scalar(wa[:, i, :], iota[:, :], idxf[:, i, 0:1], w1[:, i:i + 1], ALU.is_equal, ALU.mult)
                last = dve.tensor_scalar(wc[:, i, :], iota[:, :], idxf[:, i, 1:2], w2[:, i:i + 1], ALU.is_equal, ALU.mult)
            link(last)
            link(dve.tensor_tensor(wa[:, :, :], wa[:, :, :], wc[:, :, :], ALU.add))

            def widen(i):
                if i >= 2:
                    dve.wait_ge(wxT_done, i - 1)
                dve.tensor_scalar(wx[:, i % 2, :].rearrange("p (e r) -> p e r", e=NE),
                                  wa[:, i, :].unsqueeze(2).broadcast_to([P, NE, RANK]), LORA_SCALE, None, ALU.mult)\
                   .then_inc(wx_ready, 1)

            widen(0)
            dve.wait_ge(small_ready, 2 * NHALF)
            for i in range(NT + 1):
                if i + 1 < NT:
                    widen(i + 1)
                if i < NT:
                    dve.wait_ge(wxT_done, i + 1)
                    if i >= 2:
                        dve.wait_ge(out_done, i - 1)
                    dve.tensor_tensor(hwT[:, i % 2, :], ps[:, WX, 0:P], hT[:, i * P:(i + 1) * P], ALU.mult)\
                       .then_inc(hw_ready, 1)
                if i >= 1:
                    j = i - 1
                    dve.wait_ge(out_done, i)
                    dve.wait_ge(xb_ready, i)
                    dve.scalar_tensor_tensor(x[:, j, :], ps[:, OUT[j % 4], :], gate[:, 2:3], x[:, j, :], ALU.mult, ALU.add)\
                       .then_inc(x_ready, 1)
                    dve.wait_ge(x_ready, i)
                    row_sums(dve, g, st, j)
                if i == 2:
                    groups_of(1)
            groups_of(2)
            row_variances(dve, g, st)

        @block.tensor
        def _(pe):
            norm_tensor(pe, g, n, xn, XT)
            pe.wait_ge(wl_ready, 1)
            for h in range(NHALF):
                t = slice(h * HALF, (h + 1) * HALF)
                pe.wait_ge(n["xl_ready"], TPH * (h + 1))
                for part, cols in enumerate((slice(ER, ER + NE), slice(0, ER))):
                    if h >= 1:
                        pe.wait_ge(small_ready, 2 * (h - 1) + part + 1)
                    m = cols.stop - cols.start
                    three_passes(pe, ps[0:m, SMALL[part], :], lambda c: (lah[:, c, cols], lal[:, c, cols]),
                                 lambda c: (g["xh"][:, c, t], g["xl"][:, c, t]), DC).then_inc(small_done, 1)
            pe.wait_ge(small_ready, 2 * NHALF - 1)
            for i in range(NT):
                last = pe.transpose(ps[:, LG, NE * i:NE * i + NE], lgT[:, i * P:(i + 1) * P], ident[0:NE, 0:NE])
            last.then_inc(lg_done, 1)

            def base(i):
                t = slice(i * P, (i + 1) * P)
                if i >= 4:
                    pe.wait_ge(x_ready, i - 3)
                three_passes(pe, ps[:, OUT[i % 4], :], lambda c: (g["xh"][:, c, t], g["xl"][:, c, t]),
                             lambda c: (wbh[:, c, :], wbl[:, c, :]), DC, final=False)

            def experts(i):
                pe.wait_ge(wx_ready, i + 1)
                if i >= 1:
                    pe.wait_ge(hw_ready, i)
                pe.transpose(ps[:, WX, 0:P], wx[:, i % 2, :], ident[:, :]).then_inc(wxT_done, 1)
                if i + 3 < NT and i >= 1:
                    base(i + 3)
                pe.wait_ge(hw_ready, i + 1)
                pe.matmul(ps[:, OUT[i % 4], :], hwT[:, i % 2, :], lb[:, :], start=False, stop=True).then_inc(out_done, 1)

            pe.wait_ge(wl_ready, 2)
            for i in range(4):
                base(i)
            for i in range(NT):
                experts(i)


def rotary_attention(nc, a, g):
    ps, x, ident, gate = g["ps"], g["x"], g["ident"], g["gate"]
    wq_raw, wo_raw, wkv_raw = g["wq_raw"], g["wo_raw"], g["wkv_raw"]
    SCALE = float(np.float32(1.0) / np.sqrt(np.float32(DK)))
    with ExitStack() as ctx:
        def sb(name, shape, dt=F32):
            return ctx.enter_context(nc.sbuf_tensor(name, shape, dt))

        def sem(name):
            return ctx.enter_context(nc.semaphore("c_" + name))

        ch, cl = g["ch"], g["cl"]
        cs = sb("cs", [P, 2, C])
        mask = sb("mask", [P, NT, C])
        wqh = sb("wqh", [P, DC, GRP * DK], F32R)
        wql = sb("wql", [P, DC, GRP * DK], F32R)
        wkvh = sb("wkvh", [P, 2, DC, DK], F32R)
        wkvl = sb("wkvl", [P, 2, DC, DK], F32R)
        woh = sb("woh", [P, GRP, D], F32R)
        wol = sb("wol", [P, GRP, D], F32R)
        qT = sb("qT", [P, GRP, TOK])
        kT = sb("kT", [P, TOK])
        vT = sb("vT", [P, 2, HALF])
        v = sb("v", [P, NT, DK])
        ra = sb("ra", [P, 2, HALF])
        rb = sb("rb", [P, 2, HALF])
        xn = ra
        s = sb("s", [P, 2, GRP, C])
        mx = sb("c_mx", [P, GRP])
        sm = sb("c_sm", [P, GRP])
        rs = sb("c_rs", [P, 2, GRP])
        bd = sb("bd", [P, 2, GRP, P])
        aT = sb("aT", [P, GRP * P])
        oh = sb("oh", [P, 2, GRP * P], F32R)
        ol = sb("ol", [P, 2, GRP * P], F32R)

        n = norm_sems(sem, "n")
        loaded = sem("loaded")
        st = stat_sems(sem)
        bd_zeroed = sem("bd_zeroed")
        wkvh_ready, wkvl_ready = sem("wkvh_ready"), sem("wkvl_ready")
        wqh_ready, wql_ready = sem("wqh_ready"), sem("wql_ready")
        woh_ready, wol_ready = sem("woh_ready"), sem("wol_ready")
        proj_done = sem("proj_done")
        rope_a = sem("rope_a")
        rope_ready = sem("rope_ready")
        vproj_done = sem("vproj_done")
        vT_ready = sem("vT_ready")
        vtr_done = sem("vtr_done")
        v_ready = sem("v_ready")
        sc_done = sem("sc_done")
        masked = sem("masked")
        max_ready = sem("max_ready")
        shifted = sem("shifted")
        exp_ready = sem("exp_ready")
        rs_ready = sem("rs_ready")
        bd_ready = sem("bd_ready")
        aT_done = sem("aT_done")
        aT_ready = sem("aT_ready")
        pv_done = sem("pv_done")
        oh_ready, ol_ready = sem("oh_ready"), sem("ol_ready")
        wo_done = sem("wo_done")
        x_ready = sem("x_ready")
        sum_step = sem("sum_step")

        PROJ = (0, 1)
        SCB = (2, 3)
        TR, PV, WO, VT = 4, 5, (6, 7), 4
        NPROJ = (1 + GRP) * NHALF
        LAST = NT + 3

        block = ctx.enter_context(nc.Block())

        @block.sync
        def _(sp):
            sp.dma_start(cs[:, :, :], a["rope"].rearrange("p (a t) -> p a t", a=2)).then_inc(loaded, 16)
            sp.dma_start(mask[:, :, :], a["mask"].rearrange("(i b) q k -> (b q) i k", b=BT)).then_inc(loaded, 16)
            for kv in range(1, NKV):
                sp.wait_ge(wkvl_ready, kv)
                sp.wait_ge(wql_ready, kv)
                qkv_weight_loads(sp, a, g, kv)
                sp.wait_ge(wol_ready, kv)
                out_weight_load(sp, a, g, kv)

        @block.gpsimd
        def _(pool):
            pool.memset(bd[:, :, :, :], 0.0).then_inc(bd_zeroed, 1)
            def low_kv(kv):
                pool.wait_ge(wkvh_ready, kv + 1)
                pool.tensor_tensor(wkvl[:, :, :, :], wkv_raw[:, :, :, :], wkvh[:, :, :, :].bitcast(F32), ALU.subtract)\
                    .then_inc(wkvl_ready, 1)

            def low_q(kv):
                pool.wait_ge(wqh_ready, kv + 1)
                pool.tensor_tensor(wql[:, :, :], wq_raw[:, :, :], wqh[:, :, :].bitcast(F32), ALU.subtract)\
                    .then_inc(wql_ready, 1)

            def low_o(kv):
                pool.wait_ge(woh_ready, kv + 1)
                pool.tensor_tensor(wol[:, :, :], wo_raw[:, :, :], woh[:, :, :].bitcast(F32), ALU.subtract)\
                    .then_inc(wol_ready, 1)

            def rotary_sum(kv, u):
                m = NPROJ * kv + u
                pool.wait_ge(rope_a, m + 1)
                if u < NHALF:
                    if kv >= 1:
                        pool.wait_ge(sc_done, NT * kv)
                    dst = kT[:, u * HALF:(u + 1) * HALF]
                else:
                    h, head = (u - NHALF) // GRP, (u - NHALF) % GRP
                    dst = qT[:, head, h * HALF:(h + 1) * HALF]
                pool.tensor_tensor(dst, ra[:, m % 2, :], rb[:, m % 2, :], ALU.add).then_inc(rope_ready, 1)

            def shift(m):
                pool.wait_ge(max_ready, m + 1)
                pool.tensor_tensor(s[:, m % 2, :, :], s[:, m % 2, :, :],
                                   mx[:, :].unsqueeze(2).broadcast_to([P, GRP, C]), ALU.subtract).then_inc(shifted, 1)

            low_kv(0)
            low_q(0)
            for u in range(NHALF):
                rotary_sum(0, u)
            for kv in range(NKV):
                low_o(kv)
                for u in range(NHALF, NPROJ):
                    rotary_sum(kv, u)
                    if u == NHALF + GRP + 1:
                        shift(NT * kv)
                    if u == NPROJ - 1:
                        shift(NT * kv + 1)
                for i in range(2, NT):
                    m = NT * kv + i
                    shift(m)
                    if i == 4 and kv + 1 < NKV:
                        low_kv(kv + 1)
                    if i == 6 and kv + 1 < NKV:
                        low_q(kv + 1)
                if kv + 1 < NKV:
                    for u in range(NHALF):
                        rotary_sum(kv + 1, u)
            row_scales(pool, g, st)

        @block.scalar
        def _(act):
            def high_kv(kv):
                act.wait_ge(g["wkv_landed"], 32 * (kv + 1))
                if kv >= 1:
                    act.wait_ge(vproj_done, NHALF * kv)
                act.activation(wkvh[:, :, :, :], wkv_raw[:, :, :, :], ACT.Copy).then_inc(wkvh_ready, 1)

            def high_q(kv):
                act.wait_ge(g["wq_landed"], 16 * (kv + 1))
                if kv >= 1:
                    act.wait_ge(proj_done, NPROJ * kv)
                act.activation(wqh[:, :, :], wq_raw[:, :, :], ACT.Copy).then_inc(wqh_ready, 1)

            def high_o(kv):
                act.wait_ge(g["wo_landed"], 16 * (kv + 1))
                if kv >= 1:
                    act.wait_ge(wo_done, NT * kv)
                act.activation(woh[:, :, :], wo_raw[:, :, :], ACT.Copy).then_inc(woh_ready, 1)

            def values(kv):
                for h in range(NHALF):
                    m = NHALF * kv + h
                    act.wait_ge(vproj_done, m + 1)
                    act.activation(vT[:, h, :], ps[:, PROJ[h], :], ACT.Copy).then_inc(vT_ready, 1)
                for h in range(NHALF):
                    m = NHALF * kv + h
                    act.wait_ge(vtr_done, m + 1)
                    act.activation(v[:, h * TPH:(h + 1) * TPH, :], ps[:, VT, :].rearrange("p (i d) -> p i d", i=TPH),
                                   ACT.Copy).then_inc(v_ready, 1)

            def exps(m):
                act.wait_ge(shifted, m + 1)
                act.activation(s[:, m % 2, :, :], s[:, m % 2, :, :], ACT.Exp).then_inc(exp_ready, 1)

            def turned(m):
                act.wait_ge(aT_done, m + 1)
                if m >= 1:
                    act.wait_ge(pv_done, m)
                act.activation(aT[:, :], ps[:, TR, :], ACT.Copy).then_inc(aT_ready, 1)

            def high_out(m):
                act.wait_ge(pv_done, m + 1)
                if m >= 2:
                    act.wait_ge(wo_done, m - 1)
                act.activation(oh[:, m % 2, :], ps[:, PV, :], ACT.Copy).then_inc(oh_ready, 1)

            high_kv(0)
            high_q(0)
            norm_scalar(act, g, n, PROJ)
            values(0)
            for kv in range(NKV):
                high_o(kv)
                for i in range(NT + 2):
                    m = NT * kv + i
                    if i >= 2:
                        turned(m - 2)
                    if i < NT:
                        exps(m)
                    if i == 2 and kv + 1 < NKV:
                        high_kv(kv + 1)
                        high_q(kv + 1)
                    if i >= 2:
                        high_out(m - 2)
                if kv + 1 < NKV:
                    values(kv + 1)

        @block.vector
        def _(dve):
            dve.wait_ge(loaded, 32)
            norm_vector(dve, g, n, xn, PROJ)
            dve.wait_ge(bd_zeroed, 1)

            def rotary(kv, u):
                m = NPROJ * kv + u
                bank = ps[:, PROJ[u % 2], :].rearrange("p (b t) -> p b t", t=C)
                dve.wait_ge(proj_done, m + 1)
                if m == 0:
                    dve.wait_ge(n["xt_done"], NT)
                if m >= 2:
                    dve.wait_ge(rope_ready, m - 1)
                A = ra[:, m % 2, :].rearrange("p (b t) -> p b t", t=C)
                R_ = rb[:, m % 2, :].rearrange("p (b t) -> p b t", t=C)
                nb = HALF // C
                hd = DK // 2
                dve.tensor_tensor(A, bank, cs[:, 0, :].unsqueeze(1).broadcast_to([P, nb, C]), ALU.mult)
                dve.tensor_tensor(R_[0:hd], bank[hd:DK], cs[0:hd, 1, :].unsqueeze(1).broadcast_to([hd, nb, C]), ALU.mult)
                dve.tensor_tensor(R_[hd:DK], bank[0:hd], cs[hd:DK, 1, :].unsqueeze(1).broadcast_to([hd, nb, C]), ALU.mult)\
                   .then_inc(rope_a, 1)

            def maximum(m, i):
                dve.wait_ge(sc_done, m + 1)
                if m >= 2:
                    dve.wait_ge(bd_ready, 2 * (m - 1))
                bank = ps[:, SCB[m % 2], :].rearrange("p (h k) -> p h k", h=GRP)
                for b in range(BT):
                    rows = slice(b * C, (b + 1) * C)
                    last = dve.scalar_tensor_tensor(s[rows, m % 2, :, :], bank[rows, :, b * C:(b + 1) * C], SCALE,
                                                    mask[rows, i, :].unsqueeze(1).broadcast_to([C, GRP, C]), ALU.mult, ALU.add)
                    last.then_inc(masked, 1)
                dve.wait_ge(masked, 2 * (m + 1))
                if m >= 1:
                    dve.wait_ge(shifted, m)
                dve.tensor_reduce(mx[:, :], s[:, m % 2, :, :], AX.X, ALU.max).then_inc(max_ready, 1)

            def sums(m):
                dve.wait_ge(exp_ready, m + 1)
                dve.tensor_reduce(sm[:, :], s[:, m % 2, :, :], AX.X, ALU.add).then_inc(sum_step, 1)
                dve.wait_ge(sum_step, m + 1)
                dve.reciprocal(rs[:, m % 2, :], sm[:, :]).then_inc(rs_ready, 1)
                dve.wait_ge(rs_ready, m + 1)
                if m >= 2:
                    dve.wait_ge(aT_done, m - 1)
                for b in range(BT):
                    rows = slice(b * C, (b + 1) * C)
                    dve.tensor_tensor(bd[rows, m % 2, :, b * C:(b + 1) * C], s[rows, m % 2, :, :],
                                      rs[rows, m % 2, :].unsqueeze(2).broadcast_to([C, GRP, C]), ALU.mult)\
                       .then_inc(bd_ready, 1)

            def low_out(m):
                dve.wait_ge(oh_ready, m + 1)
                dve.tensor_tensor(ol[:, m % 2, :], ps[:, PV, :], oh[:, m % 2, :].bitcast(F32), ALU.subtract).then_inc(ol_ready, 1)

            def add(m, i):
                dve.wait_ge(wo_done, m + 1)
                dve.scalar_tensor_tensor(x[:, i, :], ps[:, WO[m % 2], :], gate[:, 1:2], x[:, i, :], ALU.mult, ALU.add)\
                   .then_inc(x_ready, 1)
                if m >= NT * (NKV - 1):
                    dve.wait_ge(x_ready, m + 1)
                    row_sums(dve, g, st, i)

            for u in range(NHALF):
                rotary(0, u)
            for kv in range(NKV):
                for u in range(NHALF, NPROJ):
                    rotary(kv, u)
                    if u == NHALF + GRP:
                        maximum(NT * kv, 0)
                    if u == NPROJ - 2:
                        sums(NT * kv)
                        maximum(NT * kv + 1, 1)
                for i in range(2, LAST):
                    m = NT * kv + i
                    if i - 1 < NT:
                        sums(m - 1)
                    if i < NT:
                        maximum(m, i)
                    if i >= 3:
                        add(m - 3, i - 3)
                    if 2 <= i < NT + 2:
                        low_out(m - 2)
                    if NT <= i < NT + NHALF and kv + 1 < NKV:
                        rotary(kv + 1, i - NT)
            row_variances(dve, g, st)

        @block.tensor
        def _(pe):
            norm_tensor(pe, g, n, xn, PROJ)

            def project(kv, u):
                m = NPROJ * kv + u
                if u == 0:
                    pe.wait_ge(wkvl_ready, kv + 1)
                if u == NHALF:
                    pe.wait_ge(wql_ready, kv + 1)
                if m >= 2:
                    pe.wait_ge(rope_a, m - 1)
                if NHALF <= u < 2 * NHALF:
                    pe.wait_ge(vT_ready, NHALF * kv + u - NHALF + 1)
                if u < NHALF:
                    t = slice(u * HALF, (u + 1) * HALF)
                    last = three_passes(pe, ps[:, PROJ[u % 2], :], lambda c: (wkvh[:, 0, c, :], wkvl[:, 0, c, :]),
                                        lambda c: (ch[:, c, t], cl[:, c, t]), DC)
                else:
                    h, head = (u - NHALF) // GRP, (u - NHALF) % GRP
                    t = slice(h * HALF, (h + 1) * HALF)
                    cols = slice(head * DK, (head + 1) * DK)
                    last = three_passes(pe, ps[:, PROJ[u % 2], :], lambda c: (wqh[:, c, cols], wql[:, c, cols]),
                                        lambda c: (g["xh"][:, c, t], g["xl"][:, c, t]), DC)
                last.then_inc(proj_done, 1)

            def project_v(kv, h):
                m = NHALF * kv + h
                t = slice(h * HALF, (h + 1) * HALF)
                pe.wait_ge(rope_a, NPROJ * kv + h + 1)
                three_passes(pe, ps[:, PROJ[h], :], lambda c: (wkvh[:, 1, c, :], wkvl[:, 1, c, :]),
                             lambda c: (ch[:, c, t], cl[:, c, t]), DC).then_inc(vproj_done, 1)

            def turn_v(kv, h):
                m = NHALF * kv + h
                pe.wait_ge(vT_ready, m + 1)
                if kv >= 1:
                    pe.wait_ge(aT_ready, NT * kv)
                if m >= 1:
                    pe.wait_ge(v_ready, m)
                for i in range(TPH):
                    last = pe.transpose(ps[:, VT, i * P:(i + 1) * P], vT[:, h, i * P:(i + 1) * P], ident[:, :])
                last.then_inc(vtr_done, 1)

            def scores(m, i):
                pe.wait_ge(rope_ready, NPROJ * (m // NT) + NHALF + GRP * (i // TPH + 1))
                if m >= 2:
                    pe.wait_ge(masked, 2 * (m - 1))
                t = slice(i * P, (i + 1) * P)
                for h in range(GRP):
                    last = pe.matmul(ps[:, SCB[m % 2], h * P:(h + 1) * P], qT[:, h, t], kT[:, t], start=True, stop=True)
                last.then_inc(sc_done, 1)

            def turn(m):
                pe.wait_ge(bd_ready, 2 * (m + 1))
                if m >= 1:
                    pe.wait_ge(aT_ready, m)
                if m % NT == 0:
                    pe.wait_ge(v_ready, NHALF * (m // NT + 1))
                for h in range(GRP):
                    last = pe.transpose(ps[:, TR, h * P:(h + 1) * P], bd[:, m % 2, h, :], ident[:, :])
                last.then_inc(aT_done, 1)

            def weighted(m, i):
                pe.wait_ge(aT_ready, m + 1)
                if m >= 1:
                    pe.wait_ge(ol_ready, m)
                pe.matmul(ps[:, PV, :], v[:, i, :], aT[:, :], start=True, stop=True).then_inc(pv_done, 1)

            def project_out(m):
                if m % NT == 0:
                    pe.wait_ge(wol_ready, m // NT + 1)
                pe.wait_ge(ol_ready, m + 1)
                if m >= 2:
                    pe.wait_ge(x_ready, m - 1)
                three_passes(pe, ps[:, WO[m % 2], :],
                             lambda h: (oh[:, m % 2, h * P:(h + 1) * P], ol[:, m % 2, h * P:(h + 1) * P]),
                             lambda h: (woh[:, h, :], wol[:, h, :]), GRP).then_inc(wo_done, 1)

            pe.wait_ge(n["xl_ready"], NT)
            project(0, 0)
            project(0, 1)
            project_v(0, 0)
            project_v(0, 1)
            for kv in range(NKV):
                for u in range(NHALF, NPROJ):
                    project(kv, u)
                    if u < 2 * NHALF:
                        turn_v(kv, u - NHALF)
                    if u == NHALF + GRP:
                        scores(NT * kv, 0)
                    if u == NPROJ - 2:
                        scores(NT * kv + 1, 1)
                for i in range(2, LAST):
                    m = NT * kv + i
                    more = kv + 1 < NKV
                    if i < NT:
                        scores(m, i)
                    if i < NT + 2:
                        turn(m - 2)
                    if i >= 3:
                        project_out(m - 3)
                    if i < NT + 2:
                        weighted(m - 2, i - 2)
                    if more and i == NT:
                        project(kv + 1, 0)
                    if more and i == NT + 1:
                        project(kv + 1, 1)
                    if more and i == NT + 2:
                        project_v(kv + 1, 0)
                        project_v(kv + 1, 1)


def gate_up(nc, a, g):
    ps, x, ident, gate, h, wd = g["ps"], g["x"], g["ident"], g["gate"], g["h"], g["wd"]
    QR = P // PACK
    onehot, rows = g["onehot"], g["rows"]
    with ExitStack() as ctx:
        def sb(name, shape, dt=F32):
            return ctx.enter_context(nc.sbuf_tensor(name, shape, dt))

        def sem(name):
            return ctx.enter_context(nc.semaphore("d_" + name))

        xn = sb("d_xn", [P, 2, D])
        nib = sb("nib", [P, 1], I32)
        qraw = sb("qraw", [P, 2, D], I32)
        qn = sb("qn", [P, D], I32)
        wf = sb("wf", [P, 2, D])
        wh = sb("wh", [P, 4, D], F32R)
        wl = sb("wl", [P, 4, D], F32R)
        th = sb("th", [P, HALF])
        sg = sb("sg", [P, HALF])

        n = norm_sems(sem, "n")
        consts = sem("consts")
        step = sem("step")
        q_landed = [sem(f"q_landed{i}") for i in range(2)]
        zs_done = sem("zs_done")
        q_used = sem("q_used")
        unit_ready = sem("unit_ready")
        wh_ready = sem("wh_ready")
        wl_ready = sem("wl_ready")
        gu_done = sem("gu_done")
        th_ready = sem("th_ready")
        h_ready = sem("h_ready")

        Z, SC = (0, 1), (2, 3)
        GU = (4, 5, 6, 7)
        UNITS = 3 * NTI

        block = ctx.enter_context(nc.Block())

        def packed(t, m):
            name, k, ncols, _ = MATS[m]
            q = a[name + "_qweight"]
            if m < 2:
                return [(QR, bass.AP(q.tensor, q.offset + QR * c * ncols + P * t, [[ncols, QR], [0, PACK], [1, inner(t)]]))
                        for c in range(DC)]
            r = inner(t) // PACK
            return [(r, bass.AP(q.tensor, q.offset + QR * t * ncols, [[ncols, r], [0, PACK], [1, ncols]]))]

        def load_unit(sp, u):
            t, m = u // 3, u % 3
            if u >= 2:
                sp.wait_ge(q_used, u - 1)
            for c, (r, src) in enumerate(packed(t, m)):
                w = inner(t) if m < 2 else D
                dst = qraw[0:PACK * r, u % 2, c * P:c * P + w]
                sp.dma_start(dst, src).then_inc(q_landed[u % 2], 16)

        @block.sync
        def _(sp):
            sp.dma_start(nib[:, :], a["nib"]).then_inc(consts, 16)
            for u in range(UNITS):
                load_unit(sp, u)

        def landed(u):
            return 16 * sum(DC if v % 3 < 2 else 1 for v in range(u % 2, u + 1, 2))

        def unit_view(buf, t, m):
            if m == 2:
                return buf[0:inner(t), :]
            return buf.rearrange("p (c n) -> p c n", c=DC)[:, :, 0:inner(t)]

        @block.gpsimd
        def _(pool):
            for u in range(UNITS):
                t, m = u // 3, u % 3
                if m == 2:
                    continue
                k = 2 * t + m
                pool.wait_ge(wh_ready, k + 1)
                pool.tensor_tensor(unit_view(wl[:, k % 4, :], t, m), unit_view(wf[:, m, :], t, m),
                                   unit_view(wh[:, k % 4, :], t, m).bitcast(F32), ALU.subtract).then_inc(wl_ready, 1)

        @block.scalar
        def _(act):
            def high(t, m):
                k = 2 * t + m
                act.wait_ge(unit_ready, 3 * t + m + 1)
                if k >= 4:
                    act.wait_ge(gu_done, 4 * (t - 1))
                act.activation(unit_view(wh[:, k % 4, :], t, m), unit_view(wf[:, m, :], t, m), ACT.Copy).then_inc(wh_ready, 1)

            high(0, 0)
            high(0, 1)
            norm_scalar(act, g, n, GU)
            for t in range(NTI):
                if t + 1 < NTI:
                    high(t + 1, 0)
                    high(t + 1, 1)
                for hf in range(NHALF):
                    w = inner(t)
                    act.wait_ge(gu_done, 4 * t + 2 * hf + 1)
                    if 2 * t + hf >= 1:
                        act.wait_ge(h_ready, 2 * t + hf)
                    act.activation(th[0:w, :], ps[0:w, GU[2 * hf], :], ACT.Tanh, scale=0.5).then_inc(th_ready, 1)

        @block.vector
        def _(dve):
            chain = [0]

            def link(ins):
                chain[0] += 1
                ins.then_inc(step, 1)
                dve.wait_ge(step, chain[0])

            def unpack(u):
                t, m = u // 3, u % 3
                dve.wait_ge(q_landed[u % 2], landed(u))
                rows_of = inner(t) if m == 2 else P
                dve.tensor_scalar(unit_view(qn[:, :], t, m), unit_view(qraw[:, u % 2, :], t, m), nib[0:rows_of, 0:1],
                                  15, ALU.logical_shift_right, ALU.bitwise_and).then_inc(q_used, 1)
                dve.wait_ge(q_used, u + 1)
                dve.wait_ge(zs_done, u + 1)
                if m == 2:
                    dst = wd[0:inner(t), t, :]
                else:
                    if t >= 1:
                        dve.wait_ge(wl_ready, 2 * (t - 1) + m + 1)
                    dst = unit_view(wf[:, m, :], t, m)
                link(dve.tensor_tensor(dst, unit_view(qn[:, :], t, m), unit_view(ps[:, Z[u % 2], :], t, m), ALU.subtract))
                dve.tensor_tensor(dst, dst, unit_view(ps[:, SC[u % 2], :], t, m), ALU.mult).then_inc(unit_ready, 1)

            dve.wait_ge(consts, 16)
            unpack(0)
            unpack(1)
            norm_vector(dve, g, n, xn, GU)
            unpack(2)
            for t in range(NTI):
                w = inner(t)
                if t + 1 < NTI:
                    unpack(3 * t + 3)
                    unpack(3 * t + 4)
                for hf in range(NHALF):
                    dve.wait_ge(th_ready, 2 * t + hf + 1)
                    link(dve.scalar_tensor_tensor(sg[0:w, :], th[0:w, :], 1.0, ps[0:w, GU[2 * hf], :], ALU.add, ALU.mult))
                    dve.wait_ge(gu_done, 4 * t + 2 * hf + 2)
                    dve.scalar_tensor_tensor(h[0:w, t, hf * HALF:(hf + 1) * HALF], sg[0:w, :], 0.5, ps[0:w, GU[2 * hf + 1], :],
                                             ALU.mult, ALU.mult).then_inc(h_ready, 1)
                if t + 1 < NTI:
                    unpack(3 * t + 5)

        @block.tensor
        def _(pe):
            def zeros_and_scales(u):
                t, m = u // 3, u % 3
                if u >= 2:
                    pe.wait_ge(unit_ready, u - 1)
                pieces = [(ROW0[m] + c * P, P, COL0[m] + t * P, c * P, inner(t)) for c in range(DC)]
                if m == 2:
                    pieces = [(ROW0[m] + t * P, inner(t), COL0[m], 0, D)]
                for r0, k, c0, at, width in pieces:
                    pe.matmul(ps[0:k, Z[u % 2], at:at + width], onehot[96:128, r0:r0 + k], rows[96:128, c0:c0 + width],
                              start=True, stop=True)
                    last = pe.matmul(ps[0:k, SC[u % 2], at:at + width], onehot[0:96, r0:r0 + k], rows[0:96, c0:c0 + width],
                                     start=True, stop=True)
                last.then_inc(zs_done, 1)

            def products(t, hf, m):
                w, k = inner(t), 2 * t + m
                tok = slice(hf * HALF, (hf + 1) * HALF)
                pe.wait_ge(wl_ready, k + 1)
                if t >= 1:
                    pe.wait_ge(h_ready, 2 * (t - 1) + hf + 1)
                view = lambda buf: buf[:, k % 4, :].rearrange("p (c n) -> p c n", c=DC)
                three_passes(pe, ps[0:w, GU[2 * hf + m], :], lambda c: (view(wh)[:, c, 0:w], view(wl)[:, c, 0:w]),
                             lambda c: (g["xh"][:, c, tok], g["xl"][:, c, tok]), DC).then_inc(gu_done, 1)

            zeros_and_scales(0)
            zeros_and_scales(1)
            norm_tensor(pe, g, n, xn, GU)
            zeros_and_scales(2)
            pe.wait_ge(n["xl_ready"], NT)
            for t in range(NTI):
                for hf in range(NHALF):
                    for m in range(2):
                        if t + 1 < NTI and 2 * hf + m < 3:
                            zeros_and_scales(3 * (t + 1) + 2 * hf + m)
                        products(t, hf, m)


def down(nc, a, g, out):
    ps, x, gate, h, wd = g["ps"], g["x"], g["gate"], g["h"], g["wd"]
    with ExitStack() as ctx:
        def sb(name, shape, dt=F32):
            return ctx.enter_context(nc.sbuf_tensor(name, shape, dt))

        def sem(name):
            return ctx.enter_context(nc.semaphore("e_" + name))

        hh = sb("hh", [P, 2, TOK], F32R)
        hl = sb("hl", [P, 2, TOK], F32R)
        wdh = sb("wdh", [P, 2, D], F32R)
        wdl = sb("wdl", [P, 2, D], F32R)
        res = sb("res", [P, 2, D])
        wh_ready = sem("wh_ready")
        wl_ready = sem("wl_ready")
        hh_ready = sem("hh_ready")
        hl_ready = sem("hl_ready")
        tile_done = sem("tile_done")
        out_done = sem("out_done")
        res_ready = sem("res_ready")
        stored = [sem(f"stored{i}") for i in range(2)]
        block = ctx.enter_context(nc.Block())

        @block.sync
        def _(sp):
            rows = out.rearrange("b s d -> (b s) d")
            for i in range(NT):
                sp.wait_ge(res_ready, i + 1)
                sp.dma_start(rows[i * P:(i + 1) * P, :], res[:, i % 2, :]).then_inc(stored[i % 2], 16)
            sp.wait_ge(stored[0], 16 * (NT // 2))
            sp.wait_ge(stored[1], 16 * (NT // 2))

        @block.scalar
        def _(act):
            for t in range(NTI):
                w = inner(t)
                if t >= 2:
                    act.wait_ge(tile_done, t - 1)
                act.activation(wdh[0:w, t % 2, :], wd[0:w, t, :], ACT.Copy).then_inc(wh_ready, 1)
                act.activation(hh[0:w, t % 2, :], h[0:w, t, :], ACT.Copy).then_inc(hh_ready, 1)

        @block.gpsimd
        def _(pool):
            for t in range(NTI):
                w = inner(t)
                pool.wait_ge(wh_ready, t + 1)
                pool.tensor_tensor(wdl[0:w, t % 2, :], wd[0:w, t, :], wdh[0:w, t % 2, :].bitcast(F32), ALU.subtract)\
                    .then_inc(wl_ready, 1)

        @block.vector
        def _(dve):
            for t in range(NTI):
                w = inner(t)
                dve.wait_ge(hh_ready, t + 1)
                dve.tensor_tensor(hl[0:w, t % 2, :], h[0:w, t, :], hh[0:w, t % 2, :].bitcast(F32), ALU.subtract)\
                   .then_inc(hl_ready, 1)
            for i in range(NT):
                dve.wait_ge(out_done, i + 1)
                if i >= 2:
                    dve.wait_ge(stored[i % 2], 16 * (i // 2))
                dve.scalar_tensor_tensor(res[:, i % 2, :], ps[:, i, :], gate[:, 3:4], x[:, i, :], ALU.mult, ALU.add)\
                   .then_inc(res_ready, 1)

        @block.tensor
        def _(pe):
            for t in range(NTI):
                w = inner(t)
                pe.wait_ge(wl_ready, t + 1)
                pe.wait_ge(hl_ready, t + 1)
                for i in range(NT):
                    tok = slice(i * P, (i + 1) * P)
                    last = three_passes(pe, ps[:, i, :], lambda c: (hh[0:w, t % 2, tok], hl[0:w, t % 2, tok]),
                                        lambda c: (wdh[0:w, t % 2, :], wdl[0:w, t % 2, :]), 1,
                                        first=(t == 0), final=(t == NTI - 1))
                    if t == NTI - 1:
                        last.then_inc(out_done, 1)
                if t < NTI - 1:
                    last.then_inc(tile_done, 1)


def constants():
    f = np.float32
    pos = np.arange(C, dtype=f)
    inv = (f(1.0) / np.power(f(10000.0), np.arange(0, DK, 2, dtype=f) / f(DK))).astype(f)
    ang = inv[:, None] * pos[None, :]
    cos, sin = np.cos(ang).astype(f), np.sin(ang).astype(f)
    rope = np.concatenate([np.concatenate([cos, cos]), np.concatenate([-sin, sin])], axis=1)
    ch = np.arange(P)
    sel = np.zeros((P, 2, 2 * BH), f)
    spread = np.zeros((P, WG, P), f)
    for e in range(2):
        sel[ch, e, e * BH + ch // LHD] = 1
    for w in range(WG):
        spread[w * BH + ch // LHD, w, ch] = 1
    return {
        "ident": np.eye(P, dtype=f),
        "rope": rope,
        "sel": sel.reshape(P, -1),
        "spread": spread.reshape(P, -1),
        "iota": np.arange(NE, dtype=f),
        "nib": (BITS * (ch % PACK)).astype(np.int32)[:, None],
        "gnum": (ch % 32).astype(f)[:, None],
    }


def block_diagonal(w):
    r = np.zeros((P, P), w.dtype)
    for b in range(BT):
        r[b * C:(b + 1) * C, b * C:(b + 1) * C] = w.T
    return r


def kernel(**inputs):
    import numpy as _np
    import concourse.bacc as _bacc
    from concourse import mybir as _mybir
    from concourse.bass_utils import run_bass_kernel_spmd as _run

    i = {k: _np.asarray(v) for k, v in inputs.items()}
    arrays = {
        "x": i["x"], "ctx": i["ctx_4096"], "ctxT": i["ctx_4096"].reshape(TOK, D).T, "mask": i["mask_BxSxS2_ff0"],
        "g_xattn": i["g_xattn"], "g_ffn": i["g_ffn"],
        "W_base": i["L0_ffn_W_base"].T, "b_base": i["L0_ffn_b_base"], "W_router": i["L0_ffn_W_router"].T,
        "lora_A": i["L0_ffn_lora_A"].reshape(NE * RANK, D).T,
        "lora_B": i["L0_ffn_lora_B"].transpose(0, 2, 1).reshape(NE * RANK, D),
    }
    for n in "qkvo":
        arrays["W" + n] = block_diagonal(i["L0_xattn_W" + n])
        arrays["b" + n] = i["L0_xattn_b" + n]
        arrays["w" + n] = i["L1_xattn_w" + n]
    for m in ("gate", "up", "down"):
        for part in ("qweight", "scales", "qzeros", "g_idx"):
            arrays[f"{m}_{part}"] = i[f"L1_ffn_{m}_{part}"]
    arrays.update(constants())

    nc = _bacc.Bacc("TRN2", target_bir_lowering=False, num_devices=1)
    given, aps = {}, {}
    for n, v in arrays.items():
        v = _np.ascontiguousarray(v)
        given[f"in_{n}"] = v
        aps[n] = nc.dram_tensor(f"in_{n}", v.shape, _mybir.dt.from_np(v.dtype), kind="ExternalInput").ap()
    out = nc.dram_tensor("out", (B, C, D), F32, kind="ExternalOutput").ap()
    build_program(nc, aps, out)
    return _run(nc, [given], core_ids=[0]).results[0]["out"]
```

```python
from contextlib import ExitStack

import numpy as np

import concourse.bass as bass
from concourse import mybir

F32 = mybir.dt.float32
F32R = mybir.dt.float32r
I32 = mybir.dt.int32
U32 = mybir.dt.uint32
BF16 = mybir.dt.bfloat16
ALU = mybir.AluOpType
ACT = mybir.ActivationFunctionType
AX = mybir.AxisListType

P = 128
B, C, D = 16, 64, 512
TOK = B * C
NT = TOK // P
BT = P // C
DC = D // P
HALF = 512
NHALF = TOK // HALF
TPH = HALF // P
EPS = 1e-5

LH, LHD, WIN = 8, 8, 16
PAD_L = WIN // 2
TPAD = D + WIN - 1
BH = BT * LH
WG = P // BH
GW = 4

NE, RANK = 8, 16
LORA_SCALE = 32.0 / 16.0

NQ, NKV, DK = 32, 8, 128
GRP = NQ // NKV

INTER, PACK, BITS = 1376, 8, 4
NTI = -(-INTER // P)
GK, GD = D // 128, INTER // 128


MATS = (("gate", D, INTER, GK), ("up", D, INTER, GK), ("down", INTER, D, GD))
ROW0 = (0, D, 2 * D)
COL0 = (0, INTER, 2 * INTER)


def inner(t):
    return min(P, INTER - P * t)


def build_program(nc, a, out):
    with ExitStack() as top:
        def sbuf(ctx, name, shape, dt=F32):
            return ctx.enter_context(nc.sbuf_tensor(name, shape, dt))

        ps = top.enter_context(nc.psum_tensor("ps", [P, 8, 512], F32))
        x = sbuf(top, "x", [P, NT, D])
        ident = sbuf(top, "ident", [P, P])
        gate = sbuf(top, "gate", [P, 4])
        stats = sbuf(top, "stats", [P, NT, 6])
        mv = sbuf(top, "mv", [P, NT, 2])
        veps = sbuf(top, "veps", [P, NT])
        rstd = sbuf(top, "rstd", [P, NT])
        mhalf = sbuf(top, "mhalf", [P, NT])
        g = dict(ps=ps, x=x, ident=ident, gate=gate, stats=stats, mv=mv, veps=veps, rstd=rstd, mhalf=mhalf)
        g["piece_landed"] = [top.enter_context(nc.semaphore(f"piece_landed{i}")) for i in range(2)]
        for name in ("high_ready", "low_ready"):
            g[name] = top.enter_context(nc.semaphore(name))
        g["onehot"] = sbuf(top, "onehot", [P, 2 * D + INTER], BF16)
        g["rows"] = sbuf(top, "rows", [P, 2 * INTER + D], BF16)
        with ExitStack() as first:
            g["stage"] = sbuf(first, "stage", [P, 2, 2 * D])
            windowed_attention(nc, a, g)
            for name in ("xh", "xl", "ch", "cl"):
                g[name] = sbuf(first, name, [P, DC, TOK], F32R)
            for part in ("h", "l"):
                g["wq" + part] = sbuf(first, "wq" + part, [P, DC, GRP * DK], F32R)
                g["wkv" + part] = sbuf(first, "wkv" + part, [P, 2, DC, DK], F32R)
            routed_lora(nc, a, g)
            rotary_attention(nc, a, g)
        with ExitStack() as last:
            for name in ("xh", "xl"):
                g[name] = sbuf(last, name + "4", [P, DC, TOK], F32R)
            g["h"] = sbuf(last, "h", [P, NTI, TOK])
            g["wd"] = sbuf(last, "wd", [P, NTI, D])
            gate_up(nc, a, g)
            down(nc, a, g, out)


KV, Q01, Q23, O01, O23 = range(5)


def stage_view(g, kv, piece):
    buf = g["stage"][:, (5 * kv + piece) % 2, :]
    if piece == KV:
        return buf.rearrange("p (j c n) -> p j c n", j=2, c=DC)
    if piece in (Q01, Q23):
        return buf.rearrange("p (c n) -> p c n", c=DC)
    return buf.rearrange("p (h n) -> p h n", h=2)


def piece_view(g, kv, piece, part):
    if piece == KV:
        return g["wkv" + part][:, :, :, :]
    if piece in (Q01, Q23):
        half = piece - Q01
        return g["wq" + part][:, :, half * 2 * DK:(half + 1) * 2 * DK]
    half = piece - O01
    return g["wo" + part][:, kv % 2, 2 * half:2 * half + 2, :]


def load_piece(sp, a, g, kv, piece):
    n = 5 * kv + piece
    if n >= 2:
        sp.wait_ge(g["low_ready"], n - 1)
    dst = stage_view(g, kv, piece)
    landed = g["piece_landed"][n % 2]
    if piece == KV:
        for j, w in enumerate(("wk", "wv")):
            sp.dma_start(dst[:, j, :, :], a[w].rearrange("(c p) n -> p c n", p=P)[:, :, kv * DK:(kv + 1) * DK])\
              .then_inc(landed, 16)
    elif piece in (Q01, Q23):
        w = 2 * DK
        at = (2 * kv + piece - Q01) * w
        sp.dma_start(dst, a["wq"].rearrange("(c p) n -> p c n", p=P)[:, :, at:at + w]).then_inc(landed, 16)
    else:
        w = 2 * DK
        at = (2 * kv + piece - O01) * w
        sp.dma_start(dst, a["wo"][at:at + w, :].rearrange("(h p) n -> p h n", p=P)).then_inc(landed, 16)


def landed_count(n):
    return 16 * sum(2 if k % 5 == KV else 1 for k in range(n % 2, n + 1, 2))


def high_piece(act, g, kv, piece):
    n = 5 * kv + piece
    act.wait_ge(g["piece_landed"][n % 2], landed_count(n))
    act.activation(piece_view(g, kv, piece, "h"), stage_view(g, kv, piece), ACT.Copy).then_inc(g["high_ready"], 1)


def low_piece(pool, g, kv, piece):
    n = 5 * kv + piece
    pool.wait_ge(g["high_ready"], n + 1)
    pool.tensor_tensor(piece_view(g, kv, piece, "l"), stage_view(g, kv, piece),
                       piece_view(g, kv, piece, "h").bitcast(F32), ALU.subtract).then_inc(g["low_ready"], 1)


def windowed_attention(nc, a, g):
    ps, x, ident, gate = g["ps"], g["x"], g["ident"], g["gate"]
    stats, mv, veps, rstd, mhalf = g["stats"], g["mv"], g["veps"], g["rstd"], g["mhalf"]
    with ExitStack() as ctx:
        def sb(name, shape, dt=F32):
            return ctx.enter_context(nc.sbuf_tensor(name, shape, dt))

        def sem(name):
            return ctx.enter_context(nc.semaphore(name))

        ctxt = sb("ctxt", [P, NT, D])
        w4 = sb("w4", [P, 4, P])
        bias = sb("bias", [P, 4])
        gbo = sb("gbo", [P, 1])
        graw = sb("graw", [P, 4])
        sel = sb("sel", [P, 2, 32])
        spread_f = sb("spread_f", [P, WG, P])
        spread = sb("spread", [P, WG, P], F32R)
        xn = sb("xn", [P, 2, D])
        q = sb("q", [P, 2, D])
        kpad = sb("kpad", [P, 2, TPAD])
        vpad = sb("vpad", [P, 3, TPAD])
        prod = sb("prod", [P, WIN, D])
        sc = sb("sc", [P, 2, D])
        mx = sb("mx", [P, D // P, BH])
        att = sb("att", [P, D // P, WIN, BH])
        sm = sb("sm", [P, D // P, BH])
        rs = sb("rs", [P, D // P, BH])
        ath = sb("ath", [P, 2, D], F32R)
        atl = sb("atl", [P, 2, D], F32R)
        r = sb("r", [P, WIN, D])
        r2 = sb("r2", [P, WIN // 2, D])
        o = sb("o", [P, D])

        x_landed = [sem(f"x_landed{i}") for i in range(NT)]
        ctx_landed = [sem(f"ctx_landed{i}") for i in range(NT)]
        const_landed = sem("const_landed")
        half_set = sem("half_set")
        pad_zeroed = sem("pad_zeroed")
        gate_ready = sem("gate_ready")
        spread_ready = sem("spread_ready")
        dve_step = sem("dve_step")
        var_ready = sem("var_ready")
        rstd_ready = sem("rstd_ready")
        xn_ready = sem("xn_ready")
        qkv_done = sem("qkv_done")
        qkv_ready = sem("qkv_ready")
        prod_ready = sem("prod_ready")
        last_prod_ready = sem("last_prod_ready")
        prod_used = sem("prod_used")
        sc_ready = sem("sc_ready")
        fwd_done = sem("fwd_done")
        shifted = sem("shifted")
        exp_ready = sem("exp_ready")
        att_ready = sem("att_ready")
        back_done = sem("back_done")
        ath_ready = sem("ath_ready")
        atl_ready = sem("atl_ready")
        spread_done = sem("spread_done")
        r_ready = sem("r_ready")
        rsum_ready = sem("rsum_ready")
        out_done = sem("out_done")
        o_ready = sem("o_ready")
        x_ready = sem("x_ready")
        st = stat_sems(sem)

        S = [ps[:, 0, :], ps[:, 1, :]]
        T2 = ps[:, 2:4, :]
        T_time = T2.rearrange("p a (b g m) -> p (a b) g m", b=2, g=2)
        T_win = T2.rearrange("p a (b w h) -> p (a b) w h", b=2, w=WIN)
        RING = [ps[:, 4, :], ps[:, 5, :], ps[:, 6, :]]
        M = ps[:, 7, :]

        NCONST = 14
        ORDER = [w + d for w in range(0, WIN // 2, 2) for d in (0, 1, WIN // 2, WIN // 2 + 1)]
        RINGS = 2 + WIN

        PARTS = WIN // GW

        def products(eng, i, part):
            w0 = GW * part
            k0 = kpad[:, i % 2, w0:w0 + D]
            windows = bass.AP(k0.tensor, k0.offset, [list(k0.ap[0]), [1, GW], [1, D]])
            qb = q[:, i % 2, :].unsqueeze(1).broadcast_to([P, GW, D])
            return eng.tensor_tensor(prod[:, w0:w0 + GW, :], qb, windows, ALU.mult)

        block = ctx.enter_context(nc.Block())

        @block.sync
        def _(sp):
            xr = a["x"].rearrange("b s d -> (b s) d")
            cr = a["ctx"].rearrange("b s d -> (b s) d")
            sp.dma_start(x[:, 0, :], xr[0:P, :]).then_inc(x_landed[0], 16)
            sp.dma_start(ctxt[:, 0, :], cr[0:P, :]).then_inc(ctx_landed[0], 16)
            for j, w in enumerate(("Wq", "Wk", "Wv", "Wo")):
                sp.dma_start(w4[:, j, :], a[w]).then_inc(const_landed, 16)
            for j, w in enumerate(("bq", "bk", "bv", "bo")):
                for b in range(BT):
                    sp.dma_start(bias[b * C:(b + 1) * C, j:j + 1], a[w].rearrange("(c o) -> c o", o=1))\
                      .then_inc(const_landed, 16)
            sp.dma_start(sel[:, :, :], a["sel"].rearrange("p (a b) -> p a b", a=2)).then_inc(const_landed, 16)
            sp.dma_start(ident[:, :], a["ident"]).then_inc(const_landed, 16)
            for i in range(1, NT):
                sp.dma_start(x[:, i, :], xr[i * P:(i + 1) * P, :]).then_inc(x_landed[i], 16)
                sp.dma_start(ctxt[:, i, :], cr[i * P:(i + 1) * P, :]).then_inc(ctx_landed[i], 16)
            load_piece(sp, a, g, 0, KV)
            load_piece(sp, a, g, 0, Q01)

        @block.gpsimd
        def _(pool):
            pool.memset(kpad[:, :, :], 0.0).then_inc(pad_zeroed, 1)
            pool.memset(vpad[:, :, :], 0.0).then_inc(pad_zeroed, 1)
            pool.memset(mhalf[:, :], -0.5).then_inc(half_set, 1)
            pool.wait_ge(half_set, 1)
            pool.wait_ge(var_ready, 1)
            pool.tensor_tensor(rstd[:, 0:1], veps[:, 0:1], mhalf[:, 0:1], ALU.pow).then_inc(rstd_ready, 1)
            pool.wait_ge(var_ready, 2)
            pool.tensor_tensor(rstd[:, 1:NT], veps[:, 1:NT], mhalf[:, 1:NT], ALU.pow).then_inc(rstd_ready, 1)
            for s in range(NT + 1):
                if s < NT:
                    pool.wait_ge(qkv_ready, 3 * s + 2)
                    if s >= 1:
                        pool.wait_ge(prod_used, 4 * s)
                    products(pool, s, PARTS - 1).then_inc(last_prod_ready, 1)
                if s >= 1:
                    i = s - 1
                    for w in range(0, WIN // 2, 2):
                        pool.wait_ge(r_ready, WIN * i + 2 * w + 4)
                        if i >= 1 and w == 0:
                            pool.wait_ge(out_done, i)
                        pool.tensor_tensor(r2[:, w:w + 2, :], r[:, w:w + 2, :], r[:, WIN // 2 + w:WIN // 2 + w + 2, :],
                                           ALU.add).then_inc(rsum_ready, 1)
            row_scales(pool, g, st)

        @block.scalar
        def _(act):
            act.dma_start(spread_f[:, :, :], a["spread"].rearrange("p (w c) -> p w c", w=WG)).then_inc(const_landed, 16)
            act.dma_start(graw[:, 0:2], a["g_xattn"].partition_broadcast(P)).then_inc(const_landed, 16)
            act.dma_start(graw[:, 2:4], a["g_ffn"].partition_broadcast(P)).then_inc(const_landed, 16)
            act.wait_ge(const_landed, 16 * (NCONST + 3))
            act.activation(gate[:, :], graw[:, :], ACT.Tanh).then_inc(gate_ready, 1)
            act.wait_ge(gate_ready, 1)
            act.activation(gbo[:, :], bias[:, 3:4], ACT.Copy, scale=gate[:, 0:1]).then_inc(gate_ready, 1)
            act.activation(spread[:, :, :], spread_f[:, :, :], ACT.Copy).then_inc(spread_ready, 1)
            act.wait_ge(pad_zeroed, 2)

            def project(i):
                act.wait_ge(qkv_done, 3 * i + 1)
                if i >= 2:
                    act.wait_ge(prod_ready, (PARTS - 1) * (i - 1))
                    act.wait_ge(last_prod_ready, i - 1)
                act.activation(q[:, i % 2, :], M, ACT.Identity, bias=bias[:, 0:1]).then_inc(qkv_ready, 1)
                act.wait_ge(qkv_done, 3 * i + 2)
                act.activation(kpad[:, i % 2, PAD_L:PAD_L + D], RING[0], ACT.Identity, bias=bias[:, 1:2])\
                   .then_inc(qkv_ready, 1)
                act.wait_ge(qkv_done, 3 * i + 3)
                if i >= 3:
                    act.wait_ge(r_ready, WIN * (i - 2))
                act.activation(vpad[:, i % 3, PAD_L:PAD_L + D], RING[1], ACT.Identity, bias=bias[:, 2:3])\
                   .then_inc(qkv_ready, 1)

            def output(i):
                act.wait_ge(out_done, i + 1)
                if i >= 1:
                    act.wait_ge(x_ready, i)
                act.activation(o[:, :], M, ACT.Identity, bias=gbo[:, 0:1], scale=gate[:, 0:1]).then_inc(o_ready, 1)

            project(0)
            for s in range(NT + 2):
                if 1 <= s <= NT:
                    act.wait_ge(shifted, s)
                    act.activation(att[:, :, :, :], att[:, :, :, :], ACT.Exp, scale=float(LHD) ** -0.5)\
                       .then_inc(exp_ready, 1)
                if s >= 2:
                    output(s - 2)
                if 1 <= s <= NT:
                    act.wait_ge(back_done, s)
                    if s >= 2:
                        act.wait_ge(spread_done, WIN * (s - 1))
                    act.activation(ath[:, :, :], T2, ACT.Copy).then_inc(ath_ready, 1)
                if s + 1 < NT:
                    project(s + 1)
                if s < NT:
                    act.wait_ge(prod_used, 4 * (s + 1))
                    if s >= 1:
                        act.wait_ge(fwd_done, s)
                    act.activation(sc[:, :, :], ps[:, 0:2, :], ACT.Copy).then_inc(sc_ready, 1)

        @block.vector
        def _(dve):
            chain = [0]

            def link(ins):
                chain[0] += 1
                ins.then_inc(dve_step, 1)
                dve.wait_ge(dve_step, chain[0])

            def statistics(i):
                dve.wait_ge(x_landed[i], 16)
                link(dve.bn_stats(stats[:, i, :], x[:, i, :]))
                link(dve.bn_aggr(mv[:, i, :], stats[:, i, :]))

            def normalise(i):
                dve.wait_ge(rstd_ready, 1 if i == 0 else 2)
                if i >= 2:
                    dve.wait_ge(qkv_done, 3 * (i - 2) + 1)
                dve.tensor_scalar(xn[:, i % 2, :], x[:, i, :], mv[:, i, 0:1], rstd[:, i:i + 1],
                                  ALU.subtract, ALU.mult).then_inc(xn_ready, 1)

            def part_of_products(i, part):
                if i >= 1:
                    dve.wait_ge(prod_used, 4 * (i - 1) + part + 1)
                products(dve, i, part).then_inc(prod_ready, 1)

            statistics(0)
            dve.tensor_scalar(veps[:, 0:1], mv[:, 0, 1:2], EPS, None, ALU.add).then_inc(var_ready, 1)
            normalise(0)
            for i in range(1, NT):
                statistics(i)
            dve.tensor_scalar(veps[:, 1:NT], mv[:, 1:NT, 1], EPS, None, ALU.add).then_inc(var_ready, 1)
            normalise(1)
            for s in range(NT + 2):
                if 1 <= s <= NT:
                    dve.wait_ge(fwd_done, s)
                    link(dve.tensor_reduce(mx[:, :, :], T_win.rearrange("p b w h -> p b h w"), AX.X, ALU.max))
                    if s >= 2:
                        dve.wait_ge(back_done, s - 1)
                    dve.tensor_tensor(att[:, :, :, :], T_win, mx[:, :, :].unsqueeze(2).broadcast_to([P, D // P, WIN, BH]),
                                      ALU.subtract).then_inc(shifted, 1)
                if s < NT:
                    dve.wait_ge(qkv_ready, 3 * (s + 1))
                    part_of_products(s, 0)
                    part_of_products(s, 1)
                if 1 <= s <= NT:
                    dve.wait_ge(exp_ready, s)
                    link(dve.tensor_reduce(sm[:, :, :], att[:, :, :, :].rearrange("p b w h -> p b h w"), AX.X, ALU.add))
                    link(dve.reciprocal(rs[:, :, :], sm[:, :, :]))
                    dve.tensor_tensor(att[:, :, :, :], att[:, :, :, :],
                                      rs[:, :, :].unsqueeze(2).broadcast_to([P, D // P, WIN, BH]), ALU.mult)\
                       .then_inc(att_ready, 1)
                if s < NT:
                    part_of_products(s, 2)
                if 1 <= s <= NT:
                    dve.wait_ge(ath_ready, s)
                    dve.tensor_tensor(atl[:, :, :], T2, ath[:, :, :].bitcast(F32), ALU.subtract).then_inc(atl_ready, 1)
                if s >= 2:
                    i = s - 2
                    dve.wait_ge(o_ready, i + 1)
                    dve.tensor_tensor(x[:, i, :], x[:, i, :], o[:, :], ALU.add).then_inc(x_ready, 1)
                    dve.wait_ge(x_ready, i + 1)
                    row_sums(dve, g, st, i)
                if 1 <= s <= NT:
                    i = s - 1
                    for n, w in enumerate(ORDER):
                        if i >= 1 and n % 4 == 0:
                            dve.wait_ge(rsum_ready, 4 * (i - 1) + n // 4 + 1)
                        dve.wait_ge(spread_done, WIN * i + n + 1)
                        dve.tensor_tensor(r[:, w, :], RING[(2 + n) % 3], vpad[:, i % 3, w:w + D], ALU.mult)\
                           .then_inc(r_ready, 1)
                if s + 2 < NT:
                    normalise(s + 2)

            row_variances(dve, g, st)

        @block.tensor
        def _(pe):
            pe.wait_ge(const_landed, 16 * (NCONST + 3))

            def project(i):
                pe.wait_ge(xn_ready, i + 1)
                if i >= 3:
                    pe.wait_ge(o_ready, i - 2)
                pe.matmul(M, w4[:, 0, :], xn[:, i % 2, :], start=True, stop=True).then_inc(qkv_done, 1)
                pe.wait_ge(ctx_landed[i], 16)
                if i >= 3:
                    pe.wait_ge(r_ready, WIN * (i - 2))
                for j in (1, 2):
                    pe.matmul(RING[j - 1], w4[:, j, :], ctxt[:, i, :], start=True, stop=True).then_inc(qkv_done, 1)

            def reduce_heads(i, part):
                if part < PARTS - 1:
                    pe.wait_ge(prod_ready, (PARTS - 1) * i + part + 1)
                else:
                    pe.wait_ge(last_prod_ready, i + 1)
                if i >= 1 and part == 0:
                    pe.wait_ge(sc_ready, i)
                for u in (2 * part, 2 * part + 1):
                    dst = S[u // 4][32 * (u % 4):32 * (u % 4) + 32, :]
                    pe.matmul(dst, sel[:, 0, :], prod[:, 2 * u, :], start=True, stop=False)
                    last = pe.matmul(dst, sel[:, 1, :], prod[:, 2 * u + 1, :], start=False, stop=True)
                last.then_inc(prod_used, 1)

            def output(i):
                if i + 2 < NT:
                    pe.wait_ge(qkv_ready, 3 * (i + 2) + 1)
                for w in range(WIN // 2):
                    pe.wait_ge(rsum_ready, 4 * i + w // 2 + 1)
                    last = pe.matmul(M, w4[:, 3, :], r2[:, w, :], start=(w == 0), stop=(w == WIN // 2 - 1))
                last.then_inc(out_done, 1)

            def scores_turned(i):
                pe.wait_ge(sc_ready, i + 1)
                for b in range(D // P):
                    for grp in range(2):
                        last = pe.transpose(T_time[:, b, grp, :], sc[:, grp, b * P:(b + 1) * P], ident[:, :])
                last.then_inc(fwd_done, 1)

            project(0)
            for s in range(NT + 2):
                if s >= 2:
                    output(s - 2)
                if s > NT:
                    continue
                if s < NT:
                    reduce_heads(s, 0)
                    reduce_heads(s, 1)
                if s >= 1:
                    pe.wait_ge(att_ready, s)
                    for grp in range(2):
                        for b in range(D // P):
                            last = pe.transpose(T2[:, grp, b * P:(b + 1) * P],
                                                att[:, b, grp * WG:(grp + 1) * WG, :].rearrange("p w h -> p (w h)"), ident[:, :])
                    last.then_inc(back_done, 1)
                if s + 1 < NT:
                    project(s + 1)
                if s < NT:
                    reduce_heads(s, 2)
                    reduce_heads(s, 3)
                if s >= 1:
                    i = s - 1
                    if i == 0:
                        pe.wait_ge(spread_ready, 1)
                    pe.wait_ge(atl_ready, s)
                    for n, w in enumerate(ORDER):
                        if n < 3:
                            pe.wait_ge(qkv_ready, 3 * min(s + 2, NT))
                        if n >= 3:
                            pe.wait_ge(r_ready, WIN * i + n - 2)
                        elif i >= 1:
                            pe.wait_ge(r_ready, WIN * i)
                        pe.matmul(RING[(2 + n) % 3], spread[:, w % WG, :], ath[:, w // WG, :], start=True, stop=False)
                        pe.matmul(RING[(2 + n) % 3], spread[:, w % WG, :], atl[:, w // WG, :], start=False, stop=True)\
                          .then_inc(spread_done, 1)
                        if n == WIN // 2 and s < NT:
                            scores_turned(s)
                else:
                    scores_turned(s)


def norm_sems(sem, tag):
    names = ("xn_ready", "xt_done", "xh_ready", "xl_ready")
    return {n: sem(f"{tag}_{n}") for n in names}


def stat_sems(sem):
    return {n: sem(f"next_{n}") for n in ("sums_done", "aggr_done", "var_ready", "rstd_ready")}


def row_sums(dve, g, st, i):
    dve.bn_stats(g["stats"][:, i, :], g["x"][:, i, :]).then_inc(st["sums_done"], 1)


def row_variances(dve, g, st):
    dve.wait_ge(st["sums_done"], NT)
    for i in range(NT):
        last = dve.bn_aggr(g["mv"][:, i, :], g["stats"][:, i, :])
    last.then_inc(st["aggr_done"], 1)
    dve.wait_ge(st["aggr_done"], 1)
    dve.tensor_scalar(g["veps"][:, :], g["mv"][:, :, 1], EPS, None, ALU.add).then_inc(st["var_ready"], 1)


def row_scales(pool, g, st):
    pool.wait_ge(st["var_ready"], 1)
    pool.tensor_tensor(g["rstd"][:, :], g["veps"][:, :], g["mhalf"][:, :], ALU.pow).then_inc(st["rstd_ready"], 1)


def norm_rows(dve, g, n, xn, i):
    if i >= 2:
        dve.wait_ge(n["xt_done"], i - 1)
    dve.tensor_scalar(xn[:, i % 2, :], g["x"][:, i, :], g["mv"][:, i, 0:1], g["rstd"][:, i:i + 1],
                      ALU.subtract, ALU.mult).then_inc(n["xn_ready"], 1)


def norm_turn(pe, g, n, xn, banks, i):
    pe.wait_ge(n["xn_ready"], i + 1)
    if i >= 2:
        pe.wait_ge(n["xl_ready"], i - 1)
    for c in range(DC):
        last = pe.transpose(g["ps"][:, banks[i % 2], c * P:(c + 1) * P], xn[:, i % 2, c * P:(c + 1) * P], g["ident"][:, :])
    last.then_inc(n["xt_done"], 1)


def norm_high(act, g, n, banks, i):
    act.wait_ge(n["xt_done"], i + 1)
    act.activation(g["xh"][:, :, i * P:(i + 1) * P], g["ps"][:, banks[i % 2], :].rearrange("p (c t) -> p c t", c=DC),
                   ACT.Copy).then_inc(n["xh_ready"], 1)


def norm_low(dve, g, n, banks, i):
    dve.wait_ge(n["xh_ready"], i + 1)
    t = slice(i * P, (i + 1) * P)
    dve.tensor_tensor(g["xl"][:, :, t], g["ps"][:, banks[i % 2], :].rearrange("p (c t) -> p c t", c=DC),
                      g["xh"][:, :, t].bitcast(F32), ALU.subtract).then_inc(n["xl_ready"], 1)


def norm_vector(dve, g, n, xn, banks):
    norm_rows(dve, g, n, xn, 0)
    for i in range(1, NT):
        norm_rows(dve, g, n, xn, i)
        norm_low(dve, g, n, banks, i - 1)
    norm_low(dve, g, n, banks, NT - 1)


def norm_scalar(act, g, n, banks):
    for i in range(NT):
        norm_high(act, g, n, banks, i)


def norm_tensor(pe, g, n, xn, banks):
    for i in range(NT):
        norm_turn(pe, g, n, xn, banks, i)


def three_passes(pe, dst, lhs, rhs, chunks, first=True, final=True):
    for c in range(chunks):
        (lh, ll), (rh, rl) = lhs(c), rhs(c)
        pe.matmul(dst, lh, rh, start=(first and c == 0), stop=False)
        pe.matmul(dst, lh, rl, start=False, stop=False)
        last = pe.matmul(dst, ll, rh, start=False, stop=(final and c == chunks - 1))
    return last


def routed_lora(nc, a, g):
    ps, x, ident, gate = g["ps"], g["x"], g["ident"], g["gate"]
    ER = NE * RANK
    with ExitStack() as ctx:
        def sb(name, shape, dt=F32):
            return ctx.enter_context(nc.sbuf_tensor(name, shape, dt))

        def sem(name):
            return ctx.enter_context(nc.semaphore("b_" + name))

        xn = sb("b_xn", [P, 2, D])
        wb_raw = sb("wb_raw", [P, DC, D])
        wbh = sb("wbh", [P, DC, D], F32R)
        wbl = sb("wbl", [P, DC, D], F32R)
        la_raw = sb("la_raw", [P, DC, ER + NE])
        lah = sb("lah", [P, DC, ER + NE], F32R)
        lal = sb("lal", [P, DC, ER + NE], F32R)
        lb = sb("lb", [P, D])
        bb = sb("bb", [P, D])
        gb = sb("gb", [P, D])
        iota = sb("iota", [P, NE])
        lgT = sb("lgT", [NE, TOK])
        hT = sb("hT", [P, TOK])
        lg = sb("lg", [P, NT, NE])
        top8 = sb("top8", [P, NT, 8])
        idx = sb("idx", [P, NT, 8], U32)
        idxf = sb("idxf", [P, NT, 8])
        dl = sb("dl", [P, NT])
        e2 = sb("e2", [P, NT])
        den = sb("den", [P, NT])
        w1 = sb("w1", [P, NT])
        w2 = sb("w2", [P, NT])
        wa = sb("wa", [P, NT, NE])
        wc = sb("wc", [P, NT, NE])
        wx = sb("wx", [P, 2, ER])
        hwT = sb("hwT", [P, 2, P])
        c_raw = sb("c_raw", [P, 2, HALF])
        ch, cl = g["ch"], g["cl"]
        gnum = sb("gnum", [P, 1])
        gi = sb("gi", [P, INTER], I32)
        gf = sb("gf", [P, INTER])
        srow = sb("srow", [P, INTER])
        rest = sb("rest", [P, INTER])
        zq = sb("zq", [P, INTER // PACK], I32)

        loaded = sem("loaded")
        wh_ready = sem("wh_ready")
        wl_ready = sem("wl_ready")
        gb_ready = sem("gb_ready")
        xb_ready = sem("xb_ready")
        step = sem("step")
        n = norm_sems(sem, "n")
        st = stat_sems(sem)
        c_landed = [sem(f"c_landed{i}") for i in range(2)]
        ch_ready = sem("ch_ready")
        cl_ready = sem("cl_ready")
        gnum_landed = sem("gnum_landed")
        cleared = sem("cleared")
        idx_landed = sem("idx_landed")
        rows_ready = sem("rows_ready")
        small_done = sem("small_done")
        small_ready = sem("small_ready")
        lg_done = sem("lg_done")
        lg_ready = sem("lg_ready")
        diff_ready = sem("diff_ready")
        e2_ready = sem("e2_ready")
        wx_ready = sem("wx_ready")
        wxT_done = sem("wxT_done")
        hw_ready = sem("hw_ready")
        out_done = sem("out_done")
        x_ready = sem("x_ready")

        XT = (0, 1)
        SMALL = (2, 3)
        LG, WX, OUT = 4, 5, (6, 7, 0, 1)

        block = ctx.enter_context(nc.Block())

        def load_groups(sp, m):
            name, k, ncols, groups = MATS[m]
            if m == 0:
                sp.wait_ge(cleared, 2)
            else:
                sp.wait_ge(rows_ready, m)
            sp.dma_start(gi[:, 0:k], a[name + "_g_idx"].partition_broadcast(P)).then_inc(idx_landed, 16)
            for b in range(3):
                sp.dma_start(srow[32 * b:32 * b + groups, 0:ncols], a[name + "_scales"]).then_inc(idx_landed, 16)
            sp.dma_start(zq[96:96 + groups, 0:ncols // PACK], a[name + "_qzeros"]).then_inc(idx_landed, 16)

        @block.sync
        def _(sp):
            sp.dma_start(wb_raw[:, :, :], a["W_base"].rearrange("(c p) n -> p c n", p=P)).then_inc(loaded, 16)
            sp.dma_start(la_raw[:, :, 0:ER], a["lora_A"].rearrange("(c p) n -> p c n", p=P)).then_inc(loaded, 16)
            sp.dma_start(la_raw[:, :, ER:], a["W_router"].rearrange("(c p) n -> p c n", p=P)).then_inc(loaded, 16)
            sp.dma_start(lb[:, :], a["lora_B"]).then_inc(loaded, 16)
            sp.dma_start(bb[:, :], a["b_base"].partition_broadcast(P)).then_inc(loaded, 16)
            sp.dma_start(iota[:, :], a["iota"].partition_broadcast(P)).then_inc(loaded, 16)
            sp.dma_start(gnum[:, :], a["gnum"]).then_inc(gnum_landed, 16)
            load_groups(sp, 0)
            cT = a["ctxT"].rearrange("(c p) t -> p c t", p=P)
            for u in range(DC * NHALF):
                c, h = u % DC, u // DC
                if u >= 2:
                    sp.wait_ge(cl_ready, u - 1)
                sp.dma_start(c_raw[:, u % 2, :], cT[:, c, h * HALF:(h + 1) * HALF]).then_inc(c_landed[u % 2], 16)
            load_groups(sp, 1)
            load_groups(sp, 2)
            load_piece(sp, a, g, 0, Q23)
            load_piece(sp, a, g, 0, O01)

        @block.gpsimd
        def _(pool):
            pool.memset(srow[:, :], 0.0).then_inc(cleared, 1)
            pool.memset(zq[:, :], 0).then_inc(cleared, 1)
            pool.wait_ge(wh_ready, 2)
            pool.tensor_tensor(lal[:, :, :], la_raw[:, :, :], lah[:, :, :].bitcast(F32), ALU.subtract).then_inc(wl_ready, 1)
            pool.tensor_tensor(wbl[:, :, :], wb_raw[:, :, :], wbh[:, :, :].bitcast(F32), ALU.subtract).then_inc(wl_ready, 1)
            pool.wait_ge(gb_ready, 1)
            for i in range(NT):
                pool.wait_ge(n["xn_ready"], i + 1)
                pool.tensor_tensor(x[:, i, :], x[:, i, :], gb[:, :], ALU.add).then_inc(xb_ready, 1)
            for u in range(DC * NHALF):
                c, h = u % DC, u // DC
                t = slice(h * HALF, (h + 1) * HALF)
                pool.wait_ge(ch_ready, u + 1)
                pool.tensor_tensor(cl[:, c, t], c_raw[:, u % 2, :], ch[:, c, t].bitcast(F32), ALU.subtract).then_inc(cl_ready, 1)
            for piece in (KV, Q01, Q23):
                low_piece(pool, g, 0, piece)
            row_scales(pool, g, st)

        @block.scalar
        def _(act):
            act.wait_ge(loaded, 16 * 6)
            act.activation(lah[:, :, :], la_raw[:, :, :], ACT.Copy).then_inc(wh_ready, 1)
            act.activation(wbh[:, :, :], wb_raw[:, :, :], ACT.Copy).then_inc(wh_ready, 1)
            act.activation(gb[:, :], bb[:, :], ACT.Copy, scale=gate[:, 2:3]).then_inc(gb_ready, 1)
            norm_scalar(act, g, n, XT)
            for h in range(NHALF):
                t = slice(h * HALF, (h + 1) * HALF)
                act.wait_ge(small_done, 2 * h + 1)
                act.activation(lgT[:, t], ps[0:NE, SMALL[0], :], ACT.Copy).then_inc(small_ready, 1)
                act.wait_ge(small_done, 2 * h + 2)
                act.activation(hT[:, t], ps[:, SMALL[1], :], ACT.Copy).then_inc(small_ready, 1)
            act.wait_ge(diff_ready, 1)
            act.activation(e2[:, :], dl[:, :], ACT.Exp).then_inc(e2_ready, 1)
            for u in range(DC * NHALF):
                c, h = u % DC, u // DC
                act.wait_ge(c_landed[u % 2], 16 * (u // 2 + 1))
                act.activation(ch[:, c, h * HALF:(h + 1) * HALF], c_raw[:, u % 2, :], ACT.Copy).then_inc(ch_ready, 1)
            for piece in (KV, Q01, Q23):
                high_piece(act, g, 0, piece)

        @block.vector
        def _(dve):
            norm_vector(dve, g, n, xn, XT)
            chain = [0]

            def link(ins):
                chain[0] += 1
                ins.then_inc(step, 1)
                dve.wait_ge(step, chain[0])

            def groups_of(m):
                name, k, ncols, groups = MATS[m]
                rows = g["rows"]
                dve.wait_ge(idx_landed, 80 * (m + 1))
                link(dve.tensor_copy(gf[:, 0:k], gi[:, 0:k]))
                link(dve.tensor_scalar(rest[:, 0:k], gf[:, 0:k], 0.0, float(groups), ALU.is_lt, ALU.mult))
                link(dve.tensor_tensor(gf[:, 0:k], gf[:, 0:k], rest[:, 0:k], ALU.add))
                link(dve.tensor_scalar(gf[:, 0:k], gf[:, 0:k], float(groups - 1), 0.0, ALU.min, ALU.max))
                dve.tensor_scalar(g["onehot"][:, ROW0[m]:ROW0[m] + k], gf[:, 0:k], gnum[:, 0:1], None, ALU.is_equal)
                cols = slice(COL0[m], COL0[m] + ncols)
                link(dve.tensor_copy(rows[0:96, cols], srow[0:96, 0:ncols]))
                link(dve.tensor_tensor(rest[0:96, 0:ncols], srow[0:96, 0:ncols], rows[0:96, cols], ALU.subtract))
                link(dve.tensor_copy(rows[32:64, cols], rest[32:64, 0:ncols]))
                link(dve.tensor_copy(rows[64:96, cols], rest[64:96, 0:ncols]))
                link(dve.tensor_tensor(rest[64:96, 0:ncols], rest[64:96, 0:ncols], rows[64:96, cols], ALU.subtract))
                link(dve.tensor_copy(rows[64:96, cols], rest[64:96, 0:ncols]))
                for j in range(PACK):
                    last = dve.tensor_scalar(gi[96:128, j:ncols:PACK], zq[96:128, 0:ncols // PACK], BITS * j, 15,
                                             ALU.logical_shift_right, ALU.bitwise_and)
                link(last)
                dve.tensor_scalar(rows[96:128, cols], gi[96:128, 0:ncols], 1.0, None, ALU.add).then_inc(rows_ready, 1)

            dve.wait_ge(gnum_landed, 16)
            groups_of(0)
            dve.wait_ge(lg_done, 1)
            link(dve.tensor_copy(lg[:, :, :], ps[:, LG, 0:NT * NE].rearrange("p (i e) -> p i e", e=NE)))
            for i in range(NT):
                last = dve.max(top8[:, i, :], lg[:, i, :])
            link(last)
            for i in range(NT):
                last = dve.max_index(idx[:, i, :], top8[:, i, :], lg[:, i, :])
            link(last)
            dve.tensor_tensor(dl[:, :], top8[:, :, 1], top8[:, :, 0], ALU.subtract).then_inc(diff_ready, 1)
            link(dve.tensor_copy(idxf[:, :, :], idx[:, :, :]))
            dve.wait_ge(e2_ready, 1)
            link(dve.tensor_scalar(den[:, :], e2[:, :], 1.0, None, ALU.add))
            link(dve.reciprocal(w1[:, :], den[:, :]))
            link(dve.tensor_tensor(w2[:, :], w1[:, :], e2[:, :], ALU.mult))
            for i in range(NT):
                dve.tensor_scalar(wa[:, i, :], iota[:, :], idxf[:, i, 0:1], w1[:, i:i + 1], ALU.is_equal, ALU.mult)
                last = dve.tensor_scalar(wc[:, i, :], iota[:, :], idxf[:, i, 1:2], w2[:, i:i + 1], ALU.is_equal, ALU.mult)
            link(last)
            link(dve.tensor_tensor(wa[:, :, :], wa[:, :, :], wc[:, :, :], ALU.add))

            def widen(i):
                if i >= 2:
                    dve.wait_ge(wxT_done, i - 1)
                dve.tensor_scalar(wx[:, i % 2, :].rearrange("p (e r) -> p e r", e=NE),
                                  wa[:, i, :].unsqueeze(2).broadcast_to([P, NE, RANK]), LORA_SCALE, None, ALU.mult)\
                   .then_inc(wx_ready, 1)

            widen(0)
            dve.wait_ge(small_ready, 2 * NHALF)
            for i in range(NT + 1):
                if i + 1 < NT:
                    widen(i + 1)
                if i < NT:
                    dve.wait_ge(wxT_done, i + 1)
                    if i >= 2:
                        dve.wait_ge(out_done, i - 1)
                    dve.tensor_tensor(hwT[:, i % 2, :], ps[:, WX, 0:P], hT[:, i * P:(i + 1) * P], ALU.mult)\
                       .then_inc(hw_ready, 1)
                if i >= 1:
                    j = i - 1
                    dve.wait_ge(out_done, i)
                    dve.wait_ge(xb_ready, i)
                    dve.scalar_tensor_tensor(x[:, j, :], ps[:, OUT[j % 4], :], gate[:, 2:3], x[:, j, :], ALU.mult, ALU.add)\
                       .then_inc(x_ready, 1)
                    dve.wait_ge(x_ready, i)
                    row_sums(dve, g, st, j)
                if i == 2:
                    groups_of(1)
            groups_of(2)
            row_variances(dve, g, st)

        @block.tensor
        def _(pe):
            norm_tensor(pe, g, n, xn, XT)
            pe.wait_ge(wl_ready, 1)
            for h in range(NHALF):
                t = slice(h * HALF, (h + 1) * HALF)
                pe.wait_ge(n["xl_ready"], TPH * (h + 1))
                for part, cols in enumerate((slice(ER, ER + NE), slice(0, ER))):
                    if h >= 1:
                        pe.wait_ge(small_ready, 2 * (h - 1) + part + 1)
                    m = cols.stop - cols.start
                    three_passes(pe, ps[0:m, SMALL[part], :], lambda c: (lah[:, c, cols], lal[:, c, cols]),
                                 lambda c: (g["xh"][:, c, t], g["xl"][:, c, t]), DC).then_inc(small_done, 1)
            pe.wait_ge(small_ready, 2 * NHALF - 1)
            for i in range(NT):
                last = pe.transpose(ps[:, LG, NE * i:NE * i + NE], lgT[:, i * P:(i + 1) * P], ident[0:NE, 0:NE])
            last.then_inc(lg_done, 1)

            def base(i):
                t = slice(i * P, (i + 1) * P)
                if i >= 4:
                    pe.wait_ge(x_ready, i - 3)
                three_passes(pe, ps[:, OUT[i % 4], :], lambda c: (g["xh"][:, c, t], g["xl"][:, c, t]),
                             lambda c: (wbh[:, c, :], wbl[:, c, :]), DC, final=False)

            def experts(i):
                pe.wait_ge(wx_ready, i + 1)
                if i >= 1:
                    pe.wait_ge(hw_ready, i)
                pe.transpose(ps[:, WX, 0:P], wx[:, i % 2, :], ident[:, :]).then_inc(wxT_done, 1)
                if i + 3 < NT and i >= 1:
                    base(i + 3)
                pe.wait_ge(hw_ready, i + 1)
                pe.matmul(ps[:, OUT[i % 4], :], hwT[:, i % 2, :], lb[:, :], start=False, stop=True).then_inc(out_done, 1)

            pe.wait_ge(wl_ready, 2)
            for i in range(4):
                base(i)
            for i in range(NT):
                experts(i)


def rotary_attention(nc, a, g):
    ps, x, ident, gate = g["ps"], g["x"], g["ident"], g["gate"]
    wqh, wql, wkvh, wkvl = g["wqh"], g["wql"], g["wkvh"], g["wkvl"]
    SCALE = float(np.float32(1.0) / np.sqrt(np.float32(DK)))
    SLOTS = NKV * NHALF
    STEPS = SLOTS * TPH
    NROT = 1 + GRP
    with ExitStack() as ctx:
        def sb(name, shape, dt=F32):
            return ctx.enter_context(nc.sbuf_tensor(name, shape, dt))

        def sem(name):
            return ctx.enter_context(nc.semaphore("c_" + name))

        ch, cl = g["ch"], g["cl"]
        cs = sb("cs", [P, 2, C])
        mask = sb("mask", [P, NT, C])
        woh = g["woh"] = sb("woh", [P, 2, GRP, D], F32R)
        wol = g["wol"] = sb("wol", [P, 2, GRP, D], F32R)
        qT = sb("qT", [P, GRP, TOK])
        kT = sb("kT", [P, TOK])
        vT = sb("vT", [P, HALF])
        v = sb("v", [P, NT, DK])
        ra = sb("ra", [P, 2, HALF])
        rb = sb("rb", [P, 2, HALF])
        s = sb("s", [P, 2, GRP, C])
        mx = sb("c_mx", [P, GRP])
        sm = sb("c_sm", [P, GRP])
        rs = sb("c_rs", [P, 2, GRP])
        bd = sb("bd", [P, 2, GRP, P])
        aT = sb("aT", [P, GRP * P])
        oh = sb("oh", [P, 2, GRP * P], F32R)
        ol = sb("ol", [P, 2, GRP * P], F32R)
        xn = bd[:, :, :, :].rearrange("p b h k -> p b (h k)")

        n = norm_sems(sem, "n")
        st = stat_sems(sem)
        low_ready = g["low_ready"]
        loaded = sem("loaded")
        bd_zeroed = sem("bd_zeroed")
        proj_done = sem("proj_done")
        rope_a = sem("rope_a")
        rope_ready = sem("rope_ready")
        vproj_done = sem("vproj_done")
        vT_ready = sem("vT_ready")
        vtr_done = sem("vtr_done")
        v_ready = sem("v_ready")
        sc_done = sem("sc_done")
        masked = sem("masked")
        max_ready = sem("max_ready")
        shifted = sem("shifted")
        exp_ready = sem("exp_ready")
        sum_ready = sem("sum_ready")
        rs_ready = sem("rs_ready")
        bd_ready = sem("bd_ready")
        aT_done = sem("aT_done")
        aT_ready = sem("aT_ready")
        pv_done = sem("pv_done")
        oh_ready, ol_ready = sem("oh_ready"), sem("ol_ready")
        wo_done = sem("wo_done")
        x_ready = sem("x_ready")

        PROJ = (0, 1)
        SCB = (2, 3)
        TR, PV, WO = 4, 5, (6, 7)

        block = ctx.enter_context(nc.Block())

        @block.sync
        def _(sp):
            sp.dma_start(cs[:, :, :], a["rope"].rearrange("p (a t) -> p a t", a=2)).then_inc(loaded, 16)
            sp.dma_start(mask[:, :, :], a["mask"].rearrange("(i b) q k -> (b q) i k", b=BT)).then_inc(loaded, 16)
            load_piece(sp, a, g, 0, O23)
            for kv in range(1, NKV):
                for piece in range(5):
                    load_piece(sp, a, g, kv, piece)

        def piece_due(m):
            slot, j = m // TPH, m % TPH
            if slot // NHALF + 1 >= NKV:
                return None
            return {(0, 1): KV, (0, 2): Q01, (1, 0): Q23, (1, 1): O01, (1, 2): O23}.get((slot % NHALF, j))

        BANK_OF = (0, 0, 1, 0, 1)
        ROTARY_OF = {0: (0,), 1: (1, 2), 2: (3,), 3: (4,)}

        @block.gpsimd
        def _(pool):
            def rotary_sum(slot, p):
                r = NROT * slot + p
                h = slot % NHALF
                pool.wait_ge(rope_a, r + 1)
                if slot >= NHALF:
                    pool.wait_ge(sc_done, TPH * (slot - 1))
                dst = (kT[:, :] if p == 0 else qT[:, p - 1, :])[:, h * HALF:(h + 1) * HALF]
                pool.tensor_tensor(dst, ra[:, r % 2, :], rb[:, r % 2, :], ALU.add).then_inc(rope_ready, 1)

            def shift(m):
                pool.wait_ge(max_ready, m + 1)
                pool.tensor_tensor(s[:, m % 2, :, :], s[:, m % 2, :, :],
                                   mx[:, :].unsqueeze(2).broadcast_to([P, GRP, C]), ALU.subtract).then_inc(shifted, 1)

            rotary_sum(0, 0)
            pool.wait_ge(n["xt_done"], NT)
            pool.memset(bd[:, :, :, :], 0.0).then_inc(bd_zeroed, 1)
            for p in range(1, NROT):
                rotary_sum(0, p)
            low_piece(pool, g, 0, O01)
            low_piece(pool, g, 0, O23)
            for m in range(STEPS):
                slot, j = m // TPH, m % TPH
                shift(m)
                if slot + 1 < SLOTS:
                    for p in ROTARY_OF[j]:
                        rotary_sum(slot + 1, p)
                if piece_due(m) is not None:
                    low_piece(pool, g, slot // NHALF + 1, piece_due(m))
            row_scales(pool, g, st)

        @block.scalar
        def _(act):
            def high_part(kv, piece):
                if piece == KV:
                    act.wait_ge(vproj_done, NHALF * kv)
                elif piece in (Q01, Q23):
                    act.wait_ge(proj_done, NROT * (NHALF * kv - 1) + 2 * (piece - Q01) + 3)
                elif kv >= 2:
                    act.wait_ge(wo_done, NT * (kv - 1))
                high_piece(act, g, kv, piece)

            def values_out(slot):
                act.wait_ge(vproj_done, slot + 1)
                if slot >= 1:
                    act.wait_ge(vtr_done, slot)
                act.activation(vT[:, :], ps[:, PROJ[1], :], ACT.Copy).then_inc(vT_ready, 1)

            def values(slot):
                h = slot % NHALF
                act.wait_ge(vtr_done, slot + 1)
                if slot >= NHALF:
                    act.wait_ge(pv_done, TPH * (slot - 1))
                act.activation(v[:, h * TPH:(h + 1) * TPH, :], ps[:, TR, :].rearrange("p (i d) -> p i d", i=TPH),
                               ACT.Copy).then_inc(v_ready, 1)

            def exps(m):
                act.wait_ge(shifted, m + 1)
                act.activation(s[:, m % 2, :, :], s[:, m % 2, :, :], ACT.Exp).then_inc(exp_ready, 1)

            def turned(m):
                act.wait_ge(aT_done, m + 1)
                if m >= 1:
                    act.wait_ge(pv_done, m)
                act.activation(aT[:, :], ps[:, TR, :], ACT.Copy).then_inc(aT_ready, 1)

            def high_out(m):
                act.wait_ge(pv_done, m + 1)
                if m >= 2:
                    act.wait_ge(wo_done, m - 1)
                act.activation(oh[:, m % 2, :], ps[:, PV, :], ACT.Copy).then_inc(oh_ready, 1)

            for i in range(TPH):
                norm_high(act, g, n, SCB, i)
            values_out(0)
            for i in range(TPH, NT):
                norm_high(act, g, n, SCB, i)
            values(0)
            high_piece(act, g, 0, O01)
            high_piece(act, g, 0, O23)
            for m in range(STEPS + 2):
                slot, j = m // TPH, m % TPH
                if m >= 2:
                    turned(m - 2)
                if m < STEPS:
                    exps(m)
                if piece_due(m) is not None:
                    high_part(slot // NHALF + 1, piece_due(m))
                if m >= 2:
                    high_out(m - 2)
                if slot + 1 < SLOTS:
                    if j == 0:
                        values_out(slot + 1)
                    if j == 2:
                        values(slot + 1)

        @block.vector
        def _(dve):
            def rotary(slot, p):
                r = NROT * slot + p
                bank = ps[:, PROJ[BANK_OF[p]], :].rearrange("p (b t) -> p b t", t=C)
                dve.wait_ge(proj_done, r + 1)
                if r >= 2:
                    dve.wait_ge(rope_ready, r - 1)
                A = ra[:, r % 2, :].rearrange("p (b t) -> p b t", t=C)
                R_ = rb[:, r % 2, :].rearrange("p (b t) -> p b t", t=C)
                nb = HALF // C
                hd = DK // 2
                dve.tensor_tensor(A, bank, cs[:, 0, :].unsqueeze(1).broadcast_to([P, nb, C]), ALU.mult)
                dve.tensor_tensor(R_[0:hd], bank[hd:DK], cs[0:hd, 1, :].unsqueeze(1).broadcast_to([hd, nb, C]), ALU.mult)
                dve.tensor_tensor(R_[hd:DK], bank[0:hd], cs[hd:DK, 1, :].unsqueeze(1).broadcast_to([hd, nb, C]), ALU.mult)\
                   .then_inc(rope_a, 1)

            def maximum(m):
                i = m % NT
                dve.wait_ge(sc_done, m + 1)
                if m >= 2:
                    dve.wait_ge(bd_ready, 2 * (m - 1))
                bank = ps[:, SCB[m % 2], :].rearrange("p (h k) -> p h k", h=GRP)
                for b in range(BT):
                    rows = slice(b * C, (b + 1) * C)
                    dve.scalar_tensor_tensor(s[rows, m % 2, :, :], bank[rows, :, b * C:(b + 1) * C], SCALE,
                                             mask[rows, i, :].unsqueeze(1).broadcast_to([C, GRP, C]), ALU.mult, ALU.add)\
                       .then_inc(masked, 1)
                dve.wait_ge(masked, 2 * (m + 1))
                if m >= 1:
                    dve.wait_ge(shifted, m)
                dve.tensor_reduce(mx[:, :], s[:, m % 2, :, :], AX.X, ALU.max).then_inc(max_ready, 1)

            def sums(m):
                dve.wait_ge(exp_ready, m + 1)
                dve.tensor_reduce(sm[:, :], s[:, m % 2, :, :], AX.X, ALU.add).then_inc(sum_ready, 1)
                dve.wait_ge(sum_ready, m + 1)
                dve.reciprocal(rs[:, m % 2, :], sm[:, :]).then_inc(rs_ready, 1)
                dve.wait_ge(rs_ready, m + 1)
                if m >= 2:
                    dve.wait_ge(aT_done, m - 1)
                for b in range(BT):
                    rows = slice(b * C, (b + 1) * C)
                    dve.tensor_tensor(bd[rows, m % 2, :, b * C:(b + 1) * C], s[rows, m % 2, :, :],
                                      rs[rows, m % 2, :].unsqueeze(2).broadcast_to([C, GRP, C]), ALU.mult)\
                       .then_inc(bd_ready, 1)

            def low_out(m):
                dve.wait_ge(oh_ready, m + 1)
                dve.tensor_tensor(ol[:, m % 2, :], ps[:, PV, :], oh[:, m % 2, :].bitcast(F32), ALU.subtract).then_inc(ol_ready, 1)

            def add(m):
                i = m % NT
                dve.wait_ge(wo_done, m + 1)
                dve.scalar_tensor_tensor(x[:, i, :], ps[:, WO[m % 2], :], gate[:, 1:2], x[:, i, :], ALU.mult, ALU.add)\
                   .then_inc(x_ready, 1)
                if m >= NT * (NKV - 1):
                    dve.wait_ge(x_ready, m + 1)
                    row_sums(dve, g, st, i)

            dve.wait_ge(loaded, 32)
            norm_rows(dve, g, n, xn, 0)
            for i in range(1, NT):
                norm_rows(dve, g, n, xn, i)
                norm_low(dve, g, n, SCB, i - 1)
                if i == 3:
                    rotary(0, 0)
            norm_low(dve, g, n, SCB, NT - 1)
            for p in range(1, NROT):
                rotary(0, p)
            dve.wait_ge(bd_zeroed, 1)
            for m in range(STEPS + 3):
                slot, j = m // TPH, m % TPH
                if m >= 3:
                    low_out(m - 3)
                if m < STEPS:
                    maximum(m)
                if slot + 1 < SLOTS:
                    rotary(slot + 1, ROTARY_OF[j][0])
                if m >= 3:
                    add(m - 3)
                if m < STEPS:
                    sums(m)
                if slot + 1 < SLOTS and j == 1:
                    rotary(slot + 1, ROTARY_OF[j][1])
            row_variances(dve, g, st)

        @block.tensor
        def _(pe):
            def project(slot, p):
                kv, h = slot // NHALF, slot % NHALF
                r = NROT * slot + p
                t = slice(h * HALF, (h + 1) * HALF)
                dst = ps[:, PROJ[BANK_OF[p]], :]
                if p == 0 and slot >= 1:
                    pe.wait_ge(rope_a, r - 1)
                elif p == 1:
                    pe.wait_ge(rope_a, r)
                elif p == 2:
                    pe.wait_ge(vT_ready, slot + 1)
                elif p >= 3:
                    pe.wait_ge(rope_a, r - 1)
                if p == 0:
                    pe.wait_ge(low_ready, 5 * kv + KV + 1)
                    last = three_passes(pe, dst, lambda c: (wkvh[:, 0, c, :], wkvl[:, 0, c, :]),
                                        lambda c: (ch[:, c, t], cl[:, c, t]), DC)
                else:
                    pe.wait_ge(low_ready, 5 * kv + Q01 + (p - 1) // 2 + 1)
                    cols = slice((p - 1) * DK, p * DK)
                    last = three_passes(pe, dst, lambda c: (wqh[:, c, cols], wql[:, c, cols]),
                                        lambda c: (g["xh"][:, c, t], g["xl"][:, c, t]), DC)
                last.then_inc(proj_done, 1)

            def project_v(slot):
                h = slot % NHALF
                t = slice(h * HALF, (h + 1) * HALF)
                if slot >= 1:
                    pe.wait_ge(rope_a, NROT * slot)
                three_passes(pe, ps[:, PROJ[1], :], lambda c: (wkvh[:, 1, c, :], wkvl[:, 1, c, :]),
                             lambda c: (ch[:, c, t], cl[:, c, t]), DC).then_inc(vproj_done, 1)

            def turn_v(slot):
                pe.wait_ge(vT_ready, slot + 1)
                if slot >= 1:
                    pe.wait_ge(aT_ready, TPH * (slot - 1) + 1)
                for i in range(TPH):
                    last = pe.transpose(ps[:, TR, i * P:(i + 1) * P], vT[:, i * P:(i + 1) * P], ident[:, :])
                last.then_inc(vtr_done, 1)

            def scores(m):
                i = m % NT
                if m % TPH == 0:
                    pe.wait_ge(rope_ready, NROT * (m // TPH + 1))
                if m >= 2:
                    pe.wait_ge(masked, 2 * (m - 1))
                t = slice(i * P, (i + 1) * P)
                for h in range(GRP):
                    last = pe.matmul(ps[:, SCB[m % 2], h * P:(h + 1) * P], qT[:, h, t], kT[:, t], start=True, stop=True)
                last.then_inc(sc_done, 1)

            def turn(m):
                pe.wait_ge(bd_ready, 2 * (m + 1))
                if m >= 1:
                    pe.wait_ge(aT_ready, m)
                if m == 0:
                    pe.wait_ge(v_ready, 1)
                elif m % TPH == 1 and m // TPH + 1 < SLOTS:
                    pe.wait_ge(v_ready, m // TPH + 2)
                for h in range(GRP):
                    last = pe.transpose(ps[:, TR, h * P:(h + 1) * P], bd[:, m % 2, h, :], ident[:, :])
                last.then_inc(aT_done, 1)

            def weighted(m):
                pe.wait_ge(aT_ready, m + 1)
                if m >= 1:
                    pe.wait_ge(ol_ready, m)
                pe.matmul(ps[:, PV, :], v[:, m % NT, :], aT[:, :], start=True, stop=True).then_inc(pv_done, 1)

            def project_out(m):
                kv = m // NT
                if m % NT == 0:
                    pe.wait_ge(low_ready, 5 * kv + O23 + 1)
                pe.wait_ge(ol_ready, m + 1)
                if m >= 2:
                    pe.wait_ge(x_ready, m - 1)
                three_passes(pe, ps[:, WO[m % 2], :],
                             lambda h: (oh[:, m % 2, h * P:(h + 1) * P], ol[:, m % 2, h * P:(h + 1) * P]),
                             lambda h: (woh[:, kv % 2, h, :], wol[:, kv % 2, h, :]), GRP).then_inc(wo_done, 1)

            norm_turn(pe, g, n, xn, SCB, 0)
            norm_turn(pe, g, n, xn, SCB, 1)
            project(0, 0)
            norm_turn(pe, g, n, xn, SCB, 2)
            norm_turn(pe, g, n, xn, SCB, 3)
            project_v(0)
            norm_turn(pe, g, n, xn, SCB, 4)
            norm_turn(pe, g, n, xn, SCB, 5)
            project(0, 1)
            norm_turn(pe, g, n, xn, SCB, 6)
            norm_turn(pe, g, n, xn, SCB, 7)
            project(0, 2)
            turn_v(0)
            project(0, 3)
            project(0, 4)
            pe.wait_ge(n["xl_ready"], NT)
            scores(0)
            for m in range(STEPS + 3):
                slot, j = m // TPH, m % TPH
                more = slot + 1 < SLOTS
                if 2 <= m < STEPS + 2:
                    turn(m - 2)
                if more:
                    project(slot + 1, ROTARY_OF[j][0])
                if m >= 3:
                    project_out(m - 3)
                if 2 <= m < STEPS + 2:
                    weighted(m - 2)
                if more and j == 0:
                    project_v(slot + 1)
                if more and j == 1:
                    project(slot + 1, ROTARY_OF[j][1])
                if more and j == 2:
                    turn_v(slot + 1)
                if m + 1 < STEPS:
                    scores(m + 1)


def gate_up(nc, a, g):
    ps, x, ident, gate, h, wd = g["ps"], g["x"], g["ident"], g["gate"], g["h"], g["wd"]
    QR = P // PACK
    onehot, rows = g["onehot"], g["rows"]
    with ExitStack() as ctx:
        def sb(name, shape, dt=F32):
            return ctx.enter_context(nc.sbuf_tensor(name, shape, dt))

        def sem(name):
            return ctx.enter_context(nc.semaphore("d_" + name))

        xn = sb("d_xn", [P, 2, D])
        nib = sb("nib", [P, 1], I32)
        qraw = sb("qraw", [P, 2, D], I32)
        qn = sb("qn", [P, D], I32)
        wf = sb("wf", [P, 2, D])
        wh = sb("wh", [P, 4, D], F32R)
        wl = sb("wl", [P, 4, D], F32R)
        th = sb("th", [P, HALF])
        sg = sb("sg", [P, HALF])

        n = norm_sems(sem, "n")
        consts = sem("consts")
        step = sem("step")
        q_landed = [sem(f"q_landed{i}") for i in range(2)]
        zs_done = sem("zs_done")
        q_used = sem("q_used")
        unit_ready = sem("unit_ready")
        wh_ready = sem("wh_ready")
        wl_ready = sem("wl_ready")
        gu_done = sem("gu_done")
        th_ready = sem("th_ready")
        h_ready = sem("h_ready")

        Z, SC = (0, 1), (2, 3)
        GU = (4, 5, 6, 7)
        UNITS = 3 * NTI

        block = ctx.enter_context(nc.Block())

        def packed(t, m):
            name, k, ncols, _ = MATS[m]
            q = a[name + "_qweight"]
            if m < 2:
                return [(QR, bass.AP(q.tensor, q.offset + QR * c * ncols + P * t, [[ncols, QR], [0, PACK], [1, inner(t)]]))
                        for c in range(DC)]
            r = inner(t) // PACK
            return [(r, bass.AP(q.tensor, q.offset + QR * t * ncols, [[ncols, r], [0, PACK], [1, ncols]]))]

        def load_unit(sp, u):
            t, m = u // 3, u % 3
            if u >= 2:
                sp.wait_ge(q_used, u - 1)
            for c, (r, src) in enumerate(packed(t, m)):
                w = inner(t) if m < 2 else D
                dst = qraw[0:PACK * r, u % 2, c * P:c * P + w]
                sp.dma_start(dst, src).then_inc(q_landed[u % 2], 16)

        @block.sync
        def _(sp):
            sp.dma_start(nib[:, :], a["nib"]).then_inc(consts, 16)
            for u in range(UNITS):
                load_unit(sp, u)

        def landed(u):
            return 16 * sum(DC if v % 3 < 2 else 1 for v in range(u % 2, u + 1, 2))

        def unit_view(buf, t, m):
            if m == 2:
                return buf[0:inner(t), :]
            return buf.rearrange("p (c n) -> p c n", c=DC)[:, :, 0:inner(t)]

        @block.gpsimd
        def _(pool):
            for u in range(UNITS):
                t, m = u // 3, u % 3
                if m == 2:
                    continue
                k = 2 * t + m
                pool.wait_ge(wh_ready, k + 1)
                pool.tensor_tensor(unit_view(wl[:, k % 4, :], t, m), unit_view(wf[:, m, :], t, m),
                                   unit_view(wh[:, k % 4, :], t, m).bitcast(F32), ALU.subtract).then_inc(wl_ready, 1)

        @block.scalar
        def _(act):
            def high(t, m):
                k = 2 * t + m
                act.wait_ge(unit_ready, 3 * t + m + 1)
                if k >= 4:
                    act.wait_ge(gu_done, 4 * (t - 1))
                act.activation(unit_view(wh[:, k % 4, :], t, m), unit_view(wf[:, m, :], t, m), ACT.Copy).then_inc(wh_ready, 1)

            high(0, 0)
            high(0, 1)
            norm_scalar(act, g, n, GU)
            for t in range(NTI):
                if t + 1 < NTI:
                    high(t + 1, 0)
                    high(t + 1, 1)
                for hf in range(NHALF):
                    w = inner(t)
                    act.wait_ge(gu_done, 4 * t + 2 * hf + 1)
                    if 2 * t + hf >= 1:
                        act.wait_ge(h_ready, 2 * t + hf)
                    act.activation(th[0:w, :], ps[0:w, GU[2 * hf], :], ACT.Tanh, scale=0.5).then_inc(th_ready, 1)

        @block.vector
        def _(dve):
            chain = [0]

            def link(ins):
                chain[0] += 1
                ins.then_inc(step, 1)
                dve.wait_ge(step, chain[0])

            def unpack(u):
                t, m = u // 3, u % 3
                dve.wait_ge(q_landed[u % 2], landed(u))
                rows_of = inner(t) if m == 2 else P
                dve.tensor_scalar(unit_view(qn[:, :], t, m), unit_view(qraw[:, u % 2, :], t, m), nib[0:rows_of, 0:1],
                                  15, ALU.logical_shift_right, ALU.bitwise_and).then_inc(q_used, 1)
                dve.wait_ge(q_used, u + 1)
                dve.wait_ge(zs_done, u + 1)
                if m == 2:
                    dst = wd[0:inner(t), t, :]
                else:
                    if t >= 1:
                        dve.wait_ge(wl_ready, 2 * (t - 1) + m + 1)
                    dst = unit_view(wf[:, m, :], t, m)
                link(dve.tensor_tensor(dst, unit_view(qn[:, :], t, m), unit_view(ps[:, Z[u % 2], :], t, m), ALU.subtract))
                dve.tensor_tensor(dst, dst, unit_view(ps[:, SC[u % 2], :], t, m), ALU.mult).then_inc(unit_ready, 1)

            dve.wait_ge(consts, 16)
            unpack(0)
            unpack(1)
            norm_vector(dve, g, n, xn, GU)
            unpack(2)
            for t in range(NTI):
                w = inner(t)
                if t + 1 < NTI:
                    unpack(3 * t + 3)
                    unpack(3 * t + 4)
                for hf in range(NHALF):
                    dve.wait_ge(th_ready, 2 * t + hf + 1)
                    link(dve.scalar_tensor_tensor(sg[0:w, :], th[0:w, :], 1.0, ps[0:w, GU[2 * hf], :], ALU.add, ALU.mult))
                    dve.wait_ge(gu_done, 4 * t + 2 * hf + 2)
                    dve.scalar_tensor_tensor(h[0:w, t, hf * HALF:(hf + 1) * HALF], sg[0:w, :], 0.5, ps[0:w, GU[2 * hf + 1], :],
                                             ALU.mult, ALU.mult).then_inc(h_ready, 1)
                if t + 1 < NTI:
                    unpack(3 * t + 5)

        @block.tensor
        def _(pe):
            def zeros_and_scales(u):
                t, m = u // 3, u % 3
                if u >= 2:
                    pe.wait_ge(unit_ready, u - 1)
                pieces = [(ROW0[m] + c * P, P, COL0[m] + t * P, c * P, inner(t)) for c in range(DC)]
                if m == 2:
                    pieces = [(ROW0[m] + t * P, inner(t), COL0[m], 0, D)]
                for r0, k, c0, at, width in pieces:
                    pe.matmul(ps[0:k, Z[u % 2], at:at + width], onehot[96:128, r0:r0 + k], rows[96:128, c0:c0 + width],
                              start=True, stop=True)
                    last = pe.matmul(ps[0:k, SC[u % 2], at:at + width], onehot[0:96, r0:r0 + k], rows[0:96, c0:c0 + width],
                                     start=True, stop=True)
                last.then_inc(zs_done, 1)

            def products(t, hf, m):
                w, k = inner(t), 2 * t + m
                tok = slice(hf * HALF, (hf + 1) * HALF)
                pe.wait_ge(wl_ready, k + 1)
                if t >= 1:
                    pe.wait_ge(h_ready, 2 * (t - 1) + hf + 1)
                view = lambda buf: buf[:, k % 4, :].rearrange("p (c n) -> p c n", c=DC)
                three_passes(pe, ps[0:w, GU[2 * hf + m], :], lambda c: (view(wh)[:, c, 0:w], view(wl)[:, c, 0:w]),
                             lambda c: (g["xh"][:, c, tok], g["xl"][:, c, tok]), DC).then_inc(gu_done, 1)

            zeros_and_scales(0)
            zeros_and_scales(1)
            norm_tensor(pe, g, n, xn, GU)
            zeros_and_scales(2)
            pe.wait_ge(n["xl_ready"], NT)
            for t in range(NTI):
                for hf in range(NHALF):
                    for m in range(2):
                        if t + 1 < NTI and 2 * hf + m < 3:
                            zeros_and_scales(3 * (t + 1) + 2 * hf + m)
                        products(t, hf, m)


def down(nc, a, g, out):
    ps, x, gate, h, wd = g["ps"], g["x"], g["gate"], g["h"], g["wd"]
    with ExitStack() as ctx:
        def sb(name, shape, dt=F32):
            return ctx.enter_context(nc.sbuf_tensor(name, shape, dt))

        def sem(name):
            return ctx.enter_context(nc.semaphore("e_" + name))

        hh = sb("hh", [P, 2, TOK], F32R)
        hl = sb("hl", [P, 2, TOK], F32R)
        wdh = sb("wdh", [P, 2, D], F32R)
        wdl = sb("wdl", [P, 2, D], F32R)
        res = sb("res", [P, 2, D])
        wh_ready = sem("wh_ready")
        wl_ready = sem("wl_ready")
        hh_ready = sem("hh_ready")
        hl_ready = sem("hl_ready")
        tile_done = sem("tile_done")
        out_done = sem("out_done")
        res_ready = sem("res_ready")
        stored = [sem(f"stored{i}") for i in range(2)]
        block = ctx.enter_context(nc.Block())

        @block.sync
        def _(sp):
            rows = out.rearrange("b s d -> (b s) d")
            for i in range(NT):
                sp.wait_ge(res_ready, i + 1)
                sp.dma_start(rows[i * P:(i + 1) * P, :], res[:, i % 2, :]).then_inc(stored[i % 2], 16)
            sp.wait_ge(stored[0], 16 * (NT // 2))
            sp.wait_ge(stored[1], 16 * (NT // 2))

        @block.scalar
        def _(act):
            for t in range(NTI):
                w = inner(t)
                if t >= 2:
                    act.wait_ge(tile_done, t - 1)
                act.activation(wdh[0:w, t % 2, :], wd[0:w, t, :], ACT.Copy).then_inc(wh_ready, 1)
                act.activation(hh[0:w, t % 2, :], h[0:w, t, :], ACT.Copy).then_inc(hh_ready, 1)

        @block.gpsimd
        def _(pool):
            for t in range(NTI):
                w = inner(t)
                pool.wait_ge(wh_ready, t + 1)
                pool.tensor_tensor(wdl[0:w, t % 2, :], wd[0:w, t, :], wdh[0:w, t % 2, :].bitcast(F32), ALU.subtract)\
                    .then_inc(wl_ready, 1)

        @block.vector
        def _(dve):
            for t in range(NTI):
                w = inner(t)
                dve.wait_ge(hh_ready, t + 1)
                dve.tensor_tensor(hl[0:w, t % 2, :], h[0:w, t, :], hh[0:w, t % 2, :].bitcast(F32), ALU.subtract)\
                   .then_inc(hl_ready, 1)
            for i in range(NT):
                dve.wait_ge(out_done, i + 1)
                if i >= 2:
                    dve.wait_ge(stored[i % 2], 16 * (i // 2))
                dve.scalar_tensor_tensor(res[:, i % 2, :], ps[:, i, :], gate[:, 3:4], x[:, i, :], ALU.mult, ALU.add)\
                   .then_inc(res_ready, 1)

        @block.tensor
        def _(pe):
            for t in range(NTI):
                w = inner(t)
                pe.wait_ge(wl_ready, t + 1)
                pe.wait_ge(hl_ready, t + 1)
                for i in range(NT):
                    tok = slice(i * P, (i + 1) * P)
                    last = three_passes(pe, ps[:, i, :], lambda c: (hh[0:w, t % 2, tok], hl[0:w, t % 2, tok]),
                                        lambda c: (wdh[0:w, t % 2, :], wdl[0:w, t % 2, :]), 1,
                                        first=(t == 0), final=(t == NTI - 1))
                    if t == NTI - 1:
                        last.then_inc(out_done, 1)
                if t < NTI - 1:
                    last.then_inc(tile_done, 1)


SWDGE_BYTES = 8192


def constants():
    f = np.float32
    pos = np.arange(C, dtype=f)
    inv = (f(1.0) / np.power(f(10000.0), np.arange(0, DK, 2, dtype=f) / f(DK))).astype(f)
    ang = inv[:, None] * pos[None, :]
    cos, sin = np.cos(ang).astype(f), np.sin(ang).astype(f)
    rope = np.concatenate([np.concatenate([cos, cos]), np.concatenate([-sin, sin])], axis=1)
    ch = np.arange(P)
    sel = np.zeros((P, 2, 2 * BH), f)
    spread = np.zeros((P, WG, P), f)
    for e in range(2):
        sel[ch, e, e * BH + ch // LHD] = 1
    for w in range(WG):
        spread[w * BH + ch // LHD, w, ch] = 1
    return {
        "ident": np.eye(P, dtype=f),
        "rope": rope,
        "sel": sel.reshape(P, -1),
        "spread": spread.reshape(P, -1),
        "iota": np.arange(NE, dtype=f),
        "nib": (BITS * (ch % PACK)).astype(np.int32)[:, None],
        "gnum": (ch % 32).astype(f)[:, None],
    }


def block_diagonal(w):
    r = np.zeros((P, P), w.dtype)
    for b in range(BT):
        r[b * C:(b + 1) * C, b * C:(b + 1) * C] = w.T
    return r


def kernel(**inputs):
    import numpy as _np
    import concourse.bacc as _bacc
    from concourse import mybir as _mybir
    from concourse.bass_utils import run_bass_kernel_spmd as _run

    i = {k: _np.asarray(v) for k, v in inputs.items()}
    arrays = {
        "x": i["x"], "ctx": i["ctx_4096"], "ctxT": i["ctx_4096"].reshape(TOK, D).T, "mask": i["mask_BxSxS2_ff0"],
        "g_xattn": i["g_xattn"], "g_ffn": i["g_ffn"],
        "W_base": i["L0_ffn_W_base"].T, "b_base": i["L0_ffn_b_base"], "W_router": i["L0_ffn_W_router"].T,
        "lora_A": i["L0_ffn_lora_A"].reshape(NE * RANK, D).T,
        "lora_B": i["L0_ffn_lora_B"].transpose(0, 2, 1).reshape(NE * RANK, D),
    }
    for n in "qkvo":
        arrays["W" + n] = block_diagonal(i["L0_xattn_W" + n])
        arrays["b" + n] = i["L0_xattn_b" + n]
        arrays["w" + n] = i["L1_xattn_w" + n]
    for m in ("gate", "up", "down"):
        for part in ("qweight", "scales", "qzeros", "g_idx"):
            arrays[f"{m}_{part}"] = i[f"L1_ffn_{m}_{part}"]
    arrays.update(constants())

    nc = _bacc.Bacc("TRN2", target_bir_lowering=False, num_devices=1, dynamic_dma_scratch_size=SWDGE_BYTES)
    given, aps = {}, {}
    for n, v in arrays.items():
        v = _np.ascontiguousarray(v)
        given[f"in_{n}"] = v
        aps[n] = nc.dram_tensor(f"in_{n}", v.shape, _mybir.dt.from_np(v.dtype), kind="ExternalInput").ap()
    out = nc.dram_tensor("out", (B, C, D), F32, kind="ExternalOutput").ap()
    build_program(nc, aps, out)
    return _run(nc, [given], core_ids=[0]).results[0]["out"]
```

```python
from contextlib import ExitStack

import numpy as np

import concourse.bass as bass
from concourse import mybir

F32 = mybir.dt.float32
F32R = mybir.dt.float32r
I32 = mybir.dt.int32
U32 = mybir.dt.uint32
BF16 = mybir.dt.bfloat16
ALU = mybir.AluOpType
ACT = mybir.ActivationFunctionType
AX = mybir.AxisListType

P = 128
B, C, D = 16, 64, 512
TOK = B * C
NT = TOK // P
BT = P // C
DC = D // P
HALF = 512
NHALF = TOK // HALF
TPH = HALF // P
EPS = 1e-5

LH, LHD, WIN = 8, 8, 16
PAD_L = WIN // 2
TPAD = D + WIN - 1
BH = BT * LH
WG = P // BH
GW = 4

NE, RANK = 8, 16
LORA_SCALE = 32.0 / 16.0

NQ, NKV, DK = 32, 8, 128
GRP = NQ // NKV

INTER, PACK, BITS = 1376, 8, 4
NTI = -(-INTER // P)
PAIRED = (NTI - 2) // 2
GK, GD = D // 128, INTER // 128


MATS = (("gate", D, INTER, GK), ("up", D, INTER, GK), ("down", INTER, D, GD))
ROW0 = (0, D, 2 * D)
COL0 = (0, INTER, 2 * INTER)


def inner(t):
    return min(P, INTER - P * t)


def carve(buf, *parts):
    views, at = {}, 0
    for name, length in parts:
        views[name] = buf[:, at:at + length]
        at += length
    assert at <= buf.shape[1]
    return views


def build_program(nc, a, out):
    with ExitStack() as top:
        def sbuf(ctx, name, shape, dt=F32):
            return ctx.enter_context(nc.sbuf_tensor(name, shape, dt))

        ps = top.enter_context(nc.psum_tensor("ps", [P, 8, 512], F32))
        x = sbuf(top, "x", [P, NT, D])
        ident = sbuf(top, "ident", [P, P])
        gate = sbuf(top, "gate", [P, 4])
        stats = sbuf(top, "stats", [P, NT, 6])
        mv = sbuf(top, "mv", [P, NT, 2])
        veps = sbuf(top, "veps", [P, NT])
        rstd = sbuf(top, "rstd", [P, NT])
        mhalf = sbuf(top, "mhalf", [P, NT])
        g = dict(ps=ps, x=x, ident=ident, gate=gate, stats=stats, mv=mv, veps=veps, rstd=rstd, mhalf=mhalf)
        g["piece_landed"] = [top.enter_context(nc.semaphore(f"piece_landed{i}")) for i in range(2)]
        g["nib"] = sbuf(top, "nib", [P, 1], I32)
        g["qraw"] = sbuf(top, "qraw", [P, 2, D], I32)
        g["q_landed"] = [top.enter_context(nc.semaphore(f"q_landed{i}")) for i in range(2)]
        g["q_used"] = top.enter_context(nc.semaphore("q_used"))
        for name in ("wdh_ready", "wdl_ready", "hh_ready", "hl_ready"):
            g[name] = top.enter_context(nc.semaphore(name))
        g["iota"] = sbuf(top, "iota", [P, NE])
        g["gnum"] = sbuf(top, "gnum", [P, 1])
        g["idx_landed"] = [top.enter_context(nc.semaphore(f"idx_landed{i}")) for i in range(2)]
        for name in ("high_ready", "low_ready", "lora_landed", "cleared", "scales_landed", "scales_step", "rest_ready", "parts_ready",
                     "rows_ready"):
            g[name] = top.enter_context(nc.semaphore(name))
        g["onehot"] = sbuf(top, "onehot", [P, 2 * D + INTER], BF16)
        g["rows"] = sbuf(top, "rows", [P, 2 * INTER + D], BF16)
        with ExitStack() as first:
            g["stage"] = sbuf(first, "stage", [P, 2, 2 * D])
            shared = sbuf(first, "shared", [P, 8 * TOK])
            views = carve(shared, ("qT", GRP * TOK), ("kT", TOK), ("vT", HALF), ("mask", NT * C), ("ra", 2 * HALF), ("rb", 2 * HALF))
            g["qT"] = views["qT"].rearrange("p (h t) -> p h t", h=GRP)
            g["kT"] = views["kT"]
            g["vT"] = views["vT"]
            g["mask"] = views["mask"].rearrange("p (i k) -> p i k", i=NT)
            g["ra"], g["rb"] = (views[name].rearrange("p (b t) -> p b t", b=2) for name in ("ra", "rb"))
            views = carve(shared, ("wb_raw", DC * D), ("la_raw", DC * (NE * RANK + NE)), ("lb", D), ("bb", D), ("gi", INTER),
                          ("srow", INTER), ("rest", INTER), ("zq0", INTER // PACK), ("zq1", INTER // PACK))
            g["wb_raw"] = views["wb_raw"].rearrange("p (c n) -> p c n", c=DC)
            g["la_raw"] = views["la_raw"].rearrange("p (c n) -> p c n", c=DC)
            for name in ("lb", "bb", "srow", "rest"):
                g[name] = views[name]
            g["gi"] = [views[name].bitcast(I32) for name in ("gi", "srow")]
            g["zq"] = [views[name].bitcast(I32) for name in ("zq0", "zq1")]
            windowed_attention(nc, a, g)
            for name in ("xh", "xl", "ch", "cl"):
                g[name] = sbuf(first, name, [P, DC, TOK], F32R)
            for part in ("h", "l"):
                g["wq" + part] = sbuf(first, "wq" + part, [P, DC, GRP * DK], F32R)
                g["wkv" + part] = sbuf(first, "wkv" + part, [P, 2, DC, DK], F32R)
            routed_lora(nc, a, g)
            rotary_attention(nc, a, g)
        with ExitStack() as last:
            for name in ("xh", "xl"):
                g[name] = sbuf(last, name + "4", [P, DC, TOK], F32R)
            g["h"] = sbuf(last, "h", [P, NTI, TOK])
            g["wd"] = sbuf(last, "wd", [P, NTI, D])
            for name, cols in (("hh", TOK), ("hl", TOK), ("wdh", D), ("wdl", D)):
                g[name] = sbuf(last, name, [P, 2, cols], F32R)
            gate_up(nc, a, g)
            down(nc, a, g, out)


KV, Q01, Q23, O01, O23 = range(5)


def piece_number(pair, odd, piece):
    return 10 * pair + 5 * odd + piece


def stage_view(g, odd, piece):
    buf = g["stage"][:, (5 * odd + piece) % 2, :]
    if piece == KV:
        return buf.rearrange("p (j c n) -> p j c n", j=2, c=DC)
    if piece in (Q01, Q23):
        return buf.rearrange("p (c n) -> p c n", c=DC)
    return buf.rearrange("p (h n) -> p h n", h=2)


def piece_view(g, odd, piece, part):
    if piece == KV:
        return g["wkv" + part][:, :, :, :]
    if piece in (Q01, Q23):
        half = piece - Q01
        return g["wq" + part][:, :, half * 2 * DK:(half + 1) * 2 * DK]
    half = piece - O01
    return g["wo" + part][:, odd, 2 * half:2 * half + 2, :]


def load_piece(sp, a, g, pair, odd, piece, first=False):
    if not first:
        sp.wait_ge(g["low_ready"], piece_number(pair, odd, piece) - 1)
    dst = stage_view(g, odd, piece)
    landed = g["piece_landed"][(5 * odd + piece) % 2]
    kv, w = 2 * pair + odd, 2 * DK
    if piece == KV:
        for j, name in enumerate(("wk", "wv")):
            src = a[name].rearrange("(c p) n -> p c n", p=P)[:, :, bass.ds(kv * DK, DK)]
            sp.dma_start(dst[:, j, :, :], src).then_inc(landed, 16)
    elif piece in (Q01, Q23):
        src = a["wq"].rearrange("(c p) n -> p c n", p=P)[:, :, bass.ds((2 * kv + piece - Q01) * w, w)]
        sp.dma_start(dst, src).then_inc(landed, 16)
    else:
        src = a["wo"][bass.ds((2 * kv + piece - O01) * w, w), :].rearrange("(h p) n -> p h n", p=P)
        sp.dma_start(dst, src).then_inc(landed, 16)


def landed_count(pair, odd, piece):
    n = 5 * odd + piece
    return 96 * pair + 16 * sum(2 if k % 5 == KV else 1 for k in range(n % 2, n + 1, 2))


def high_piece(act, g, pair, odd, piece):
    act.wait_ge(g["piece_landed"][(5 * odd + piece) % 2], landed_count(pair, odd, piece))
    act.activation(piece_view(g, odd, piece, "h"), stage_view(g, odd, piece), ACT.Copy).then_inc(g["high_ready"], 1)


def low_piece(pool, g, pair, odd, piece):
    pool.wait_ge(g["high_ready"], piece_number(pair, odd, piece) + 1)
    pool.tensor_tensor(piece_view(g, odd, piece, "l"), stage_view(g, odd, piece),
                       piece_view(g, odd, piece, "h").bitcast(F32), ALU.subtract).then_inc(g["low_ready"], 1)


def windowed_attention(nc, a, g):
    ps, x, ident, gate = g["ps"], g["x"], g["ident"], g["gate"]
    stats, mv, veps, rstd, mhalf = g["stats"], g["mv"], g["veps"], g["rstd"], g["mhalf"]
    with ExitStack() as ctx:
        def sb(name, shape, dt=F32):
            return ctx.enter_context(nc.sbuf_tensor(name, shape, dt))

        def sem(name):
            return ctx.enter_context(nc.semaphore(name))

        ctxt = sb("ctxt", [P, NT, D])
        w4 = sb("w4", [P, 4, P])
        bias = sb("bias", [P, 4])
        gbo = sb("gbo", [P, 1])
        graw = sb("graw", [P, 4])
        sel = sb("sel", [P, 2, 32])
        spread_f = sb("spread_f", [P, WG, P])
        spread = sb("spread", [P, WG, P], F32R)
        xn = sb("xn", [P, 2, D])
        q = sb("q", [P, 2, D])
        kpad = sb("kpad", [P, 2, TPAD])
        vpad = sb("vpad", [P, 3, TPAD])
        prod = sb("prod", [P, WIN, D])
        sc = sb("sc", [P, 2, D])
        mx = sb("mx", [P, D // P, BH])
        att = sb("att", [P, D // P, WIN, BH])
        sm = sb("sm", [P, D // P, BH])
        rs = sb("rs", [P, D // P, BH])
        ath = sb("ath", [P, 2, D], F32R)
        atl = sb("atl", [P, 2, D], F32R)
        r = sb("r", [P, WIN, D])
        r2 = sb("r2", [P, WIN // 2, D])
        o = sb("o", [P, D])

        x_landed = [sem(f"x_landed{i}") for i in range(NT)]
        ctx_landed = [sem(f"ctx_landed{i}") for i in range(NT)]
        w4_landed = sem("w4_landed")
        small_landed = sem("small_landed")
        tables_landed = sem("tables_landed")
        half_set = sem("half_set")
        pad_zeroed = sem("pad_zeroed")
        gate_ready = sem("gate_ready")
        spread_ready = sem("spread_ready")
        dve_step = sem("dve_step")
        var_ready = sem("var_ready")
        rstd_ready = sem("rstd_ready")
        xn_ready = sem("xn_ready")
        qkv_done = sem("qkv_done")
        qkv_ready = sem("qkv_ready")
        prod_ready = sem("prod_ready")
        last_prod_ready = sem("last_prod_ready")
        prod_used = sem("prod_used")
        sc_ready = sem("sc_ready")
        fwd_done = sem("fwd_done")
        shifted = sem("shifted")
        exp_ready = sem("exp_ready")
        att_ready = sem("att_ready")
        back_done = sem("back_done")
        ath_ready = sem("ath_ready")
        atl_ready = sem("atl_ready")
        spread_done = sem("spread_done")
        r_ready = sem("r_ready")
        rsum_ready = sem("rsum_ready")
        out_done = sem("out_done")
        o_ready = sem("o_ready")
        x_ready = sem("x_ready")
        st = stat_sems(sem)

        S = [ps[:, 0, :], ps[:, 1, :]]
        T2 = ps[:, 2:4, :]
        T_time = T2.rearrange("p a (b g m) -> p (a b) g m", b=2, g=2)
        T_win = T2.rearrange("p a (b w h) -> p (a b) w h", b=2, w=WIN)
        RING = [ps[:, 4, :], ps[:, 5, :], ps[:, 6, :]]
        M = ps[:, 7, :]

        ORDER = [w + d for w in range(0, WIN // 2, 2) for d in (0, 1, WIN // 2, WIN // 2 + 1)]

        PARTS = WIN // GW

        def products(eng, i, part):
            w0 = GW * part
            k0 = kpad[:, i % 2, w0:w0 + D]
            windows = bass.AP(k0.tensor, k0.offset, [list(k0.ap[0]), [1, GW], [1, D]])
            qb = q[:, i % 2, :].unsqueeze(1).broadcast_to([P, GW, D])
            return eng.tensor_tensor(prod[:, w0:w0 + GW, :], qb, windows, ALU.mult)

        block = ctx.enter_context(nc.Block())

        @block.sync
        def _(sp):
            xr = a["x"].rearrange("b s d -> (b s) d")
            cr = a["ctx"].rearrange("b s d -> (b s) d")
            sp.dma_start(x[:, 0, :], xr[0:P, :]).then_inc(x_landed[0], 16)
            sp.dma_start(w4[:, :, :], a["W4"].rearrange("p (j c) -> p j c", j=4)).then_inc(w4_landed, 16)
            sp.dma_start(ctxt[:, 0, :], cr[0:P, :]).then_inc(ctx_landed[0], 16)
            for i in range(1, NT):
                sp.dma_start(x[:, i, :], xr[i * P:(i + 1) * P, :]).then_inc(x_landed[i], 16)
                sp.dma_start(ctxt[:, i, :], cr[i * P:(i + 1) * P, :]).then_inc(ctx_landed[i], 16)
            load_piece(sp, a, g, 0, 0, KV, first=True)
            load_piece(sp, a, g, 0, 0, Q01, first=True)
            lora_loads(sp, a, g)
            load_groups(sp, a, g, 0)
            for m in range(3):
                load_scales(sp, a, g, m)
            load_groups(sp, a, g, 1)

        @block.gpsimd
        def _(pool):
            pool.memset(kpad[:, :, :], 0.0).then_inc(pad_zeroed, 1)
            pool.memset(vpad[:, :, :], 0.0).then_inc(pad_zeroed, 1)
            pool.memset(mhalf[:, :], -0.5).then_inc(half_set, 1)
            pool.memset(g["srow"], 0.0).then_inc(g["cleared"], 1)
            for zq in g["zq"]:
                pool.memset(zq, 0).then_inc(g["cleared"], 1)
            pool.wait_ge(half_set, 1)

            def scale_of_rows(i):
                pool.wait_ge(var_ready, i + 1)
                pool.tensor_tensor(rstd[:, i:i + 1], veps[:, i:i + 1], mhalf[:, i:i + 1], ALU.pow).then_inc(rstd_ready, 1)

            scale_of_rows(0)
            scale_of_rows(1)
            for s in range(NT + 1):
                if s < NT:
                    pool.wait_ge(qkv_ready, 3 * s + 2)
                    if s >= 1:
                        pool.wait_ge(prod_used, 4 * s)
                    products(pool, s, PARTS - 1).then_inc(last_prod_ready, 1)
                if s + 2 < NT:
                    scale_of_rows(s + 2)
                m, k = (s - 2) // 2, (s - 2) % 2
                if 0 <= m < 3:
                    scales_pool(pool, g, m, k)
                if s >= 1:
                    i = s - 1
                    for w in range(0, WIN // 2, 2):
                        pool.wait_ge(r_ready, WIN * i + 2 * w + 4)
                        if i >= 1 and w == 0:
                            pool.wait_ge(out_done, i)
                        pool.tensor_tensor(r2[:, w:w + 2, :], r[:, w:w + 2, :], r[:, WIN // 2 + w:WIN // 2 + w + 2, :],
                                           ALU.add).then_inc(rsum_ready, 1)
            row_scales(pool, g, st)

        @block.scalar
        def _(act):
            act.dma_start(bias[:, :], a["bias"]).then_inc(small_landed, 16)
            act.dma_start(graw[:, :], a["gates"].partition_broadcast(P)).then_inc(small_landed, 16)
            act.dma_start(sel[:, :, :], a["sel"].rearrange("p (a b) -> p a b", a=2)).then_inc(tables_landed, 16)
            act.dma_start(ident[:, :], a["ident"]).then_inc(tables_landed, 16)
            act.dma_start(spread_f[:, :, :], a["spread"].rearrange("p (w c) -> p w c", w=WG)).then_inc(tables_landed, 16)
            act.wait_ge(small_landed, 32)
            act.activation(gate[:, :], graw[:, :], ACT.Tanh).then_inc(gate_ready, 1)
            act.wait_ge(gate_ready, 1)
            act.activation(gbo[:, :], bias[:, 3:4], ACT.Copy, scale=gate[:, 0:1]).then_inc(gate_ready, 1)
            act.wait_ge(pad_zeroed, 2)

            def project(i):
                act.wait_ge(qkv_done, 3 * i + 1)
                if i >= 2:
                    act.wait_ge(prod_ready, (PARTS - 1) * (i - 1))
                    act.wait_ge(last_prod_ready, i - 1)
                act.activation(q[:, i % 2, :], M, ACT.Identity, bias=bias[:, 0:1]).then_inc(qkv_ready, 1)
                act.wait_ge(qkv_done, 3 * i + 2)
                act.activation(kpad[:, i % 2, PAD_L:PAD_L + D], RING[0], ACT.Identity, bias=bias[:, 1:2])\
                   .then_inc(qkv_ready, 1)
                act.wait_ge(qkv_done, 3 * i + 3)
                if i >= 3:
                    act.wait_ge(r_ready, WIN * (i - 2))
                act.activation(vpad[:, i % 3, PAD_L:PAD_L + D], RING[1], ACT.Identity, bias=bias[:, 2:3])\
                   .then_inc(qkv_ready, 1)

            def output(i):
                act.wait_ge(out_done, i + 1)
                if i >= 1:
                    act.wait_ge(x_ready, i)
                act.activation(o[:, :], M, ACT.Identity, bias=gbo[:, 0:1], scale=gate[:, 0:1]).then_inc(o_ready, 1)

            project(0)
            act.wait_ge(tables_landed, 48)
            act.activation(spread[:, :, :], spread_f[:, :, :], ACT.Copy).then_inc(spread_ready, 1)
            for s in range(NT + 2):
                if 1 <= s <= NT:
                    act.wait_ge(shifted, s)
                    act.activation(att[:, :, :, :], att[:, :, :, :], ACT.Exp, scale=float(LHD) ** -0.5)\
                       .then_inc(exp_ready, 1)
                if s >= 2:
                    output(s - 2)
                if s + 1 < NT:
                    project(s + 1)
                if 1 <= s <= NT:
                    act.wait_ge(back_done, s)
                    if s >= 2:
                        act.wait_ge(spread_done, WIN * (s - 1))
                    act.activation(ath[:, :, :], T2, ACT.Copy).then_inc(ath_ready, 1)
                if s < NT:
                    act.wait_ge(prod_used, 4 * (s + 1))
                    if s >= 1:
                        act.wait_ge(fwd_done, s)
                    act.activation(sc[:, :, :], ps[:, 0:2, :], ACT.Copy).then_inc(sc_ready, 1)
                m, k = (s - 1) // 2, (s - 1) % 2
                if k == 0 and 1 <= m <= 3:
                    scales_scalar(act, g, m - 1, 2)
                if 0 <= m < 3:
                    scales_scalar(act, g, m, k)

        @block.vector
        def _(dve):
            chain = [0]

            def link(ins):
                chain[0] += 1
                ins.then_inc(dve_step, 1)
                dve.wait_ge(dve_step, chain[0])

            def statistics(i):
                dve.wait_ge(x_landed[i], 16)
                link(dve.bn_stats(stats[:, i, :], x[:, i, :]))
                link(dve.bn_aggr(mv[:, i, :], stats[:, i, :]))
                dve.tensor_scalar(veps[:, i:i + 1], mv[:, i, 1:2], EPS, None, ALU.add).then_inc(var_ready, 1)

            def normalise(i):
                dve.wait_ge(rstd_ready, i + 1)
                if i >= 2:
                    dve.wait_ge(qkv_done, 3 * (i - 2) + 1)
                dve.tensor_scalar(xn[:, i % 2, :], x[:, i, :], mv[:, i, 0:1], rstd[:, i:i + 1],
                                  ALU.subtract, ALU.mult).then_inc(xn_ready, 1)

            def part_of_products(i, part):
                if i >= 1:
                    dve.wait_ge(prod_used, 4 * (i - 1) + part + 1)
                products(dve, i, part).then_inc(prod_ready, 1)

            statistics(0)
            normalise(0)
            statistics(1)
            normalise(1)
            for s in range(NT + 2):
                if 1 <= s <= NT:
                    dve.wait_ge(fwd_done, s)
                    link(dve.tensor_reduce(mx[:, :, :], T_win.rearrange("p b w h -> p b h w"), AX.X, ALU.max))
                    if s >= 2:
                        dve.wait_ge(back_done, s - 1)
                    dve.tensor_tensor(att[:, :, :, :], T_win, mx[:, :, :].unsqueeze(2).broadcast_to([P, D // P, WIN, BH]),
                                      ALU.subtract).then_inc(shifted, 1)
                if s < NT:
                    dve.wait_ge(qkv_ready, 3 * (s + 1))
                    part_of_products(s, 0)
                    part_of_products(s, 1)
                if s + 2 < NT:
                    statistics(s + 2)
                if 1 <= s <= NT:
                    dve.wait_ge(exp_ready, s)
                    link(dve.tensor_reduce(sm[:, :, :], att[:, :, :, :].rearrange("p b w h -> p b h w"), AX.X, ALU.add))
                    link(dve.reciprocal(rs[:, :, :], sm[:, :, :]))
                    dve.tensor_tensor(att[:, :, :, :], att[:, :, :, :],
                                      rs[:, :, :].unsqueeze(2).broadcast_to([P, D // P, WIN, BH]), ALU.mult)\
                       .then_inc(att_ready, 1)
                if s < NT:
                    part_of_products(s, 2)
                if 1 <= s <= NT:
                    dve.wait_ge(ath_ready, s)
                    dve.tensor_tensor(atl[:, :, :], T2, ath[:, :, :].bitcast(F32), ALU.subtract).then_inc(atl_ready, 1)
                if s >= 2:
                    i = s - 2
                    dve.wait_ge(o_ready, i + 1)
                    dve.tensor_tensor(x[:, i, :], x[:, i, :], o[:, :], ALU.add).then_inc(x_ready, 1)
                    dve.wait_ge(x_ready, i + 1)
                    row_sums(dve, g, st, i)
                if 1 <= s <= NT:
                    i = s - 1
                    for n, w in enumerate(ORDER):
                        if i >= 1 and n % 4 == 0:
                            dve.wait_ge(rsum_ready, 4 * (i - 1) + n // 4 + 1)
                        dve.wait_ge(spread_done, WIN * i + n + 1)
                        dve.tensor_tensor(r[:, w, :], RING[(2 + n) % 3], vpad[:, i % 3, w:w + D], ALU.mult)\
                           .then_inc(r_ready, 1)
                if s + 2 < NT:
                    normalise(s + 2)

            row_variances(dve, g, st)

        @block.tensor
        def _(pe):
            pe.wait_ge(w4_landed, 16)

            def project(i):
                pe.wait_ge(xn_ready, i + 1)
                if i >= 3:
                    pe.wait_ge(o_ready, i - 2)
                pe.matmul(M, w4[:, 0, :], xn[:, i % 2, :], start=True, stop=True).then_inc(qkv_done, 1)
                pe.wait_ge(ctx_landed[i], 16)
                if i >= 3:
                    pe.wait_ge(r_ready, WIN * (i - 2))
                for j in (1, 2):
                    pe.matmul(RING[j - 1], w4[:, j, :], ctxt[:, i, :], start=True, stop=True).then_inc(qkv_done, 1)

            def reduce_heads(i, part):
                if part < PARTS - 1:
                    pe.wait_ge(prod_ready, (PARTS - 1) * i + part + 1)
                else:
                    pe.wait_ge(last_prod_ready, i + 1)
                if i >= 1 and part == 0:
                    pe.wait_ge(sc_ready, i)
                for u in (2 * part, 2 * part + 1):
                    dst = S[u // 4][32 * (u % 4):32 * (u % 4) + 32, :]
                    pe.matmul(dst, sel[:, 0, :], prod[:, 2 * u, :], start=True, stop=False)
                    last = pe.matmul(dst, sel[:, 1, :], prod[:, 2 * u + 1, :], start=False, stop=True)
                last.then_inc(prod_used, 1)

            def output(i, pairs=range(WIN // 4)):
                if i + 2 < NT:
                    pe.wait_ge(qkv_ready, 3 * (i + 2) + 1)
                for pair in pairs:
                    pe.wait_ge(rsum_ready, 4 * i + pair + 1)
                    for w in (2 * pair, 2 * pair + 1):
                        last = pe.matmul(M, w4[:, 3, :], r2[:, w, :], start=(w == 0), stop=(w == WIN // 2 - 1))
                if WIN // 4 - 1 in pairs:
                    last.then_inc(out_done, 1)

            def scores_turned(i):
                pe.wait_ge(sc_ready, i + 1)
                for b in range(D // P):
                    for grp in range(2):
                        last = pe.transpose(T_time[:, b, grp, :], sc[:, grp, b * P:(b + 1) * P], ident[:, :])
                last.then_inc(fwd_done, 1)

            project(0)
            pe.wait_ge(tables_landed, 48)
            for s in range(NT + 2):
                if s > NT:
                    output(NT - 1, (2, 3))
                    continue
                if s >= 2:
                    output(s - 2)
                if s < NT:
                    reduce_heads(s, 0)
                    reduce_heads(s, 1)
                if s + 1 < NT:
                    project(s + 1)
                if s >= 1:
                    pe.wait_ge(att_ready, s)
                    for grp in range(2):
                        for b in range(D // P):
                            last = pe.transpose(T2[:, grp, b * P:(b + 1) * P],
                                                att[:, b, grp * WG:(grp + 1) * WG, :].rearrange("p w h -> p (w h)"), ident[:, :])
                    last.then_inc(back_done, 1)
                if s < NT:
                    reduce_heads(s, 2)
                    reduce_heads(s, 3)
                if s >= 1:
                    i = s - 1
                    if i == 0:
                        pe.wait_ge(spread_ready, 1)
                    pe.wait_ge(atl_ready, s)
                    for n, w in enumerate(ORDER):
                        if n < 3:
                            pe.wait_ge(qkv_ready, 3 * min(s + 2, NT))
                        if n >= 3:
                            pe.wait_ge(r_ready, WIN * i + n - 2)
                        elif i >= 1:
                            pe.wait_ge(r_ready, WIN * i)
                        pe.matmul(RING[(2 + n) % 3], spread[:, w % WG, :], ath[:, w // WG, :], start=True, stop=False)
                        pe.matmul(RING[(2 + n) % 3], spread[:, w % WG, :], atl[:, w // WG, :], start=False, stop=True)\
                          .then_inc(spread_done, 1)
                        if n == WIN // 2 and s < NT:
                            scores_turned(s)
                        if s == NT and n in (10, 14):
                            output(NT - 1, (n // 4 - 2,))
                else:
                    scores_turned(s)


def norm_sems(sem, tag):
    names = ("xn_ready", "xt_done", "xh_ready", "xl_ready")
    return {n: sem(f"{tag}_{n}") for n in names}


def stat_sems(sem):
    return {n: sem(f"next_{n}") for n in ("sums_done", "aggr_done", "var_ready", "rstd_ready")}


def row_sums(dve, g, st, i):
    dve.bn_stats(g["stats"][:, i, :], g["x"][:, i, :]).then_inc(st["sums_done"], 1)


def row_variances(dve, g, st):
    dve.wait_ge(st["sums_done"], NT)
    for i in range(NT):
        last = dve.bn_aggr(g["mv"][:, i, :], g["stats"][:, i, :])
    last.then_inc(st["aggr_done"], 1)
    dve.wait_ge(st["aggr_done"], 1)
    dve.tensor_scalar(g["veps"][:, :], g["mv"][:, :, 1], EPS, None, ALU.add).then_inc(st["var_ready"], 1)


def row_scales(pool, g, st):
    pool.wait_ge(st["var_ready"], 1)
    pool.tensor_tensor(g["rstd"][:, :], g["veps"][:, :], g["mhalf"][:, :], ALU.pow).then_inc(st["rstd_ready"], 1)


def norm_rows(dve, g, n, xn, i):
    if i >= 2:
        dve.wait_ge(n["xt_done"], i - 1)
    dve.tensor_scalar(xn[:, i % 2, :], g["x"][:, i, :], g["mv"][:, i, 0:1], g["rstd"][:, i:i + 1],
                      ALU.subtract, ALU.mult).then_inc(n["xn_ready"], 1)


def norm_turn(pe, g, n, xn, banks, i):
    pe.wait_ge(n["xn_ready"], i + 1)
    if i >= len(banks):
        pe.wait_ge(n["xl_ready"], i - len(banks) + 1)
    for c in range(DC):
        last = pe.transpose(g["ps"][:, banks[i % len(banks)], c * P:(c + 1) * P], xn[:, i % 2, c * P:(c + 1) * P], g["ident"][:, :])
    last.then_inc(n["xt_done"], 1)


def norm_high(act, g, n, banks, i):
    act.wait_ge(n["xt_done"], i + 1)
    act.activation(g["xh"][:, :, i * P:(i + 1) * P], g["ps"][:, banks[i % len(banks)], :].rearrange("p (c t) -> p c t", c=DC),
                   ACT.Copy).then_inc(n["xh_ready"], 1)


def norm_low(dve, g, n, banks, i):
    dve.wait_ge(n["xh_ready"], i + 1)
    t = slice(i * P, (i + 1) * P)
    dve.tensor_tensor(g["xl"][:, :, t], g["ps"][:, banks[i % len(banks)], :].rearrange("p (c t) -> p c t", c=DC),
                      g["xh"][:, :, t].bitcast(F32), ALU.subtract).then_inc(n["xl_ready"], 1)


def norm_vector(dve, g, n, xn, banks):
    norm_rows(dve, g, n, xn, 0)
    norm_rows(dve, g, n, xn, 1)
    for i in range(2, NT):
        norm_rows(dve, g, n, xn, i)
        norm_low(dve, g, n, banks, i - 2)
    norm_low(dve, g, n, banks, NT - 2)
    norm_low(dve, g, n, banks, NT - 1)


def norm_scalar(act, g, n, banks):
    for i in range(NT):
        norm_high(act, g, n, banks, i)


def norm_tensor(pe, g, n, xn, banks):
    for i in range(NT):
        norm_turn(pe, g, n, xn, banks, i)


def three_passes(pe, dst, lhs, rhs, chunks, first=True, final=True):
    for c in range(chunks):
        (lh, ll), (rh, rl) = lhs(c), rhs(c)
        pe.matmul(dst, lh, rh, start=(first and c == 0), stop=False)
        pe.matmul(dst, lh, rl, start=False, stop=False)
        last = pe.matmul(dst, ll, rh, start=False, stop=(final and c == chunks - 1))
    return last


def lora_loads(sp, a, g):
    er = NE * RANK
    landed = g["lora_landed"]
    sp.dma_start(g["wb_raw"], a["W_base"].rearrange("(c p) n -> p c n", p=P)).then_inc(landed, 16)
    sp.dma_start(g["la_raw"][:, :, 0:er], a["lora_A"].rearrange("(c p) n -> p c n", p=P)).then_inc(landed, 16)
    sp.dma_start(g["la_raw"][:, :, er:], a["W_router"].rearrange("(c p) n -> p c n", p=P)).then_inc(landed, 16)
    sp.dma_start(g["lb"], a["lora_B"]).then_inc(landed, 16)
    sp.dma_start(g["bb"], a["b_base"].partition_broadcast(P)).then_inc(landed, 16)
    sp.dma_start(g["iota"][:, :], a["iota"].partition_broadcast(P)).then_inc(landed, 16)
    sp.dma_start(g["gnum"][:, :], a["gnum"]).then_inc(landed, 16)
    sp.dma_start(g["nib"][:, :], a["nib"]).then_inc(landed, 16)


LORA_LOADS = 8


def load_scales(sp, a, g, m):
    name, _, ncols, groups = MATS[m]
    if m == 0:
        sp.wait_ge(g["cleared"], 3)
    else:
        sp.wait_ge(g["parts_ready"], m)
    for b in range(3):
        sp.dma_start(g["srow"][32 * b:32 * b + groups, 0:ncols], a[name + "_scales"]).then_inc(g["scales_landed"], 16)


def scales_scalar(act, g, m, k):
    ncols = MATS[m][2]
    rows, rest, cols = g["rows"], g["rest"], slice(COL0[m], COL0[m] + ncols)
    if k == 0:
        act.wait_ge(g["scales_landed"], 48 * (m + 1))
        act.activation(rows[0:96, cols], g["srow"][0:96, 0:ncols], ACT.Copy).then_inc(g["scales_step"], 1)
    elif k == 1:
        act.wait_ge(g["rest_ready"], 2 * m + 1)
        act.activation(rows[32:64, cols], rest[32:64, 0:ncols], ACT.Copy).then_inc(g["scales_step"], 1)
        act.activation(rows[64:96, cols], rest[64:96, 0:ncols], ACT.Copy).then_inc(g["scales_step"], 1)
    else:
        act.wait_ge(g["rest_ready"], 2 * m + 2)
        act.activation(rows[64:96, cols], rest[64:96, 0:ncols], ACT.Copy).then_inc(g["parts_ready"], 1)


def scales_pool(pool, g, m, k):
    ncols = MATS[m][2]
    cols = slice(COL0[m], COL0[m] + ncols)
    before = (g["srow"] if k == 0 else g["rest"])[0:96, 0:ncols]
    pool.wait_ge(g["scales_step"], 3 * m + (1 if k == 0 else 3))
    pool.tensor_tensor(g["rest"][0:96, 0:ncols], before, g["rows"][0:96, cols], ALU.subtract).then_inc(g["rest_ready"], 1)


def load_groups(sp, a, g, m):
    name, k, ncols, groups = MATS[m]
    landed = g["idx_landed"][m % 2]
    if m == 0:
        sp.wait_ge(g["cleared"], 3)
    elif m == 1:
        sp.wait_ge(g["parts_ready"], 3)
    else:
        sp.wait_ge(g["rows_ready"], m - 1)
    sp.dma_start(g["gi"][m % 2][:, 0:k], a[name + "_g_idx"].partition_broadcast(P)).then_inc(landed, 16)
    sp.dma_start(g["zq"][m % 2][96:96 + groups, 0:ncols // PACK], a[name + "_qzeros"]).then_inc(landed, 16)


def routed_lora(nc, a, g):
    ps, x, ident, gate = g["ps"], g["x"], g["ident"], g["gate"]
    ER = NE * RANK
    with ExitStack() as ctx:
        def sb(name, shape, dt=F32):
            return ctx.enter_context(nc.sbuf_tensor(name, shape, dt))

        def sem(name):
            return ctx.enter_context(nc.semaphore("b_" + name))

        xn = sb("b_xn", [P, 2, D])
        wbh = sb("wbh", [P, DC, D], F32R)
        wbl = sb("wbl", [P, DC, D], F32R)
        lah = sb("lah", [P, DC, ER + NE], F32R)
        lal = sb("lal", [P, DC, ER + NE], F32R)
        gb = sb("gb", [P, D])
        lgT = sb("lgT", [NE, TOK])
        hT = sb("hT", [P, TOK])
        lg = sb("lg", [P, NT, NE])
        top8 = sb("top8", [P, NT, 8])
        idx = sb("idx", [P, NT, 8], U32)
        idxf = sb("idxf", [P, NT, 8])
        dl = sb("dl", [P, NT])
        e2 = sb("e2", [P, NT])
        den = sb("den", [P, NT])
        w1 = sb("w1", [P, NT])
        w2 = sb("w2", [P, NT])
        wa = sb("wa", [P, NT, NE])
        wc = sb("wc", [P, NT, NE])
        wx = sb("wx", [P, 2, ER])
        hwT = sb("hwT", [P, 2, P])
        c_raw = sb("c_raw", [P, 2, HALF])
        ch, cl = g["ch"], g["cl"]
        gf = sb("gf", [P, INTER])
        neg = sb("neg", [P, INTER])
        wb_raw, la_raw, lb, bb, iota, gnum = (g[name] for name in ("wb_raw", "la_raw", "lb", "bb", "iota", "gnum"))

        wh_ready = sem("wh_ready")
        wl_ready = sem("wl_ready")
        gb_ready = sem("gb_ready")
        xb_ready = sem("xb_ready")
        step = sem("step")
        n = norm_sems(sem, "n")
        st = stat_sems(sem)
        c_landed = [sem(f"c_landed{i}") for i in range(2)]
        ch_ready = sem("ch_ready")
        cl_ready = sem("cl_ready")
        small_done = sem("small_done")
        small_ready = sem("small_ready")
        lg_done = sem("lg_done")
        diff_ready = sem("diff_ready")
        e2_ready = sem("e2_ready")
        wx_ready = sem("wx_ready")
        wxT_done = sem("wxT_done")
        hw_ready = sem("hw_ready")
        out_done = sem("out_done")
        x_ready = sem("x_ready")

        XT = (0, 1, 6, 7)
        SMALL = (2, 3)
        LG, WX, OUT = 4, 5, (6, 7, 0, 1)

        block = ctx.enter_context(nc.Block())

        @block.sync
        def _(sp):
            cT = a["ctxT"].rearrange("(c p) t -> p c t", p=P)
            for u in range(DC * NHALF):
                c, h = u % DC, u // DC
                if u >= 2:
                    sp.wait_ge(cl_ready, u - 1)
                if u == 2:
                    load_groups(sp, a, g, 2)
                sp.dma_start(c_raw[:, u % 2, :], cT[:, c, h * HALF:(h + 1) * HALF]).then_inc(c_landed[u % 2], 16)
            load_piece(sp, a, g, 0, 0, Q23)
            load_piece(sp, a, g, 0, 0, O01)

        @block.gpsimd
        def _(pool):
            pool.wait_ge(g["lora_landed"], 16 * LORA_LOADS)
            pool.wait_ge(wh_ready, 1)
            pool.tensor_tensor(lal[:, :, :], la_raw[:, :, :], lah[:, :, :].bitcast(F32), ALU.subtract).then_inc(wl_ready, 1)
            pool.wait_ge(wh_ready, 2)
            pool.tensor_tensor(wbl[:, :, :], wb_raw[:, :, :], wbh[:, :, :].bitcast(F32), ALU.subtract).then_inc(wl_ready, 1)
            pool.wait_ge(gb_ready, 1)
            for i in range(NT):
                pool.wait_ge(n["xn_ready"], i + 1)
                pool.tensor_tensor(x[:, i, :], x[:, i, :], gb[:, :], ALU.add).then_inc(xb_ready, 1)
            for u in range(DC * NHALF):
                c, h = u % DC, u // DC
                t = slice(h * HALF, (h + 1) * HALF)
                pool.wait_ge(ch_ready, u + 1)
                pool.tensor_tensor(cl[:, c, t], c_raw[:, u % 2, :], ch[:, c, t].bitcast(F32), ALU.subtract).then_inc(cl_ready, 1)
            for piece in (KV, Q01, Q23):
                low_piece(pool, g, 0, 0, piece)
            row_scales(pool, g, st)

        @block.scalar
        def _(act):
            act.wait_ge(g["lora_landed"], 16 * LORA_LOADS)
            act.activation(lah[:, :, :], la_raw[:, :, :], ACT.Copy).then_inc(wh_ready, 1)
            norm_scalar(act, g, n, XT)
            act.activation(wbh[:, :, :], wb_raw[:, :, :], ACT.Copy).then_inc(wh_ready, 1)
            act.activation(gb[:, :], bb[:, :], ACT.Copy, scale=gate[:, 2:3]).then_inc(gb_ready, 1)
            for h in range(NHALF):
                act.wait_ge(small_done, h + 1)
                act.activation(lgT[:, h * HALF:(h + 1) * HALF], ps[0:NE, SMALL[h], :], ACT.Copy).then_inc(small_ready, 1)
            for h in range(NHALF):
                act.wait_ge(small_done, NHALF + h + 1)
                act.activation(hT[:, h * HALF:(h + 1) * HALF], ps[:, SMALL[h], :], ACT.Copy).then_inc(small_ready, 1)
            act.wait_ge(diff_ready, 1)
            act.activation(e2[:, :], dl[:, :], ACT.Exp).then_inc(e2_ready, 1)
            for u in range(DC * NHALF):
                c, h = u % DC, u // DC
                act.wait_ge(c_landed[u % 2], 16 * (u // 2 + 1))
                act.activation(ch[:, c, h * HALF:(h + 1) * HALF], c_raw[:, u % 2, :], ACT.Copy).then_inc(ch_ready, 1)
            for piece in (KV, Q01, Q23):
                high_piece(act, g, 0, 0, piece)

        @block.vector
        def _(dve):
            norm_vector(dve, g, n, xn, XT)
            chain = [0]

            def link(ins):
                chain[0] += 1
                ins.then_inc(step, 1)
                dve.wait_ge(step, chain[0])

            GROUP_STEPS = 7

            def groups_of(m, k):
                _, rows_of, ncols, groups = MATS[m]
                f, t = gf[:, 0:rows_of], neg[:, 0:rows_of]
                z = slice(96, 128)
                gi, zq = g["gi"][m % 2], g["zq"][m % 2]
                if k == 0:
                    dve.wait_ge(g["idx_landed"][m % 2], 32 * (m // 2 + 1))
                    link(dve.tensor_copy(f, gi[:, 0:rows_of]))
                elif k == 1:
                    link(dve.tensor_scalar(t, f, 0.0, float(groups), ALU.is_lt, ALU.mult))
                elif k == 2:
                    link(dve.tensor_tensor(f, f, t, ALU.add))
                elif k == 3:
                    link(dve.tensor_scalar(f, f, float(groups - 1), 0.0, ALU.min, ALU.max))
                elif k == 4:
                    dve.tensor_scalar(g["onehot"][:, ROW0[m]:ROW0[m] + rows_of], f, gnum[:, 0:1], None, ALU.is_equal)
                elif k == 5:
                    for j in range(PACK):
                        last = dve.tensor_scalar(gi[z, j:ncols:PACK], zq[z, 0:ncols // PACK], BITS * j, 15,
                                                 ALU.logical_shift_right, ALU.bitwise_and)
                    link(last)
                else:
                    dve.tensor_scalar(g["rows"][z, COL0[m]:COL0[m] + ncols], gi[z, 0:ncols], 1.0, None, ALU.add)\
                       .then_inc(g["rows_ready"], 1)

            dve.wait_ge(g["lora_landed"], 16 * LORA_LOADS)
            for k in range(GROUP_STEPS):
                groups_of(0, k)
            dve.wait_ge(lg_done, 1)
            link(dve.tensor_copy(lg[:, :, :], ps[:, LG, 0:NT * NE].rearrange("p (i e) -> p i e", e=NE)))
            for i in range(NT):
                last = dve.max(top8[:, i, :], lg[:, i, :])
            link(last)
            for i in range(NT):
                last = dve.max_index(idx[:, i, :], top8[:, i, :], lg[:, i, :])
            link(last)
            dve.tensor_tensor(dl[:, :], top8[:, :, 1], top8[:, :, 0], ALU.subtract).then_inc(diff_ready, 1)
            link(dve.tensor_copy(idxf[:, :, :], idx[:, :, :]))
            dve.wait_ge(e2_ready, 1)
            link(dve.tensor_scalar(den[:, :], e2[:, :], 1.0, None, ALU.add))
            link(dve.reciprocal(w1[:, :], den[:, :]))
            link(dve.tensor_tensor(w2[:, :], w1[:, :], e2[:, :], ALU.mult))
            for i in range(NT):
                dve.tensor_scalar(wa[:, i, :], iota[:, :], idxf[:, i, 0:1], w1[:, i:i + 1], ALU.is_equal, ALU.mult)
                last = dve.tensor_scalar(wc[:, i, :], iota[:, :], idxf[:, i, 1:2], w2[:, i:i + 1], ALU.is_equal, ALU.mult)
            link(last)
            link(dve.tensor_tensor(wa[:, :, :], wa[:, :, :], wc[:, :, :], ALU.add))

            def widen(i):
                if i >= 2:
                    dve.wait_ge(wxT_done, i - 1)
                dve.tensor_scalar(wx[:, i % 2, :].rearrange("p (e r) -> p e r", e=NE),
                                  wa[:, i, :].unsqueeze(2).broadcast_to([P, NE, RANK]), LORA_SCALE, None, ALU.mult)\
                   .then_inc(wx_ready, 1)

            widen(0)
            for k in range(GROUP_STEPS):
                groups_of(1, k)
            dve.wait_ge(small_ready, 2 * NHALF)
            for i in range(NT + 1):
                if i + 1 < NT:
                    widen(i + 1)
                if i < NT:
                    dve.wait_ge(wxT_done, i + 1)
                    if i >= 2:
                        dve.wait_ge(out_done, i - 1)
                    dve.tensor_tensor(hwT[:, i % 2, :], ps[:, WX, 0:P], hT[:, i * P:(i + 1) * P], ALU.mult)\
                       .then_inc(hw_ready, 1)
                if i >= 1:
                    j = i - 1
                    dve.wait_ge(out_done, i)
                    dve.wait_ge(xb_ready, i)
                    dve.scalar_tensor_tensor(x[:, j, :], ps[:, OUT[j % 4], :], gate[:, 2:3], x[:, j, :], ALU.mult, ALU.add)\
                       .then_inc(x_ready, 1)
                    dve.wait_ge(x_ready, i)
                    row_sums(dve, g, st, j)
                if i < GROUP_STEPS:
                    groups_of(2, i)
            row_variances(dve, g, st)

        @block.tensor
        def _(pe):
            norm_tensor(pe, g, n, xn, XT)
            pe.wait_ge(wl_ready, 1)

            def small(part, h):
                cols = slice(ER, ER + NE) if part == 0 else slice(0, ER)
                t = slice(h * HALF, (h + 1) * HALF)
                if part == 0:
                    pe.wait_ge(n["xl_ready"], TPH * (h + 1))
                else:
                    pe.wait_ge(small_ready, h + 1)
                three_passes(pe, ps[0:cols.stop - cols.start, SMALL[h], :], lambda c: (lah[:, c, cols], lal[:, c, cols]),
                             lambda c: (g["xh"][:, c, t], g["xl"][:, c, t]), DC).then_inc(small_done, 1)

            small(0, 0)
            small(0, 1)
            small(1, 0)
            pe.wait_ge(small_ready, NHALF)
            for i in range(NT):
                last = pe.transpose(ps[:, LG, NE * i:NE * i + NE], lgT[:, i * P:(i + 1) * P], ident[0:NE, 0:NE])
            last.then_inc(lg_done, 1)
            small(1, 1)

            def base(i):
                t = slice(i * P, (i + 1) * P)
                if i >= 4:
                    pe.wait_ge(x_ready, i - 3)
                three_passes(pe, ps[:, OUT[i % 4], :], lambda c: (g["xh"][:, c, t], g["xl"][:, c, t]),
                             lambda c: (wbh[:, c, :], wbl[:, c, :]), DC, final=False)

            def experts(i):
                pe.wait_ge(wx_ready, i + 1)
                if i >= 1:
                    pe.wait_ge(hw_ready, i)
                pe.transpose(ps[:, WX, 0:P], wx[:, i % 2, :], ident[:, :]).then_inc(wxT_done, 1)
                if i + 2 < NT:
                    base(i + 2)
                pe.wait_ge(hw_ready, i + 1)
                pe.matmul(ps[:, OUT[i % 4], :], hwT[:, i % 2, :], lb[:, :], start=False, stop=True).then_inc(out_done, 1)

            pe.wait_ge(wl_ready, 2)
            base(0)
            base(1)
            for i in range(NT):
                experts(i)


def rotary_attention(nc, a, g):
    ps, x, ident, gate = g["ps"], g["x"], g["ident"], g["gate"]
    wqh, wql, wkvh, wkvl = g["wqh"], g["wql"], g["wkvh"], g["wkvl"]
    SCALE = float(np.float32(1.0) / np.sqrt(np.float32(DK)))
    NROT = 1 + GRP
    PIECE_OF = {(0, 1): KV, (0, 2): Q01, (1, 0): Q23, (1, 1): O01, (1, 2): O23}
    PAIRS, SLOTS2, STEPS2 = NKV // 2, 2 * NHALF, 2 * NHALF * TPH
    HEAD = 5
    BODY = range(HEAD, HEAD + STEPS2)

    def projecting(c, last):
        return not (last and c // TPH + 1 >= SLOTS2)

    def tile_exists(c, last):
        return c >= 0 and not (last and c >= STEPS2)

    def piece_due(c, last):
        sl = c // TPH
        if last and sl // NHALF + 1 >= 2:
            return None
        piece = PIECE_OF.get((sl % NHALF, c % TPH))
        return None if piece is None else (piece, (sl // NHALF + 1) // 2, (sl // NHALF + 1) % 2)

    def step_number(b, c):
        return STEPS2 * b + c
    with ExitStack() as ctx:
        def sb(name, shape, dt=F32):
            return ctx.enter_context(nc.sbuf_tensor(name, shape, dt))

        def sem(name):
            return ctx.enter_context(nc.semaphore("c_" + name))

        ch, cl = g["ch"], g["cl"]
        cs = sb("cs", [P, 2, C])
        woh = g["woh"] = sb("woh", [P, 2, GRP, D], F32R)
        wol = g["wol"] = sb("wol", [P, 2, GRP, D], F32R)
        vh = sb("vh", [P, NT, DK], F32R)
        vl = sb("vl", [P, NT, DK], F32R)
        s = sb("s", [P, 2, GRP, C])
        mx = sb("c_mx", [P, GRP])
        sm = sb("c_sm", [P, GRP])
        rs = sb("c_rs", [P, 2, GRP])
        bd = sb("bd", [P, 2, GRP, P])
        ah = sb("ah", [P, GRP * P], F32R)
        al = sb("al", [P, GRP * P], F32R)
        oh = sb("oh", [P, 2, GRP * P], F32R)
        ol = sb("ol", [P, 2, GRP * P], F32R)
        xn = bd[:, :, :, :].rearrange("p b h k -> p b (h k)")

        n = norm_sems(sem, "n")
        st = stat_sems(sem)
        low_ready = g["low_ready"]
        qT, kT, vT, mask, ra, rb = (g[name] for name in ("qT", "kT", "vT", "mask", "ra", "rb"))
        loaded = sem("loaded")
        bd_zeroed = sem("bd_zeroed")
        proj_done = sem("proj_done")
        rope_a = sem("rope_a")
        rope_ready = sem("rope_ready")
        vproj_done = sem("vproj_done")
        vT_ready = sem("vT_ready")
        vtr_done = sem("vtr_done")
        vh_ready, vl_ready = sem("vh_ready"), sem("vl_ready")
        sc_done = sem("sc_done")
        masked = sem("masked")
        max_ready = sem("max_ready")
        shifted = sem("shifted")
        exp_ready = sem("exp_ready")
        sum_ready = sem("sum_ready")
        rs_ready = sem("rs_ready")
        bd_ready = sem("bd_ready")
        aT_done = sem("aT_done")
        ah_ready, al_ready = sem("ah_ready"), sem("al_ready")
        pv_done = sem("pv_done")
        oh_ready, ol_ready = sem("oh_ready"), sem("ol_ready")
        wo_done = sem("wo_done")
        x_ready = sem("x_ready")

        PROJ = (0, 1)
        SCB = (2, 3)
        TR, PV, WO = 4, 5, (6, 7)
        XT = (2, 3, 6, 7)

        block = ctx.enter_context(nc.Block())

        @block.sync
        def _(sp):
            sp.dma_start(cs[:, :, :], a["rope"].rearrange("p (a t) -> p a t", a=2)).then_inc(loaded, 16)
            sp.dma_start(mask[:, :, :], a["mask"].rearrange("(i b) q k -> (b q) i k", b=BT)).then_inc(loaded, 16)
            load_piece(sp, a, g, 0, 0, O23)
            with sp.Fori(0, PAIRS - 1) as b:
                for piece in range(5):
                    load_piece(sp, a, g, b, 1, piece)
                for piece in range(5):
                    load_piece(sp, a, g, b + 1, 0, piece)
            for piece in range(5):
                load_piece(sp, a, g, PAIRS - 1, 1, piece)
            load_unit(sp, a, g, 0)
            load_unit(sp, a, g, 1)

        BANK_OF = (0, 0, 1, 0, 1)
        ROTARY_OF = {0: (0,), 1: (1, 2), 2: (3,), 3: (4,)}

        @block.gpsimd
        def _(pool):
            def rotary_sum(b, sl, p):
                r = NROT * sl + p
                h = sl % NHALF
                pool.wait_ge(rope_a, SLOTS2 * NROT * b + r + 1)
                if sl >= 1:
                    pool.wait_ge(sc_done, STEPS2 * b + max(TPH * (sl - 1), 1))
                dst = (kT[:, :] if p == 0 else qT[:, p - 1, :])[:, h * HALF:(h + 1) * HALF]
                pool.tensor_tensor(dst, ra[:, r % 2, :], rb[:, r % 2, :], ALU.add).then_inc(rope_ready, 1)

            def shift(b, c):
                pool.wait_ge(max_ready, STEPS2 * b + c + 1)
                pool.tensor_tensor(s[:, c % 2, :, :], s[:, c % 2, :, :],
                                   mx[:, :].unsqueeze(2).broadcast_to([P, GRP, C]), ALU.subtract).then_inc(shifted, 1)

            def steps(b, last):
                for c in range(STEPS2):
                    sl, j = c // TPH, c % TPH
                    shift(b, c)
                    if projecting(c, last):
                        for p in ROTARY_OF[j]:
                            rotary_sum(b, sl + 1, p)
                    due = piece_due(c, last)
                    if due:
                        piece, db, odd = due
                        low_piece(pool, g, b + db, odd, piece)

            rotary_sum(0, 0, 0)
            pool.wait_ge(n["xt_done"], NT)
            pool.memset(bd[:, :, :, :], 0.0).then_inc(bd_zeroed, 1)
            for p in range(1, NROT):
                rotary_sum(0, 0, p)
            low_piece(pool, g, 0, 0, O01)
            low_piece(pool, g, 0, 0, O23)
            with pool.Fori(0, PAIRS - 1) as b:
                steps(b, False)
            steps(PAIRS - 1, True)
            row_scales(pool, g, st)

        @block.scalar
        def _(act):
            def high_part(b, piece, odd):
                if piece == KV:
                    act.wait_ge(vproj_done, SLOTS2 * b + NHALF * odd)
                elif piece in (Q01, Q23):
                    act.wait_ge(proj_done, NROT * (SLOTS2 * b + NHALF * odd - 1) + 2 * (piece - Q01) + 3)
                else:
                    act.wait_ge(wo_done, step_number(b, NT * (odd - 1)) + 1)
                high_piece(act, g, b, odd, piece)

            def values_out(b, sl):
                act.wait_ge(vproj_done, SLOTS2 * b + sl + 1)
                if sl >= 1:
                    act.wait_ge(vtr_done, SLOTS2 * b + sl)
                act.activation(vT, ps[:, PROJ[1], :], ACT.Copy).then_inc(vT_ready, 1)

            def values(b, sl):
                h = sl % NHALF
                act.wait_ge(vtr_done, SLOTS2 * b + sl + 1)
                if sl >= NHALF:
                    act.wait_ge(pv_done, step_number(b, TPH * (sl - 1)))
                act.activation(vh[:, h * TPH:(h + 1) * TPH, :], ps[:, TR, :].rearrange("p (i d) -> p i d", i=TPH),
                               ACT.Copy).then_inc(vh_ready, 1)

            def exps(b, c):
                act.wait_ge(shifted, step_number(b, c) + 1)
                act.activation(s[:, c % 2, :, :], s[:, c % 2, :, :], ACT.Exp).then_inc(exp_ready, 1)

            def turned(b, c):
                act.wait_ge(aT_done, step_number(b, c) + 1)
                if c >= 1:
                    act.wait_ge(pv_done, step_number(b, c))
                act.activation(ah[:, :], ps[:, TR, :], ACT.Copy).then_inc(ah_ready, 1)

            def high_out(b, c):
                act.wait_ge(pv_done, step_number(b, c) + 1)
                if c >= 2:
                    act.wait_ge(wo_done, step_number(b, c) - 1)
                act.activation(oh[:, c % 2, :], ps[:, PV, :], ACT.Copy).then_inc(oh_ready, 1)

            def step(b, c, last=False):
                sl, j = c // TPH, c % TPH
                if tile_exists(c - 2, last):
                    turned(b, c - 2)
                if projecting(c, last) and j == 2:
                    values(b, sl + 1)
                if tile_exists(c, last):
                    exps(b, c)
                due = piece_due(c, last)
                if due:
                    piece, db, odd = due
                    high_part(b + db, piece, odd)
                if tile_exists(c - 2, last):
                    high_out(b, c - 2)
                if projecting(c, last) and j == 0:
                    values_out(b, sl + 1)

            for i in range(TPH):
                norm_high(act, g, n, XT, i)
            values_out(0, 0)
            for i in range(TPH, NT):
                norm_high(act, g, n, XT, i)
            values(0, 0)
            high_piece(act, g, 0, 0, O01)
            high_piece(act, g, 0, 0, O23)
            for c in range(HEAD):
                step(0, c)
            with act.Fori(0, PAIRS - 1) as b:
                for c in BODY:
                    step(b, c)
            for c in BODY:
                step(PAIRS - 1, c, last=True)

        @block.vector
        def _(dve):
            def rotary(b, sl, p):
                r = NROT * sl + p
                count = NROT * SLOTS2 * b + r
                bank = ps[:, PROJ[BANK_OF[p]], :].rearrange("p (b t) -> p b t", t=C)
                dve.wait_ge(proj_done, count + 1)
                if r >= 2:
                    dve.wait_ge(rope_ready, count - 1)
                A = ra[:, r % 2, :].rearrange("p (b t) -> p b t", t=C)
                R_ = rb[:, r % 2, :].rearrange("p (b t) -> p b t", t=C)
                nb = HALF // C
                hd = DK // 2
                dve.tensor_tensor(A, bank, cs[:, 0, :].unsqueeze(1).broadcast_to([P, nb, C]), ALU.mult)
                dve.tensor_tensor(R_[0:hd], bank[hd:DK], cs[0:hd, 1, :].unsqueeze(1).broadcast_to([hd, nb, C]), ALU.mult)
                dve.tensor_tensor(R_[hd:DK], bank[0:hd], cs[hd:DK, 1, :].unsqueeze(1).broadcast_to([hd, nb, C]), ALU.mult)\
                   .then_inc(rope_a, 1)

            def maximum(b, c):
                i, m = c % NT, step_number(b, c)
                dve.wait_ge(sc_done, m + 1)
                if c >= 2:
                    dve.wait_ge(bd_ready, 2 * (m - 1))
                bank = ps[:, SCB[c % 2], :].rearrange("p (h k) -> p h k", h=GRP)
                for k in range(BT):
                    rows = slice(k * C, (k + 1) * C)
                    dve.scalar_tensor_tensor(s[rows, c % 2, :, :], bank[rows, :, k * C:(k + 1) * C], SCALE,
                                             mask[rows, i, :].unsqueeze(1).broadcast_to([C, GRP, C]), ALU.mult, ALU.add)\
                       .then_inc(masked, 1)
                dve.wait_ge(masked, 2 * (m + 1))
                if c >= 1:
                    dve.wait_ge(shifted, m)
                dve.tensor_reduce(mx[:, :], s[:, c % 2, :, :], AX.X, ALU.max).then_inc(max_ready, 1)

            def sums(b, c):
                m = step_number(b, c)
                dve.wait_ge(exp_ready, m + 1)
                dve.tensor_reduce(sm[:, :], s[:, c % 2, :, :], AX.X, ALU.add).then_inc(sum_ready, 1)
                dve.wait_ge(sum_ready, m + 1)
                dve.reciprocal(rs[:, c % 2, :], sm[:, :]).then_inc(rs_ready, 1)
                dve.wait_ge(rs_ready, m + 1)
                if c >= 2:
                    dve.wait_ge(aT_done, m - 1)
                for k in range(BT):
                    rows = slice(k * C, (k + 1) * C)
                    dve.tensor_tensor(bd[rows, c % 2, :, k * C:(k + 1) * C], s[rows, c % 2, :, :],
                                      rs[rows, c % 2, :].unsqueeze(2).broadcast_to([C, GRP, C]), ALU.mult)\
                       .then_inc(bd_ready, 1)

            def low_values(b, sl):
                i0 = sl % NHALF * TPH
                dve.wait_ge(vh_ready, SLOTS2 * b + sl + 1)
                dve.tensor_tensor(vl[:, i0:i0 + TPH, :], ps[:, TR, :].rearrange("p (i d) -> p i d", i=TPH),
                                  vh[:, i0:i0 + TPH, :].bitcast(F32), ALU.subtract).then_inc(vl_ready, 1)

            def low_turned(b, c):
                dve.wait_ge(ah_ready, step_number(b, c) + 1)
                dve.tensor_tensor(al[:, :], ps[:, TR, :], ah[:, :].bitcast(F32), ALU.subtract).then_inc(al_ready, 1)

            def low_out(b, c):
                dve.wait_ge(oh_ready, step_number(b, c) + 1)
                dve.tensor_tensor(ol[:, c % 2, :], ps[:, PV, :], oh[:, c % 2, :].bitcast(F32), ALU.subtract).then_inc(ol_ready, 1)

            def add(b, c, last):
                i, m = c % NT, step_number(b, c)
                dve.wait_ge(wo_done, m + 1)
                dve.scalar_tensor_tensor(x[:, i, :], ps[:, WO[c % 2], :], gate[:, 1:2], x[:, i, :], ALU.mult, ALU.add)\
                   .then_inc(x_ready, 1)
                if last and c >= NT:
                    dve.wait_ge(x_ready, m + 1)
                    row_sums(dve, g, st, i)

            def step(b, c, last=False):
                sl, j = c // TPH, c % TPH
                early = last and c >= STEPS2 - TPH
                if tile_exists(c - 3, last) and not (last and c > STEPS2 - TPH):
                    low_out(b, c - 3)
                if tile_exists(c - 2, last):
                    low_turned(b, c - 2)
                if tile_exists(c, last):
                    maximum(b, c)
                if projecting(c, last):
                    rotary(b, sl + 1, ROTARY_OF[j][0])
                    if j == 2:
                        low_values(b, sl + 1)
                if tile_exists(c - 3, last):
                    add(b, c - 3, last)
                if early and tile_exists(c - 2, last):
                    low_out(b, c - 2)
                if tile_exists(c, last):
                    sums(b, c)
                if projecting(c, last) and j == 1:
                    rotary(b, sl + 1, ROTARY_OF[j][1])

            norm_rows(dve, g, n, xn, 0)
            norm_rows(dve, g, n, xn, 1)
            for i in range(2, NT):
                norm_rows(dve, g, n, xn, i)
                norm_low(dve, g, n, XT, i - 2)
                if i == 3:
                    dve.wait_ge(loaded, 32)
                    rotary(0, 0, 0)
            norm_low(dve, g, n, XT, NT - 2)
            norm_low(dve, g, n, XT, NT - 1)
            for p in range(1, NROT):
                rotary(0, 0, p)
                if p == 2:
                    low_values(0, 0)
            dve.wait_ge(bd_zeroed, 1)
            for c in range(HEAD):
                step(0, c)
            with dve.Fori(0, PAIRS - 1) as b:
                for c in BODY:
                    step(b, c)
            for c in BODY:
                step(PAIRS - 1, c, last=True)
            row_variances(dve, g, st)

        @block.tensor
        def _(pe):
            def project(b, sl, p):
                h = sl % NHALF
                count = NROT * (SLOTS2 * b + sl) + p
                t = slice(h * HALF, (h + 1) * HALF)
                dst = ps[:, PROJ[BANK_OF[p]], :]
                if p == 0 and sl >= 1:
                    pe.wait_ge(rope_a, count - 1)
                elif p == 1:
                    pe.wait_ge(rope_a, count)
                elif p == 2:
                    pe.wait_ge(vT_ready, SLOTS2 * b + sl + 1)
                elif p >= 3:
                    pe.wait_ge(rope_a, count - 1)
                pieces = 10 * b + 5 * (sl // NHALF)
                if p == 0:
                    pe.wait_ge(low_ready, pieces + KV + 1)
                    last = three_passes(pe, dst, lambda k: (wkvh[:, 0, k, :], wkvl[:, 0, k, :]),
                                        lambda k: (ch[:, k, t], cl[:, k, t]), DC)
                else:
                    pe.wait_ge(low_ready, pieces + Q01 + (p - 1) // 2 + 1)
                    cols = slice((p - 1) * DK, p * DK)
                    last = three_passes(pe, dst, lambda k: (wqh[:, k, cols], wql[:, k, cols]),
                                        lambda k: (g["xh"][:, k, t], g["xl"][:, k, t]), DC)
                last.then_inc(proj_done, 1)

            def project_v(b, sl):
                h = sl % NHALF
                t = slice(h * HALF, (h + 1) * HALF)
                if sl >= 1:
                    pe.wait_ge(rope_a, NROT * (SLOTS2 * b + sl))
                three_passes(pe, ps[:, PROJ[1], :], lambda k: (wkvh[:, 1, k, :], wkvl[:, 1, k, :]),
                             lambda k: (ch[:, k, t], cl[:, k, t]), DC).then_inc(vproj_done, 1)

            def turn_v(b, sl):
                pe.wait_ge(vT_ready, SLOTS2 * b + sl + 1)
                if sl >= 1:
                    pe.wait_ge(al_ready, step_number(b, TPH * (sl - 1)) + 1)
                for i in range(TPH):
                    last = pe.transpose(ps[:, TR, i * P:(i + 1) * P], vT[:, i * P:(i + 1) * P], ident[:, :])
                last.then_inc(vtr_done, 1)

            def scores(b, c):
                m = step_number(b, c)
                if c % TPH == 0:
                    pe.wait_ge(rope_ready, NROT * (SLOTS2 * b + c // TPH + 1))
                if c >= 2:
                    pe.wait_ge(masked, 2 * (m - 1))
                t = slice(c % NT * P, (c % NT + 1) * P)
                for h in range(GRP):
                    last = pe.matmul(ps[:, SCB[c % 2], h * P:(h + 1) * P], qT[:, h, t], kT[:, t], start=True, stop=True)
                last.then_inc(sc_done, 1)

            def turn(b, c, end):
                m = step_number(b, c)
                pe.wait_ge(bd_ready, 2 * (m + 1))
                if c >= 1:
                    pe.wait_ge(al_ready, m)
                if c == 0:
                    pe.wait_ge(vl_ready, 1)
                elif c % TPH == 1 and projecting(c, end):
                    pe.wait_ge(vl_ready, SLOTS2 * b + c // TPH + 2)
                for h in range(GRP):
                    last = pe.transpose(ps[:, TR, h * P:(h + 1) * P], bd[:, c % 2, h, :], ident[:, :])
                last.then_inc(aT_done, 1)

            def weighted(b, c):
                m, i = step_number(b, c), c % NT
                pe.wait_ge(al_ready, m + 1)
                if c >= 1:
                    pe.wait_ge(ol_ready, m)
                three_passes(pe, ps[:, PV, :], lambda k: (vh[:, i, :], vl[:, i, :]),
                             lambda k: (ah[:, :], al[:, :]), 1).then_inc(pv_done, 1)

            def project_out(b, c):
                m, head = step_number(b, c), c // NT
                if c % NT == 0:
                    pe.wait_ge(low_ready, 10 * b + 5 * head + O23 + 1)
                pe.wait_ge(ol_ready, m + 1)
                if c >= 2:
                    pe.wait_ge(x_ready, m - 1)
                three_passes(pe, ps[:, WO[c % 2], :],
                             lambda h: (oh[:, c % 2, h * P:(h + 1) * P], ol[:, c % 2, h * P:(h + 1) * P]),
                             lambda h: (woh[:, head % 2, h, :], wol[:, head % 2, h, :]), GRP).then_inc(wo_done, 1)

            def step(b, c, last=False):
                sl, j = c // TPH, c % TPH
                more = projecting(c, last)
                if tile_exists(c - 2, last):
                    turn(b, c - 2, last)
                if more:
                    project(b, sl + 1, ROTARY_OF[j][0])
                    if j == 2:
                        turn_v(b, sl + 1)
                if tile_exists(c - 3, last):
                    project_out(b, c - 3)
                if tile_exists(c - 2, last):
                    weighted(b, c - 2)
                if more and j == 0:
                    project_v(b, sl + 1)
                if more and j == 1:
                    project(b, sl + 1, ROTARY_OF[j][1])
                if tile_exists(c + 1, last):
                    scores(b, c + 1)

            project(0, 0, 0)
            norm_turn(pe, g, n, xn, XT, 0)
            norm_turn(pe, g, n, xn, XT, 1)
            norm_turn(pe, g, n, xn, XT, 2)
            norm_turn(pe, g, n, xn, XT, 3)
            project_v(0, 0)
            norm_turn(pe, g, n, xn, XT, 4)
            norm_turn(pe, g, n, xn, XT, 5)
            pe.wait_ge(n["xl_ready"], TPH)
            project(0, 0, 1)
            norm_turn(pe, g, n, xn, XT, 6)
            norm_turn(pe, g, n, xn, XT, 7)
            project(0, 0, 2)
            turn_v(0, 0)
            project(0, 0, 3)
            project(0, 0, 4)
            pe.wait_ge(n["xl_ready"], NT)
            scores(0, 0)
            for c in range(HEAD):
                step(0, c)
            with pe.Fori(0, PAIRS - 1) as b:
                for c in BODY:
                    step(b, c)
            for c in BODY:
                step(PAIRS - 1, c, last=True)


def load_unit(sp, a, g, u):
    t, m = u // 3, u % 3
    rows_packed = P // PACK
    name, _, ncols, _ = MATS[m]
    q = a[name + "_qweight"]
    if u >= 2:
        sp.wait_ge(g["q_used"], u - 1)
    w = inner(t)
    if m < 2:
        for c in range(DC):
            src = bass.AP(q.tensor, q.offset + rows_packed * c * ncols + P * t, [[ncols, rows_packed], [0, PACK], [1, w]])
            sp.dma_start(g["qraw"][:, u % 2, c * P:c * P + w], src).then_inc(g["q_landed"][u % 2], 16)
    else:
        src = bass.AP(q.tensor, q.offset + rows_packed * t * ncols, [[ncols, w // PACK], [0, PACK], [1, ncols]])
        sp.dma_start(g["qraw"][0:w, u % 2, :], src).then_inc(g["q_landed"][u % 2], 16)


def gate_up(nc, a, g):
    ps, h, wd = g["ps"], g["h"], g["wd"]
    onehot, rows = g["onehot"], g["rows"]
    with ExitStack() as ctx:
        def sb(name, shape, dt=F32):
            return ctx.enter_context(nc.sbuf_tensor(name, shape, dt))

        def sem(name):
            return ctx.enter_context(nc.semaphore("d_" + name))

        xn = sb("d_xn", [P, 2, D])
        nib, qraw, q_landed, q_used = g["nib"], g["qraw"], g["q_landed"], g["q_used"]
        qn = sb("qn", [P, D], I32)
        wf = sb("wf", [P, 2, D])
        wh = sb("wh", [P, 4, D], F32R)
        wl = sb("wl", [P, 4, D], F32R)
        th = sb("th", [P, HALF])
        sg = sb("sg", [P, HALF])

        n = norm_sems(sem, "n")
        step = sem("step")
        zs_done = sem("zs_done")
        unit_ready = sem("unit_ready")
        wh_ready = sem("wh_ready")
        wl_ready = sem("wl_ready")
        gu_done = sem("gu_done")
        th_ready = sem("th_ready")
        h_ready = sem("h_ready")

        Z, SC = (0, 1), (2, 3)
        GU = (4, 5, 6, 7)
        XT = (6, 7)
        UNITS = 3 * NTI
        UNPACK_AT = {4: 0, 6: 1}

        block = ctx.enter_context(nc.Block())

        @block.sync
        def _(sp):
            for u in range(2, UNITS):
                load_unit(sp, a, g, u)

        def landed(u):
            return 16 * sum(DC if v % 3 < 2 else 1 for v in range(u % 2, u + 1, 2))

        def unit_view(buf, t, m):
            if m == 2:
                return buf[0:inner(t), :]
            return buf.rearrange("p (c n) -> p c n", c=DC)[:, :, 0:inner(t)]

        @block.gpsimd
        def _(pool):
            for u in range(UNITS):
                t, m = u // 3, u % 3
                if u == UNITS - 1:
                    down_low_weights(pool, g, 0, 0)
                if m == 2:
                    continue
                k = 2 * t + m
                pool.wait_ge(wh_ready, k + 1)
                pool.tensor_tensor(unit_view(wl[:, k % 4, :], t, m), unit_view(wf[:, m, :], t, m),
                                   unit_view(wh[:, k % 4, :], t, m).bitcast(F32), ALU.subtract).then_inc(wl_ready, 1)

        @block.scalar
        def _(act):
            def high(t, m):
                k = 2 * t + m
                act.wait_ge(unit_ready, 3 * t + m + 1)
                if k >= 4:
                    act.wait_ge(gu_done, 4 * (t - 1))
                act.activation(unit_view(wh[:, k % 4, :], t, m), unit_view(wf[:, m, :], t, m), ACT.Copy).then_inc(wh_ready, 1)

            for i in range(NT):
                norm_high(act, g, n, XT, i)
                if i in UNPACK_AT:
                    high(0, UNPACK_AT[i])
            for t in range(NTI):
                if t + 1 < NTI:
                    high(t + 1, 0)
                    high(t + 1, 1)
                for hf in range(NHALF):
                    w = inner(t)
                    act.wait_ge(gu_done, 4 * t + 2 * hf + 1)
                    if 2 * t + hf >= 1:
                        act.wait_ge(h_ready, 2 * t + hf)
                    act.activation(th[0:w, :], ps[0:w, GU[2 * hf], :], ACT.Tanh, scale=0.5).then_inc(th_ready, 1)
                if t == 1:
                    down_high(act, g, 0, 0)

        @block.vector
        def _(dve):
            chain = [0]

            def link(ins):
                chain[0] += 1
                ins.then_inc(step, 1)
                dve.wait_ge(step, chain[0])

            def unpack(u):
                t, m = u // 3, u % 3
                dve.wait_ge(q_landed[u % 2], landed(u))
                rows_of = inner(t) if m == 2 else P
                dve.tensor_scalar(unit_view(qn[:, :], t, m), unit_view(qraw[:, u % 2, :], t, m), nib[0:rows_of, 0:1],
                                  15, ALU.logical_shift_right, ALU.bitwise_and).then_inc(q_used, 1)
                dve.wait_ge(q_used, u + 1)
                dve.wait_ge(zs_done, u + 1)
                if m == 2:
                    dst = wd[0:inner(t), t, :]
                else:
                    if t >= 1:
                        dve.wait_ge(wl_ready, 2 * (t - 1) + m + 1)
                    dst = unit_view(wf[:, m, :], t, m)
                link(dve.tensor_tensor(dst, unit_view(qn[:, :], t, m), unit_view(ps[:, Z[u % 2], :], t, m), ALU.subtract))
                dve.tensor_tensor(dst, dst, unit_view(ps[:, SC[u % 2], :], t, m), ALU.mult).then_inc(unit_ready, 1)

            norm_rows(dve, g, n, xn, 0)
            for i in range(1, NT):
                norm_rows(dve, g, n, xn, i)
                norm_low(dve, g, n, XT, i - 1)
                if i in UNPACK_AT:
                    unpack(UNPACK_AT[i])
            norm_low(dve, g, n, XT, NT - 1)
            unpack(2)
            for t in range(NTI):
                w = inner(t)
                if t + 1 < NTI:
                    unpack(3 * t + 3)
                    unpack(3 * t + 4)
                for hf in range(NHALF):
                    dve.wait_ge(th_ready, 2 * t + hf + 1)
                    link(dve.scalar_tensor_tensor(sg[0:w, :], th[0:w, :], 1.0, ps[0:w, GU[2 * hf], :], ALU.add, ALU.mult))
                    dve.wait_ge(gu_done, 4 * t + 2 * hf + 2)
                    dve.scalar_tensor_tensor(h[0:w, t, hf * HALF:(hf + 1) * HALF], sg[0:w, :], 0.5, ps[0:w, GU[2 * hf + 1], :],
                                             ALU.mult, ALU.mult).then_inc(h_ready, 1)
                if t + 1 < NTI:
                    unpack(3 * t + 5)
                if t == 2:
                    down_low_h(dve, g, 0, 0)

        @block.tensor
        def _(pe):
            def zeros_and_scales(u):
                t, m = u // 3, u % 3
                if u >= 2:
                    pe.wait_ge(unit_ready, u - 1)
                pieces = [(ROW0[m] + c * P, P, COL0[m] + t * P, c * P, inner(t)) for c in range(DC)]
                if m == 2:
                    pieces = [(ROW0[m] + t * P, inner(t), COL0[m], 0, D)]
                for r0, k, c0, at, width in pieces:
                    pe.matmul(ps[0:k, Z[u % 2], at:at + width], onehot[96:128, r0:r0 + k], rows[96:128, c0:c0 + width],
                              start=True, stop=True)
                    last = pe.matmul(ps[0:k, SC[u % 2], at:at + width], onehot[0:96, r0:r0 + k], rows[0:96, c0:c0 + width],
                                     start=True, stop=True)
                last.then_inc(zs_done, 1)

            def products(t, hf, m):
                w, k = inner(t), 2 * t + m
                tok = slice(hf * HALF, (hf + 1) * HALF)
                pe.wait_ge(wl_ready, k + 1)
                if t >= 1:
                    pe.wait_ge(h_ready, 2 * (t - 1) + hf + 1)
                view = lambda buf: buf[:, k % 4, :].rearrange("p (c n) -> p c n", c=DC)
                three_passes(pe, ps[0:w, GU[2 * hf + m], :], lambda c: (view(wh)[:, c, 0:w], view(wl)[:, c, 0:w]),
                             lambda c: (g["xh"][:, c, tok], g["xl"][:, c, tok]), DC).then_inc(gu_done, 1)

            zeros_and_scales(0)
            zeros_and_scales(1)
            for i in range(NT - 2):
                norm_turn(pe, g, n, xn, XT, i)
            zeros_and_scales(2)
            pe.wait_ge(n["xl_ready"], TPH)
            products(0, 0, 0)
            norm_turn(pe, g, n, xn, XT, NT - 2)
            norm_turn(pe, g, n, xn, XT, NT - 1)
            products(0, 0, 1)
            zeros_and_scales(3)
            pe.wait_ge(n["xl_ready"], NT)
            products(0, 1, 0)
            zeros_and_scales(4)
            products(0, 1, 1)
            for t in range(1, NTI):
                zeros_and_scales(3 * t + 2)
                for hf in range(NHALF):
                    for m in range(2):
                        if t + 1 < NTI and hf == 0:
                            zeros_and_scales(3 * (t + 1) + m)
                        products(t, hf, m)


def down_high(act, g, t, odd, w=P):
    act.activation(g["wdh"][0:w, odd, :], g["wd"][0:w, t, :], ACT.Copy).then_inc(g["wdh_ready"], 1)
    act.activation(g["hh"][0:w, odd, :], g["h"][0:w, t, :], ACT.Copy).then_inc(g["hh_ready"], 1)


def down_low_weights(pool, g, t, odd, w=P):
    pool.wait_ge(g["wdh_ready"], t + 1)
    pool.tensor_tensor(g["wdl"][0:w, odd, :], g["wd"][0:w, t, :], g["wdh"][0:w, odd, :].bitcast(F32), ALU.subtract)\
        .then_inc(g["wdl_ready"], 1)


def down_low_h(dve, g, t, odd, w=P):
    dve.wait_ge(g["hh_ready"], t + 1)
    dve.tensor_tensor(g["hl"][0:w, odd, :], g["h"][0:w, t, :], g["hh"][0:w, odd, :].bitcast(F32), ALU.subtract)\
       .then_inc(g["hl_ready"], 1)


def down(nc, a, g, out):
    ps, x, gate = g["ps"], g["x"], g["gate"]
    with ExitStack() as ctx:
        def sb(name, shape, dt=F32):
            return ctx.enter_context(nc.sbuf_tensor(name, shape, dt))

        def sem(name):
            return ctx.enter_context(nc.semaphore("e_" + name))

        res = sb("res", [P, NT, D])
        hh, hl, wdh, wdl = g["hh"], g["hl"], g["wdh"], g["wdl"]
        wdl_ready, hl_ready = g["wdl_ready"], g["hl_ready"]
        tile_done = sem("tile_done")
        out_done = sem("out_done")
        res_ready = sem("res_ready")
        stored = sem("stored")
        block = ctx.enter_context(nc.Block())

        @block.sync
        def _(sp):
            rows = out.rearrange("b s d -> (b s) d")
            for i in range(NT):
                sp.wait_ge(res_ready, i + 1)
                sp.dma_start(rows[i * P:(i + 1) * P, :], res[:, i, :]).then_inc(stored, 16)
            sp.wait_ge(stored, 16 * NT)

        @block.scalar
        def _(act):
            down_high(act, g, 1, 1)
            with act.Fori(0, PAIRED) as b:
                act.wait_ge(tile_done, 2 * b + 1)
                down_high(act, g, 2 * b + 2, 0)
                act.wait_ge(tile_done, 2 * b + 2)
                down_high(act, g, 2 * b + 3, 1)
            for t in range(2 * PAIRED + 2, NTI):
                act.wait_ge(tile_done, t - 1)
                down_high(act, g, t, t % 2, inner(t))

        @block.gpsimd
        def _(pool):
            with pool.Fori(0, PAIRED) as b:
                down_low_weights(pool, g, 2 * b + 1, 1)
                down_low_weights(pool, g, 2 * b + 2, 0)
            for t in range(2 * PAIRED + 1, NTI):
                down_low_weights(pool, g, t, t % 2, inner(t))

        @block.vector
        def _(dve):
            with dve.Fori(0, PAIRED) as b:
                down_low_h(dve, g, 2 * b + 1, 1)
                down_low_h(dve, g, 2 * b + 2, 0)
            for t in range(2 * PAIRED + 1, NTI):
                down_low_h(dve, g, t, t % 2, inner(t))
            for i in range(NT):
                dve.wait_ge(out_done, i + 1)
                dve.scalar_tensor_tensor(res[:, i, :], ps[:, i, :], gate[:, 3:4], x[:, i, :], ALU.mult, ALU.add)\
                   .then_inc(res_ready, 1)

        @block.tensor
        def _(pe):
            def products(t, odd, w, first=False, final=False):
                pe.wait_ge(wdl_ready, t + 1)
                pe.wait_ge(hl_ready, t + 1)
                for i in range(NT):
                    tok = slice(i * P, (i + 1) * P)
                    last = three_passes(pe, ps[:, i, :], lambda c: (hh[0:w, odd, tok], hl[0:w, odd, tok]),
                                        lambda c: (wdh[0:w, odd, :], wdl[0:w, odd, :]), 1, first=first, final=final)
                    if final:
                        last.then_inc(out_done, 1)
                if not final:
                    last.then_inc(tile_done, 1)

            products(0, 0, P, first=True)
            with pe.Fori(0, PAIRED) as b:
                products(2 * b + 1, 1, P)
                products(2 * b + 2, 0, P)
            for t in range(2 * PAIRED + 1, NTI - 1):
                products(t, t % 2, P)
            products(NTI - 1, (NTI - 1) % 2, inner(NTI - 1), final=True)


SWDGE_BYTES = 4096


def constants():
    f = np.float32
    pos = np.arange(C, dtype=f)
    inv = (f(1.0) / np.power(f(10000.0), np.arange(0, DK, 2, dtype=f) / f(DK))).astype(f)
    ang = inv[:, None] * pos[None, :]
    cos, sin = np.cos(ang).astype(f), np.sin(ang).astype(f)
    rope = np.concatenate([np.concatenate([cos, cos]), np.concatenate([-sin, sin])], axis=1)
    ch = np.arange(P)
    sel = np.zeros((P, 2, 2 * BH), f)
    spread = np.zeros((P, WG, P), f)
    for e in range(2):
        sel[ch, e, e * BH + ch // LHD] = 1
    for w in range(WG):
        spread[w * BH + ch // LHD, w, ch] = 1
    return {
        "ident": np.eye(P, dtype=f),
        "rope": rope,
        "sel": sel.reshape(P, -1),
        "spread": spread.reshape(P, -1),
        "iota": np.arange(NE, dtype=f),
        "nib": (BITS * (ch % PACK)).astype(np.int32)[:, None],
        "gnum": (ch % 32).astype(f)[:, None],
    }


def block_diagonal(w):
    r = np.zeros((P, P), w.dtype)
    for b in range(BT):
        r[b * C:(b + 1) * C, b * C:(b + 1) * C] = w.T
    return r


def kernel(**inputs):
    import numpy as _np
    import concourse.bacc as _bacc
    from concourse import mybir as _mybir
    from concourse.bass_utils import run_bass_kernel_spmd as _run

    i = {k: _np.asarray(v) for k, v in inputs.items()}
    arrays = {
        "x": i["x"], "ctx": i["ctx_4096"], "ctxT": i["ctx_4096"].reshape(TOK, D).T, "mask": i["mask_BxSxS2_ff0"],
        "W_base": i["L0_ffn_W_base"].T, "b_base": i["L0_ffn_b_base"], "W_router": i["L0_ffn_W_router"].T,
        "lora_A": i["L0_ffn_lora_A"].reshape(NE * RANK, D).T,
        "lora_B": i["L0_ffn_lora_B"].transpose(0, 2, 1).reshape(NE * RANK, D),
    }
    arrays["W4"] = _np.concatenate([block_diagonal(i["L0_xattn_W" + n]) for n in "qkvo"], axis=1)
    arrays["bias"] = _np.stack([_np.concatenate([i["L0_xattn_b" + n]] * BT) for n in "qkvo"], axis=1)
    arrays["gates"] = _np.concatenate([i["g_xattn"], i["g_ffn"]])
    for n in "qkvo":
        arrays["w" + n] = i["L1_xattn_w" + n]
    for m in ("gate", "up", "down"):
        for part in ("qweight", "scales", "qzeros", "g_idx"):
            arrays[f"{m}_{part}"] = i[f"L1_ffn_{m}_{part}"]
    arrays.update(constants())

    nc = _bacc.Bacc("TRN2", target_bir_lowering=False, num_devices=1, dynamic_dma_scratch_size=SWDGE_BYTES)
    given, aps = {}, {}
    for n, v in arrays.items():
        v = _np.ascontiguousarray(v)
        given[f"in_{n}"] = v
        aps[n] = nc.dram_tensor(f"in_{n}", v.shape, _mybir.dt.from_np(v.dtype), kind="ExternalInput").ap()
    out = nc.dram_tensor("out", (B, C, D), F32, kind="ExternalOutput").ap()
    build_program(nc, aps, out)
    return _run(nc, [given], core_ids=[0]).results[0]["out"]
```
